# Optimizing a Trainium2 kernel written in Bass

```python
import numpy as np
import jax
import jax.numpy as jnp

def _softmax(x, axis=-1):
    return jax.nn.softmax(x, axis=axis)

def _gelu(x):
    return jax.nn.gelu(x, approximate=True)

def _silu(x):
    return jax.nn.silu(x)

def _sigmoid(x):
    return jax.nn.sigmoid(x)

def _layernorm(x, axis=-1, eps=1e-05):
    m = jnp.mean(x, axis=axis, keepdims=True)
    v = jnp.var(x, axis=axis, keepdims=True)
    return (x - m) / jnp.sqrt(v + eps)

def _scatter_add(tgt, idx, src, axis=0):
    return tgt.at[idx].add(src)

def _segment_sum(src, seg, n):
    return jax.ops.segment_sum(src, seg, n)
kernel_name = 'mk_flamingo_gated_d1_seqx_r2_9a2bf4'

def setup_inputs(seed: int=0):
    np.random.seed(seed)
    _w = jnp.asarray

    def _rec_inputs():
        import jax
        import jax.numpy as jnp
        _rk = jax.random.key(seed)
        x = -0.0003929 + 0.9999 * jax.random.normal(jax.random.fold_in(_rk, 1), (2, 2048, 512), jnp.float32)
        _lenS = 2048 - jax.random.randint(jax.random.fold_in(_rk, 7), (2,), 0, max(1, 2048 // 4) + 1, jnp.int32)
        _lenS2 = 128 - jax.random.randint(jax.random.fold_in(_rk, 8), (2,), 0, max(1, 128 // 4) + 1, jnp.int32)
        _ctx_512P = jax.random.normal(jax.random.fold_in(_rk, 11), (2, 16, 256), jnp.float32)
        _ctx_512c = jax.random.dirichlet(jax.random.fold_in(_rk, 511), 0.3 * jnp.ones((16,), jnp.float32), (2, 128))
        _ctx_512t = jnp.einsum('bsk,bkd->bsd', _ctx_512c, _ctx_512P)
        _ctx_512t = _ctx_512t * jax.lax.rsqrt(jnp.mean(jnp.square(_ctx_512t)) + 1e-12) * 0.953939
        ctx_512 = -1.39393e-06 + 0.999914 * (_ctx_512t + 0.3 * jax.random.normal(jax.random.fold_in(_rk, 611), (2, 128, 256), jnp.float32))
        _g = jax.random.normal(jax.random.fold_in(_rk, 9001), (2, 1), jnp.float32)
        _g = jnp.sign(_g) * jnp.maximum(jnp.abs(_g), 1.0) + (_g == 0) * 1.0
        g_xattn = _g[0]
        g_ffn = _g[1]
        return (x, ctx_512, g_xattn, g_ffn)
    x, ctx_512, g_xattn, g_ffn = _rec_inputs()

    def _L0_xattn_setup():
        import jax, jax.numpy as jnp
        import numpy as np
        HEADS = 16
        D_MODEL = 512
        IMG_MODEL = 256
        D_K = D_MODEL // HEADS
        key = jax.random.key(seed)
        ks = jax.random.split(key, 12)
        B, LQ, LKV = (8, 1024, 512)
        s_dm = 1.0 / np.sqrt(D_MODEL)
        s_im = 1.0 / np.sqrt(IMG_MODEL)
        return {'q': jax.random.normal(ks[0], (B, LQ, D_MODEL), jnp.float32), 'k': jax.random.normal(ks[1], (B, LKV, IMG_MODEL), jnp.float32), 'v': jax.random.normal(ks[2], (B, LKV, IMG_MODEL), jnp.float32), 'Wq': jax.random.normal(ks[3], (D_MODEL, D_MODEL), jnp.float32) * s_dm, 'bq': jnp.zeros((D_MODEL,), jnp.float32), 'Wk': jax.random.normal(ks[4], (IMG_MODEL, D_MODEL), jnp.float32) * s_im, 'bk': jnp.zeros((D_MODEL,), jnp.float32), 'Wv': jax.random.normal(ks[5], (IMG_MODEL, D_MODEL), jnp.float32) * s_im, 'bv': jnp.zeros((D_MODEL,), jnp.float32), 'Wo': jax.random.normal(ks[6], (D_MODEL, D_MODEL), jnp.float32) * s_dm, 'bo': jnp.zeros((D_MODEL,), jnp.float32)}
    _L0_xattn_all = _L0_xattn_setup()
    _L0_xattn_in = {k: v for k, v in _L0_xattn_all.items() if k in ('Wq', 'bq', 'Wk', 'bk', 'Wv', 'bv', 'Wo', 'bo')}
    del _L0_xattn_all

    def _L0_ffn_setup():
        import math
        import jax, jax.numpy as jnp
        import numpy as np
        D_MODEL = 512
        D_FF = 2048
        E = 8
        K = 2
        CAP_FACTOR = 1.25
        CLAMP = 10000.0
        LN_EPS = 1e-05
        B, S = (2, 1024)
        key = jax.random.key(seed)
        ks = jax.random.split(key, 6)
        b12 = math.sqrt(6.0 / (D_MODEL + 2 * D_FF))
        b3 = math.sqrt(6.0 / (D_FF + D_MODEL))
        br = 0.02 * math.sqrt(3.0)
        return {'x': jax.random.normal(ks[0], (B, S, D_MODEL), dtype=jnp.float32), 'ln_gamma': jnp.ones((D_MODEL,), jnp.float32), 'ln_beta': jnp.zeros((D_MODEL,), jnp.float32), 'router_w': jax.random.uniform(ks[1], (E, D_MODEL), jnp.float32, -br, br), 'w12': jax.random.uniform(ks[2], (E, 2 * D_FF, D_MODEL), jnp.float32, -b12, b12), 'w3': jax.random.uniform(ks[3], (E, D_MODEL, D_FF), jnp.float32, -b3, b3)}
    _L0_ffn_all = _L0_ffn_setup()
    _L0_ffn_in = {k: v for k, v in _L0_ffn_all.items() if k in ('ln_gamma', 'ln_beta', 'router_w', 'w12', 'w3')}
    del _L0_ffn_all
    return {'x': x, 'ctx_512': ctx_512, 'g_xattn': g_xattn, 'g_ffn': g_ffn, 'L0_xattn_Wq': _L0_xattn_in['Wq'], 'L0_xattn_bq': _L0_xattn_in['bq'], 'L0_xattn_Wk': _L0_xattn_in['Wk'], 'L0_xattn_bk': _L0_xattn_in['bk'], 'L0_xattn_Wv': _L0_xattn_in['Wv'], 'L0_xattn_bv': _L0_xattn_in['bv'], 'L0_xattn_Wo': _L0_xattn_in['Wo'], 'L0_xattn_bo': _L0_xattn_in['bo'], 'L0_ffn_ln_gamma': _L0_ffn_in['ln_gamma'], 'L0_ffn_ln_beta': _L0_ffn_in['ln_beta'], 'L0_ffn_router_w': _L0_ffn_in['router_w'], 'L0_ffn_w12': _L0_ffn_in['w12'], 'L0_ffn_w3': _L0_ffn_in['w3']}

def reference(x, ctx_512, g_xattn, g_ffn, L0_xattn_Wq, L0_xattn_bq, L0_xattn_Wk, L0_xattn_bk, L0_xattn_Wv, L0_xattn_bv, L0_xattn_Wo, L0_xattn_bo, L0_ffn_ln_gamma, L0_ffn_ln_beta, L0_ffn_router_w, L0_ffn_w12, L0_ffn_w3):
    import jax
    import jax.numpy as jnp

    def _L0_xattn_ref(q, k, v, Wq, bq, Wk, bk, Wv, bv, Wo, bo):
        import jax, jax.numpy as jnp
        import numpy as np
        HEADS = 16
        D_MODEL = 512
        IMG_MODEL = 256
        D_K = D_MODEL // HEADS
        B, LQ, _ = q.shape
        LKV = k.shape[1]
        qh = (q @ Wq + bq).reshape(B, LQ, HEADS, D_K).transpose(0, 2, 1, 3)
        kh = (k @ Wk + bk).reshape(B, LKV, HEADS, D_K).transpose(0, 2, 1, 3)
        vh = (v @ Wv + bv).reshape(B, LKV, HEADS, D_K).transpose(0, 2, 1, 3)
        scale = 1.0 / np.sqrt(D_K)
        scores = jnp.einsum('bhqd,bhkd->bhqk', qh, kh) * scale
        attn = jax.nn.softmax(scores, axis=-1)
        out = jnp.einsum('bhqk,bhkd->bhqd', attn, vh)
        concat = out.transpose(0, 2, 1, 3).reshape(B, LQ, D_MODEL)
        return concat @ Wo + bo

    def _L0_ffn_ref(x, ln_gamma, ln_beta, router_w, w12, w3):
        import math
        import jax, jax.numpy as jnp
        import numpy as np
        D_MODEL = 512
        D_FF = 2048
        E = 8
        K = 2
        CAP_FACTOR = 1.25
        CLAMP = 10000.0
        LN_EPS = 1e-05
        B, S = (2, 1024)
        Bq, Sq, D = x.shape
        T = Bq * Sq
        mu = jnp.mean(x, axis=-1, keepdims=True)
        var = jnp.mean(jnp.square(x - mu), axis=-1, keepdims=True)
        xn = (x - mu) * jax.lax.rsqrt(var + LN_EPS) * ln_gamma + ln_beta
        xf = xn.reshape(T, D)
        logits = jnp.clip(xf @ router_w.T, -CLAMP, CLAMP)
        top_v, top_i = jax.lax.top_k(logits, K)
        m = jnp.max(top_v, axis=-1, keepdims=True)
        ev = jnp.exp(top_v - m)
        top_p = ev / (jnp.sum(ev, axis=-1, keepdims=True) + 1e-12)
        Stot = T * K
        experts = top_i.reshape(-1)
        weights = top_p.reshape(-1)
        tokens = jnp.repeat(jnp.arange(T), K)
        oh = (experts[:, None] == jnp.arange(E)[None, :]).astype(jnp.int32)
        pos = jnp.take_along_axis(jnp.cumsum(oh, axis=0) - 1, experts[:, None], axis=1)[:, 0]
        C = max(1, math.ceil(T * K * CAP_FACTOR / E))
        kept = pos < C
        slot = jnp.where(kept, experts * C + pos, E * C)
        buf = jnp.zeros((E * C + 1, D), x.dtype).at[slot].set(xf[tokens])
        xb = buf[:E * C].reshape(E, C, D)
        gu = jnp.einsum('ecd,efd->ecf', xb, w12)
        g, u = jnp.split(gu, 2, axis=-1)
        h = jax.nn.silu(g) * u
        yb = jnp.einsum('ecf,edf->ecd', h, w3).reshape(E * C, D)
        ys = yb[jnp.minimum(slot, E * C - 1)] * (weights * kept.astype(weights.dtype))[:, None]
        out = jnp.zeros((T, D), x.dtype).at[tokens].add(ys)
        return out.reshape(Bq, Sq, D)
    x = x + jnp.tanh(g_xattn[0]) * _L0_xattn_ref(_layernorm(x, axis=-1), ctx_512, ctx_512, L0_xattn_Wq, L0_xattn_bq, L0_xattn_Wk, L0_xattn_bk, L0_xattn_Wv, L0_xattn_bv, L0_xattn_Wo, L0_xattn_bo)
    x = x + jnp.tanh(g_ffn[0]) * _L0_ffn_ref(_layernorm(x, axis=-1), L0_ffn_ln_gamma, L0_ffn_ln_beta, L0_ffn_router_w, L0_ffn_w12, L0_ffn_w3)
    return x

_drawn_inputs = setup_inputs


def setup_inputs(seed=0):
    import zlib

    import numpy as np

    out = dict(_drawn_inputs(seed))
    spreads = {'L0_xattn_bq': (0.0, 0.38),
     'L0_xattn_bk': (0.0, 0.8),
     'L0_xattn_bv': (0.0, 0.1),
     'L0_xattn_bo': (0.0, 0.1),
     'L0_ffn_ln_gamma': (1.0, 0.2),
     'L0_ffn_ln_beta': (0.0, 0.1)}
    factors = {}
    for name, (base, spread) in spreads.items():
        noise = np.random.default_rng([zlib.crc32(name.encode()), seed]).standard_normal(out[name].shape)
        drawn = base * np.exp(spread * noise) if base else spread * noise
        out[name] = jnp.asarray(drawn.astype(out[name].dtype))
    for name, factor in factors.items():
        out[name] = (out[name] * factor).astype(out[name].dtype)
    return out
```

```python
import concourse.bass as bass
from concourse import mybir
from contextlib import ExitStack


def flamingo_gated_layer(
    nc: bass.Bass,
    x: bass.AP,
    ctx_img: bass.AP,
    g_xattn: bass.AP,
    g_ffn: bass.AP,
    Wq: bass.AP,
    bq: bass.AP,
    Wk: bass.AP,
    bk: bass.AP,
    Wv: bass.AP,
    bv: bass.AP,
    Wo: bass.AP,
    bo: bass.AP,
    ln_gamma: bass.AP,
    ln_beta: bass.AP,
    router_w: bass.AP,
    w12: bass.AP,
    w3: bass.AP,
    out: bass.AP,
):
    fp32, f32r = mybir.dt.float32, mybir.dt.float32r
    i32, u32 = mybir.dt.int32, mybir.dt.uint32
    ALU = mybir.AluOpType
    ACT = mybir.ActivationFunctionType
    AX = mybir.AxisListType

    P = 128
    B, S, D = x.shape
    LKV, DI = ctx_img.shape[1], ctx_img.shape[2]
    H = 16
    DK = D // H
    SCALE = float(DK) ** -0.5
    E, F2, _ = w12.shape
    F = F2 // 2
    TOPK = 2
    T = B * S
    CAP = -(-T * TOPK * 5 // (4 * E))
    EPS = 1e-5
    CLAMP = 10000.0

    KD = D // P
    KI = DI // P
    HG = H // KD
    TB = 2 * P
    NB = T // TB
    NBB = NB // B
    NT = CAP // P
    SB = 2 * P
    NSB = CAP // SB
    FC = 2 * P
    NCH = F // FC
    NU12 = 2 * FC // P
    NU3 = FC // P
    NU = NU12 + NU3
    ROW = D + 8
    C_TOK, C_W0, C_W1, C_IDX = D, D + 1, D + 2, D + 3
    XR = 5

    x_tok = x.rearrange("b s d -> (b s) d")
    out_tok = out.rearrange("b s d -> (b s) d")
    xbuf = nc.dram_tensor("expert_rows", [E * CAP, ROW], fp32, kind="Internal").ap()

    with ExitStack() as whole:
        def sem(name):
            return whole.enter_context(nc.semaphore(name))

        stepped = {name: sem(f"stepped_{name}") for name in ("pool", "dve", "sp")}

        def wait_apart(eng, name, semaphore, value):
            eng.wait_ge(semaphore, value)
            eng.sem_inc(stepped[name], 1)

        ident = whole.enter_context(nc.sbuf_tensor("ident", [P, P], fp32))
        bank = [whole.enter_context(nc.psum_tensor(f"bank{i}", [P, 512], fp32)) for i in range(8)]

        with ExitStack() as stage:
            def sb(name, shape, dt=fp32):
                return stage.enter_context(nc.sbuf_tensor(name, shape, dt))

            upper = sb("upper", [P, P])
            ones = sb("ones", [P, P])
            zeros = sb("zeros", [P, 2 * ROW])
            expert_id = sb("expert_id", [P, E])
            neg_half = sb("neg_half", [P, 2])
            tok_count = sb("tok_count", [P, 2])
            gates = sb("gates", [P, 2])
            bqT = sb("bqT", [P, KD])
            bkT = sb("bkT", [P, KD])
            bv_row = sb("bv_row", [1, D])
            gamma_b = sb("gamma_b", [P, D])
            beta_b = sb("beta_b", [P, D])
            gbo_b = sb("gbo_b", [P, D])
            rwT = sb("rwT", [P, KD, E])
            wq_hi, wq_lo = (sb(f"wq_{h}", [P, KD, D], f32r) for h in ("hi", "lo"))
            wo_hi, wo_lo = (sb(f"wo_{h}", [P, KD, D], f32r) for h in ("hi", "lo"))
            k_hi, k_lo = ([sb(f"k_{h}{b}", [P, KD, HG * LKV], f32r) for b in range(B)] for h in ("hi", "lo"))
            v_hi, v_lo = ([sb(f"v_{h}{b}", [P, H, P], f32r) for b in range(B)] for h in ("hi", "lo"))
            xin = sb("xin", [P, 2, D])
            xT_hi, xT_lo = (sb(f"xT_{h}", [P, KD, TB], f32r) for h in ("hi", "lo"))
            qT_hi, qT_lo = (sb(f"qT_{h}", [P, KD, TB], f32r) for h in ("hi", "lo"))
            probs = [sb(f"probs{a}", [P, H, LKV]) for a in range(2)]
            pT_hi, pT_lo = (sb(f"pT_{h}", [P, H, TB], f32r) for h in ("hi", "lo"))
            aT_hi, aT_lo = (sb(f"aT_{h}", [P, KD, TB], f32r) for h in ("hi", "lo"))
            xres = sb("xres", [P, 2, D])
            row = sb("row", [P, 2, ROW])
            xnT = sb("xnT", [P, 2, KD, P])
            neg_max = sb("neg_max", [P, 2, H])
            sums = sb("sums", [P, 2, H])
            rsums = sb("rsums", [P, 2, H])
            bn1, bn2 = (sb(f"bn{i}", [P, 2, 6]) for i in (1, 2))
            mv1, mv2 = (sb(f"mv{i}", [P, 2, 2]) for i in (1, 2))
            var1, var2 = (sb(f"var{i}", [P, 2]) for i in (1, 2))
            rstd1, rstd2 = (sb(f"rstd{i}", [P, 2]) for i in (1, 2))
            logits = sb("logits", [P, 2, E])
            top8 = sb("top8", [P, 2, 8])
            topi = sb("topi", [P, 2, 8], u32)
            idxf = sb("idxf", [P, 2, TOPK])
            gap = sb("gap", [P, 2, 1])
            e1 = sb("e1", [P, 2, 1])
            zsum = sb("zsum", [P, 2, 1])
            zinv = sb("zinv", [P, 2, 1])
            onehot = sb("onehot", [P, 2, TOPK, E])
            chosen = sb("chosen", [P, 2, E])
            before = sb("before", [P, 2, E])
            prod = sb("prod", [P, 2, TOPK, E])
            pos = sb("pos", [P, 2, TOPK])
            over = sb("over", [P, 2, TOPK])
            slotf = sb("slotf", [P, 2, TOPK])
            slot = sb("slot", [P, 2, TOPK], i32)

            prep_loaded = sem("prep_loaded")
            consts_ready, prep_pe, prep_act, prep_dve, prep_pool = (
                sem(n) for n in ("consts_ready", "prep_pe", "prep_act", "prep_dve", "prep_pool"))
            zero_filled = sem("zero_filled")
            xin_loaded, xres_loaded, x1_stored = sem("xin_loaded"), sem("xres_loaded"), sem("x1_stored")
            w_ready, w_free = ([sem(f"{n}{i}") for i in range(2)] for n in ("w_ready", "w_free"))
            s_ready, s_free = sem("s_ready"), sem("s_free")
            pt_ready, pt_free = sem("pt_ready"), sem("pt_free")
            xhi_ready, qhi_ready, ahi_ready, pthi_ready = (
                sem(n) for n in ("xhi_ready", "qhi_ready", "ahi_ready", "pthi_ready"))
            max_ready, rs_ready, pn_ready = sem("max_ready"), sem("rs_ready"), sem("pn_ready")
            stats1_ready, rstd1_ready, xn_ready = sem("stats1_ready"), sem("rstd1_ready"), sem("xn_ready")
            stats2_ready, rstd2_ready, row_ready = sem("stats2_ready"), sem("rstd2_ready"), sem("row_ready")
            xb_ready, gap_ready, e1_ready = sem("xb_ready"), sem("gap_ready"), sem("e1_ready")
            chosen_ready, slot_ready, scattered = sem("chosen_ready"), sem("slot_ready"), sem("scattered")
            dve_done, pool_done = sem("dve_done"), sem("pool_done")

            N_PREP = 14
            V, X, O, Q, N, L, C = range(7)

            def unit(n, kind):
                if isinstance(n, int) and n == 0:
                    return {X: 2, Q: 3}[kind]
                at = 7 * n - 3 + kind
                if isinstance(n, int) and n >= NB - 1:
                    at = 7 * (NB - 1) - 3 + 5 * (n - NB + 1) + [V, O, N, L, C].index(kind)
                return at

            def steps(eng, step):
                step(0, 0, 0)
                step(1, 0, 0)
                with eng.Fori(2, NBB) as n:
                    step(n, 0, 0)
                step(NBB, 1, 0)
                with eng.Fori(NBB + 1, NB - 2) as n:
                    step(n, 1, 1)
                for n in (NB - 2, NB - 1, NB):
                    step(n, 1, 1)

            def has(n, ahead):
                return not isinstance(n, int) or 0 <= n + ahead < NB

            with nc.Block() as block:

                @block.sync
                def _(sp):
                    def prep(dst, src, **kw):
                        sp.dma_start(dst, src, **kw).then_inc(prep_loaded, 16)

                    wide = lambda w: w.rearrange("(k p) n -> p k n", p=P)
                    prep(row[:, :, 0:DI], ctx_img.rearrange("b s d -> s b d"))
                    prep(xin[:, :, :], wide(Wk))
                    prep(xres[:, :, :], wide(Wv))
                    prep(row[0:E, 0, DI:DI + D // 2], router_w[:, 0:D // 2])
                    prep(row[0:E, 1, DI:DI + D // 2], router_w[:, D // 2:D])
                    prep(bkT[:, :], bk.rearrange("(m p) -> p m", p=P), allow_slow_non_contiguous=True)
                    prep(bv_row[:, :], bv.rearrange("(a n) -> a n", a=1))
                    prep(gates[:, 0:1], g_xattn.partition_broadcast(P))
                    prep(gates[:, 1:2], g_ffn.partition_broadcast(P))
                    prep(bqT[:, :], bq.rearrange("(m p) -> p m", p=P), allow_slow_non_contiguous=True)
                    prep(gbo_b[:, :], bo.partition_broadcast(P))
                    prep(gamma_b[:, :], ln_gamma.partition_broadcast(P))
                    prep(beta_b[:, :], ln_beta.partition_broadcast(P))
                    prep(probs[0][:, :, :].rearrange("p (k a) n -> p k (a n)", k=KD), wide(Wq))

                    def load_xin(blk):
                        sp.dma_start(xin[:, :, :], x_tok[bass.ds(blk * TB, TB), :].rearrange("(a p) d -> p a d", p=P))\
                          .then_inc(xin_loaded, 16)

                    def load_xres(blk):
                        sp.dma_start(xres[:, :, :], x_tok[bass.ds(blk * TB, TB), :].rearrange("(a p) d -> p a d", p=P))\
                          .then_inc(xres_loaded, 16)

                    sp.wait_ge(prep_pe, 2)
                    load_xin(0)
                    load_xres(0)
                    sp.wait_ge(consts_ready, 1)
                    flat = xbuf.rearrange("(p r) n -> p (r n)", p=P)
                    for i in range(E * CAP // P // 2):
                        sp.dma_start(flat[:, i * 2 * ROW:(i + 1) * 2 * ROW], zeros[:, :]).then_inc(zero_filled, 16)
                    sp.wait_ge(w_ready[1], 1)
                    load_xin(1)

                    def step(n, b_s, b_v):
                        if has(n, 2):
                            sp.wait_ge(w_ready[1], unit(n, X) + 1)
                            load_xin(n + 2)
                        if has(n, -1):
                            for a in range(2):
                                sp.wait_ge(w_free[a], unit(n, O) + 1)
                                sp.dma_start(out_tok[bass.ds((n - 1) * TB + a * P, P), :], xres[:, a, :])\
                                  .then_inc(x1_stored, 16)
                            wait_apart(sp, "sp", x1_stored, n * 32)
                            if has(n, 0):
                                sp.wait_ge(row_ready, n * 2)
                                load_xres(n)

                    steps(sp, step)

                @block.gpsimd
                def _(pool):
                    nc.gpsimd.memset(zeros[:, :], 0.0).then_inc(consts_ready, 1)
                    nc.gpsimd.memset(ident[:, :], 0.0)
                    nc.gpsimd.memset(upper[:, :], 0.0)
                    nc.gpsimd.memset(ones[:, :], 1.0)
                    nc.gpsimd.memset(neg_half[:, :], -0.5)
                    nc.gpsimd.memset(before[:, 0, :], 0.0).then_inc(pool_done, 1)
                    pool.wait_ge(pool_done, 1)
                    nc.gpsimd.affine_select(out=ident[:, :], in_=ident[:, :], compare_op=ALU.not_equal, fill=1.0,
                                            base=0, pattern=[[-1, P]], channel_multiplier=1)
                    nc.gpsimd.affine_select(out=upper[:, :], in_=upper[:, :], compare_op=ALU.is_ge, fill=1.0,
                                            base=0, pattern=[[-1, P]], channel_multiplier=1)
                    nc.gpsimd.iota(expert_id[:, :], pattern=[[1, E]], base=0, channel_multiplier=0,
                                   allow_small_or_imprecise_dtypes=True)
                    nc.gpsimd.iota(tok_count[:, :], pattern=[[-P, 2]], base=T, channel_multiplier=-1,
                                   allow_small_or_imprecise_dtypes=True).then_inc(consts_ready, 1)
                    for b in range(B):
                        for t in (k_hi[b], k_lo[b], v_hi[b], v_lo[b]):
                            last = nc.gpsimd.memset(t[:, :, :].bitcast(fp32), 0.0)
                    last.then_inc(prep_pool, 1)

                    def pow1(blk):
                        wait_apart(pool, "pool", stats1_ready, blk + 1)
                        nc.gpsimd.tensor_scalar_add(var1[:, :], mv1[:, :, 1], EPS).then_inc(pool_done, 1)
                        pool.wait_ge(pool_done, pool_base(blk, 0))
                        nc.gpsimd.tensor_tensor(rstd1[:, :], var1[:, :], neg_half[:, :], ALU.pow)\
                          .then_inc(rstd1_ready, 1)

                    def pool_base(blk, which):
                        if which == 0:
                            return blk + 2 if isinstance(blk, int) and blk < 2 else 2 * blk
                        if isinstance(blk, int) and blk >= NB - 3:
                            return 2 * (NB - 3) + 5 + blk - (NB - 3)
                        return 2 * blk + 5

                    pow1(0)
                    pow1(1)

                    def norm(n, a):
                        pool.wait_ge(rs_ready, 2 * n + a + 1)
                        nc.gpsimd.tensor_tensor(probs[a][:, :, :], probs[a][:, :, :],
                                                rsums[:, a, :].unsqueeze(2).to_broadcast([P, H, LKV]),
                                                ALU.mult).then_inc(pn_ready, 1)

                    def step(n, b_s, b_v):
                        if has(n, -1):
                            if isinstance(n, int) and n == 1:
                                pool.wait_ge(prep_dve, 3)
                            pool.wait_ge(xres_loaded, 16 * n)
                            nc.gpsimd.tensor_tensor(xres[:, :, :], xres[:, :, :],
                                                    gbo_b[:, :].unsqueeze(1).to_broadcast([P, 2, D]),
                                                    ALU.add).then_inc(xb_ready, 1)
                        if has(n, 0):
                            norm(n, 0)
                        if has(n, -1):
                            wait_apart(pool, "pool", stats2_ready, n)
                            nc.gpsimd.tensor_scalar(var2[:, :], mv2[:, :, 1], 1.0 + EPS, EPS * EPS,
                                                    ALU.mult, ALU.add).then_inc(pool_done, 1)
                            pool.wait_ge(pool_done, pool_base(n - 1, 1))
                            nc.gpsimd.tensor_tensor(rstd2[:, :], var2[:, :], neg_half[:, :], ALU.pow)\
                              .then_inc(rstd2_ready, 1)
                        if has(n, 0):
                            norm(n, 1)
                        if has(n, -1):
                            wait_apart(pool, "pool", slot_ready, n)
                            if isinstance(n, int) and n == 1 or not isinstance(n, int):
                                pool.wait_ge(zero_filled, 16 * (E * CAP // P // 2))
                            for a in range(2):
                                for k in range(TOPK):
                                    nc.gpsimd.indirect_dma_start(
                                        out=xbuf[:, :],
                                        out_offset=bass.IndirectOffsetOnAxis(ap=slot[:, a, k:k + 1], axis=0),
                                        in_=row[:, a, :], in_offset=None,
                                        bounds_check=E * CAP - 1, oob_is_err=False).then_inc(scattered, 16)
                        if has(n, 2):
                            pow1(n + 2)

                    steps(pool, step)
                    pool.wait_ge(scattered, 64 * NB)

                @block.scalar
                def _(act):
                    act.wait_ge(prep_loaded, 16 * N_PREP)
                    nc.scalar.activation(gates[:, :], gates[:, :], ACT.Tanh).then_inc(prep_act, 1)
                    nc.scalar.mul(bkT[:, :], bkT[:, :], SCALE).then_inc(prep_act, 1)
                    wq_raw = probs[0][:, :, :].rearrange("p (k a) n -> p k (a n)", k=KD)
                    wo_raw = probs[1][:, :, :].rearrange("p (k a) n -> p k (a n)", k=KD)
                    act.dma_start(wo_raw, Wo.rearrange("(k p) n -> p k n", p=P)).then_inc(prep_loaded, 16)
                    nc.scalar.copy(wq_hi[:, :, :], wq_raw).then_inc(prep_act, 1)
                    act.wait_ge(prep_act, 2)
                    act.wait_ge(prep_pe, 2)
                    for b in range(B):
                        for m in range(KD):
                            nc.scalar.activation(row[:, b, m * LKV:(m + 1) * LKV], bank[4 + b][:, m * LKV:(m + 1) * LKV],
                                                 ACT.Identity, bias=bkT[:, m:m + 1], scale=SCALE).then_inc(prep_act, 1)
                    act.wait_ge(prep_loaded, 16 * (N_PREP + 1))
                    nc.scalar.copy(wo_hi[:, :, :], wo_raw).then_inc(prep_act, 1)

                    def x_hi(n, blk):
                        for i in range(2):
                            act.wait_ge(w_ready[i], 1 if isinstance(blk, int) and blk == 0 else unit(n, X) + 1)
                            nc.scalar.copy(xT_hi[:, 2 * i:2 * i + 2, :],
                                           bank[6 + i][:, :].rearrange("p (k t) -> p k t", k=2)).then_inc(xhi_ready, 1)

                    def q_hi(n, blk):
                        for m in range(KD):
                            i = m // 2
                            act.wait_ge(w_ready[i], 2 if isinstance(blk, int) and blk == 0 else unit(n, Q) + 1)
                            nc.scalar.activation(qT_hi[:, m, :], bank[6 + i][:, (m % 2) * TB:(m % 2 + 1) * TB],
                                                 ACT.Identity, bias=bqT[:, m:m + 1]).then_inc(qhi_ready, 1)

                    def exps(n, a):
                        act.wait_ge(max_ready, 2 * n + a + 1)
                        if not isinstance(n, int) or n > 0:
                            act.wait_ge(pt_ready, 8 * n + 4 * a - 4)
                        for h in range(H):
                            g, hh = divmod(h, HG)
                            ins = nc.scalar.activation(probs[a][:, h, :], bank[g][:, hh * LKV:(hh + 1) * LKV], ACT.Exp,
                                                       bias=neg_max[:, a, h:h + 1], accum_out=sums[:, a, h:h + 1])
                            if hh == HG - 1:
                                ins.then_inc(s_free, 1)

                    def pT_hi_copy(n, a):
                        for g in range(KD):
                            act.wait_ge(pt_ready, 8 * n + 4 * a + g + 1)
                            nc.scalar.copy(pT_hi[:, HG * g:HG * (g + 1), a * P:(a + 1) * P],
                                           bank[4 + g % 2][:, :].rearrange("p (h t) -> p h t", h=HG))\
                              .then_inc(pthi_ready, 1)

                    x_hi(0, 0)
                    q_hi(0, 0)
                    act.wait_ge(prep_dve, 4)

                    def step(n, b_s, b_v):
                        if has(n, 0):
                            exps(n, 0)
                        if has(n, -1):
                            for i in range(2):
                                act.wait_ge(w_ready[i], unit(n, V) + 1)
                                nc.scalar.copy(aT_hi[:, 2 * i:2 * i + 2, :],
                                               bank[6 + i][:, :].rearrange("p (k t) -> p k t", k=2)).then_inc(ahi_ready, 1)
                        if has(n, 1):
                            x_hi(n, n + 1)
                        if has(n, 0):
                            exps(n, 1)
                        if has(n, 1):
                            q_hi(n, n + 1)
                        if has(n, 0):
                            pT_hi_copy(n, 0)
                        if has(n, -1):
                            for a in range(2):
                                act.wait_ge(w_ready[a], unit(n, N) + 1)
                                nc.scalar.copy(xnT[:, a, :, :], bank[6 + a][:, :].rearrange("p (k t) -> p k t", k=KD))\
                                  .then_inc(w_free[a], 1)
                        if has(n, 0):
                            pT_hi_copy(n, 1)
                        if has(n, -1):
                            act.wait_ge(gap_ready, n)
                            nc.scalar.activation(e1[:, :, :], gap[:, :, :], ACT.Exp).then_inc(e1_ready, 1)

                    steps(act, step)

                @block.vector
                def _(dve):
                    PER_STEP, STATS1 = 20, 2
                    state = {"base": 0, "k": 0}

                    def done(ins):
                        ins.then_inc(dve_done, 1)
                        state["k"] += 1

                    def settle():
                        wait_apart(dve, "dve", dve_done, state["base"] + state["k"])

                    def stats1(blk):
                        dve.wait_ge(xin_loaded, 16 * (blk + 1))
                        for a in range(2):
                            done(nc.vector.bn_stats(bn1[:, a, :], xin[:, a, :]))
                        settle()
                        for a in range(2):
                            ins = nc.vector.bn_aggr(mv1[:, a, :], bn1[:, a, :])
                        ins.then_inc(stats1_ready, 1)

                    def xn(blk):
                        dve.wait_ge(rstd1_ready, blk + 1)
                        dve.wait_ge(stats1_ready, blk + 1)
                        for a in range(2):
                            nc.vector.tensor_scalar(xin[:, a, :], xin[:, a, :], mv1[:, a, 0:1], rstd1[:, a:a + 1],
                                                    ALU.subtract, ALU.mult).then_inc(xn_ready, 1)

                    def x_lo(n, blk):
                        for i in range(2):
                            dve.wait_ge(xhi_ready, 2 * blk + i + 1)
                            nc.vector.tensor_tensor(xT_lo[:, 2 * i:2 * i + 2, :],
                                                    bank[6 + i][:, :].rearrange("p (k t) -> p k t", k=2),
                                                    xT_hi[:, 2 * i:2 * i + 2, :].bitcast(fp32), ALU.subtract)\
                              .then_inc(w_free[i], 1)

                    def q_lo(n, blk):
                        for m in range(KD):
                            i = m // 2
                            if m % 2 == 0:
                                dve.wait_ge(qhi_ready, 4 * blk + m + 2)
                            ins = nc.vector.scalar_tensor_tensor(
                                out=qT_lo[:, m, :], in0=bank[6 + i][:, (m % 2) * TB:(m % 2 + 1) * TB],
                                scalar=bqT[:, m:m + 1], in1=qT_hi[:, m, :].bitcast(fp32),
                                op0=ALU.add, op1=ALU.subtract)
                            if m % 2:
                                ins.then_inc(w_free[i], 1)

                    dve.wait_ge(prep_pe, 1)
                    dve.wait_ge(consts_ready, 2)
                    ctxT = xnT
                    for b in range(B):
                        nc.vector.tensor_copy(ctxT[:, b, 0:KI, :], bank[b][:, 0:KI * P].rearrange("p (k t) -> p k t", k=KI))
                    nc.vector.tensor_copy(rwT[:, :, :], bank[2][:, 0:KD * E].rearrange("p (k e) -> p k e", k=KD))\
                      .then_inc(prep_dve, 1)
                    dve.wait_ge(prep_act, 3)
                    nc.vector.tensor_tensor(wq_lo[:, :, :], probs[0][:, :, :].rearrange("p (k a) n -> p k (a n)", k=KD),
                                            wq_hi[:, :, :].bitcast(fp32), ALU.subtract).then_inc(prep_dve, 1)
                    nc.vector.tensor_scalar(gbo_b[:, :], gbo_b[:, :], gates[:, 0:1], None, ALU.mult)
                    dve.wait_ge(prep_pool, 1)
                    dve.wait_ge(prep_act, 3 + B * KD)
                    dve.wait_ge(prep_pe, 2)
                    for b in range(B):
                        for hh in range(HG):
                            rows = slice(DK * hh, DK * (hh + 1))
                            cols = slice(LKV * hh, LKV * (hh + 1))
                            done(nc.vector.tensor_copy(k_hi[b][rows, :, cols],
                                                       row[rows, b, 0:KD * LKV].rearrange("p (m t) -> p m t", m=KD)))
                            vals = bank[6 + b][:, :].rearrange("p (g h d) -> p g h d", g=KD, h=HG)[:, :, hh, :]
                            done(nc.vector.tensor_copy(
                                v_hi[b][:, :, :].rearrange("p (g h) n -> p g h n", g=KD)[:, :, hh, DK * hh:DK * (hh + 1)],
                                vals))
                    settle()
                    for b in range(B):
                        for hh in range(HG):
                            rows = slice(DK * hh, DK * (hh + 1))
                            cols = slice(LKV * hh, LKV * (hh + 1))
                            nc.vector.tensor_tensor(k_lo[b][rows, :, cols],
                                                    row[rows, b, 0:KD * LKV].rearrange("p (m t) -> p m t", m=KD),
                                                    k_hi[b][rows, :, cols].bitcast(fp32), ALU.subtract)
                            vals = bank[6 + b][:, :].rearrange("p (g h d) -> p g h d", g=KD, h=HG)[:, :, hh, :]
                            mine = lambda t: t[b][:, :, :].rearrange("p (g h) n -> p g h n", g=KD)[:, :, hh, DK * hh:DK * (hh + 1)]
                            last = nc.vector.tensor_tensor(mine(v_lo), vals, mine(v_hi).bitcast(fp32), ALU.subtract)
                    last.then_inc(prep_dve, 1)
                    dve.wait_ge(prep_act, 4 + B * KD)
                    nc.vector.tensor_tensor(wo_lo[:, :, :], probs[1][:, :, :].rearrange("p (k a) n -> p k (a n)", k=KD),
                                            wo_hi[:, :, :].bitcast(fp32), ALU.subtract).then_inc(prep_dve, 1)
                    dve.wait_ge(prep_dve, 3)
                    for a in range(2):
                        nc.vector.memset(row[:, a, D:ROW], 0.0)

                    stats1(0)
                    xn(0)
                    x_lo(0, 0)
                    q_lo(0, 0)
                    stats1(1)

                    def maxima(n, a):
                        for g in range(KD):
                            dve.wait_ge(s_ready, 8 * n + 4 * a + g + 1)
                            ins = nc.vector.tensor_reduce(neg_max[:, a, HG * g:HG * (g + 1)],
                                                          bank[g][:, :].rearrange("p (h t) -> p h t", h=HG),
                                                          AX.X, ALU.max, negate=True)
                        ins.then_inc(max_ready, 1)

                    def recips(n, a):
                        dve.wait_ge(s_free, 8 * n + 4 * a + 4)
                        nc.vector.reciprocal(rsums[:, a, :], sums[:, a, :]).then_inc(rs_ready, 1)

                    def pT_lo_sub(n, a):
                        for g in range(KD):
                            dve.wait_ge(pthi_ready, 8 * n + 4 * a + g + 1)
                            nc.vector.tensor_tensor(pT_lo[:, HG * g:HG * (g + 1), a * P:(a + 1) * P],
                                                    bank[4 + g % 2][:, :].rearrange("p (h t) -> p h t", h=HG),
                                                    pT_hi[:, HG * g:HG * (g + 1), a * P:(a + 1) * P].bitcast(fp32),
                                                    ALU.subtract).then_inc(pt_free, 1)

                    def step(n, b_s, b_v):
                        prior = has(n, -1)
                        if has(n, 1):
                            xn(n + 1)
                        if has(n, 0):
                            maxima(n, 0)
                        if prior:
                            for i in range(2):
                                dve.wait_ge(ahi_ready, 2 * (n - 1) + i + 1)
                                nc.vector.tensor_tensor(aT_lo[:, 2 * i:2 * i + 2, :],
                                                        bank[6 + i][:, :].rearrange("p (k t) -> p k t", k=2),
                                                        aT_hi[:, 2 * i:2 * i + 2, :].bitcast(fp32), ALU.subtract)\
                                  .then_inc(w_free[i], 1)
                        if has(n, 1):
                            x_lo(n, n + 1)
                        if has(n, 0):
                            maxima(n, 1)
                            recips(n, 0)
                        if prior:
                            dve.wait_ge(xb_ready, n)
                            for a in range(2):
                                dve.wait_ge(w_ready[a], unit(n, O) + 1)
                                nc.vector.scalar_tensor_tensor(out=xres[:, a, :], in0=bank[6 + a][:, :],
                                                               scalar=gates[:, 0:1], in1=xres[:, a, :],
                                                               op0=ALU.mult, op1=ALU.add).then_inc(w_free[a], 1)
                            for a in range(2):
                                dve.wait_ge(w_free[a], unit(n, O) + 1)
                                done(nc.vector.bn_stats(bn2[:, a, :], xres[:, a, :]))
                            settle()
                            for a in range(2):
                                ins = nc.vector.bn_aggr(mv2[:, a, :], bn2[:, a, :])
                            ins.then_inc(stats2_ready, 1)
                        if has(n, 0):
                            recips(n, 1)
                        if has(n, 1):
                            q_lo(n, n + 1)
                        if prior:
                            dve.wait_ge(rstd2_ready, n)
                            if not isinstance(n, int) or n > 1:
                                dve.wait_ge(scattered, 64 * (n - 1))
                            dve.wait_ge(stats2_ready, n)
                            for a in range(2):
                                done(nc.vector.scalar_tensor_tensor(out=row[:, a, 0:D], in0=xres[:, a, :],
                                                                    scalar=mv2[:, a, 0:1], in1=gamma_b[:, :],
                                                                    op0=ALU.subtract, op1=ALU.mult))
                            settle()
                            for a in range(2):
                                nc.vector.scalar_tensor_tensor(out=row[:, a, 0:D], in0=row[:, a, 0:D],
                                                               scalar=rstd2[:, a:a + 1], in1=beta_b[:, :],
                                                               op0=ALU.mult, op1=ALU.add).then_inc(row_ready, 1)
                        if has(n, 0):
                            pT_lo_sub(n, 0)
                        if prior:
                            for a in range(2):
                                dve.wait_ge(w_ready[a], unit(n, L) + 1)
                                nc.vector.tensor_scalar(logits[:, a, :], bank[6 + a][:, 0:E], CLAMP, -CLAMP,
                                                        ALU.min, ALU.max).then_inc(w_free[a], 1)
                            for a in range(2):
                                wait_apart(dve, "dve", w_free[a], unit(n, L) + 1)
                                done(nc.vector.max(top8[:, a, :], logits[:, a, :]))
                            settle()
                            for a in range(2):
                                done(nc.vector.max_index(topi[:, a, :], top8[:, a, :], logits[:, a, :]))
                            nc.vector.tensor_tensor(gap[:, :, :], top8[:, :, 1:2], top8[:, :, 0:1], ALU.subtract)\
                              .then_inc(gap_ready, 1)
                            settle()
                            done(nc.vector.tensor_copy(idxf[:, :, :], topi[:, :, 0:TOPK]))
                            settle()
                            done(nc.vector.tensor_tensor(
                                onehot[:, :, :, :],
                                expert_id[:, :].unsqueeze(1).unsqueeze(1).to_broadcast([P, 2, TOPK, E]),
                                idxf[:, :, :].unsqueeze(3).to_broadcast([P, 2, TOPK, E]), ALU.is_equal))
                            settle()
                            done(nc.vector.tensor_tensor(chosen[:, :, :], onehot[:, :, 0, :], onehot[:, :, 1, :], ALU.add))
                            settle()
                            nc.vector.tensor_tensor(before[:, 1, :], before[:, 0, :], chosen[:, 0, :], ALU.add)\
                              .then_inc(chosen_ready, 1)
                        if has(n, 0):
                            pT_lo_sub(n, 1)
                        if prior:
                            dve.wait_ge(chosen_ready, n)
                            for a in range(2):
                                dve.wait_ge(w_ready[a], unit(n, C) + 1)
                                nc.vector.tensor_tensor(prod[:, a, :, :], onehot[:, a, :, :],
                                                        bank[6 + a][:, 0:E].unsqueeze(1).to_broadcast([P, TOPK, E]),
                                                        ALU.mult).then_inc(w_free[a], 1)
                            done(nc.vector.tensor_tensor(before[:, 0, :], before[:, 1, :], chosen[:, 1, :], ALU.add))
                            for a in range(2):
                                dve.wait_ge(w_free[a], unit(n, C) + 1)
                            done(nc.vector.tensor_reduce(pos[:, :, :], prod[:, :, :, :], AX.X, ALU.add))
                            dve.wait_ge(e1_ready, n)
                            done(nc.vector.tensor_scalar(zsum[:, :, :], e1[:, :, :], 1.0, 1e-12, ALU.add, ALU.add))
                            settle()
                            done(nc.vector.tensor_scalar(over[:, :, :], pos[:, :, :], float(CAP), float(E * CAP),
                                                         ALU.is_ge, ALU.mult))
                            done(nc.vector.scalar_tensor_tensor(out=slotf[:, :, :], in0=idxf[:, :, :], scalar=float(CAP),
                                                                in1=pos[:, :, :], op0=ALU.mult, op1=ALU.add))
                            done(nc.vector.reciprocal(zinv[:, :, :], zsum[:, :, :]))
                            settle()
                            nc.vector.tensor_scalar(row[:, :, C_W0], zinv[:, :, 0], gates[:, 1:2], None, ALU.mult)
                            nc.vector.scalar_tensor_tensor(out=row[:, :, C_W1], in0=e1[:, :, 0], scalar=gates[:, 1:2],
                                                           in1=zinv[:, :, 0], op0=ALU.mult, op1=ALU.mult)
                            nc.vector.tensor_copy(row[:, :, C_TOK], tok_count[:, :])
                            nc.vector.tensor_copy(row[:, :, C_IDX], idxf[:, :, 0])
                            nc.vector.tensor_tensor(slot[:, :, :], slotf[:, :, :], over[:, :, :], ALU.add)\
                              .then_inc(slot_ready, 1)
                            done(nc.vector.tensor_scalar(tok_count[:, :], tok_count[:, :], float(-TB), None, ALU.add))
                        if has(n, 2):
                            stats1(n + 2)

                    def counted(n, b_s, b_v):
                        if isinstance(n, int) and n == 0:
                            step(n, b_s, b_v)
                            state["after0"] = state["base"] + state["k"]
                            return
                        late = max(0, n - (NB - 2)) if isinstance(n, int) else 0
                        state["base"], state["k"] = state["after0"] + PER_STEP * (n - 1) - STATS1 * late, 0
                        step(n, b_s, b_v)
                        assert state["k"] == PER_STEP - (0 if has(n, 2) else STATS1), state["k"]

                    steps(dve, counted)

                @block.tensor
                def _(pe):
                    def passes(out_ap, pairs):
                        n, at = 3 * len(pairs), 0
                        for (s_hi, s_lo), (m_hi, m_lo) in pairs:
                            for st, mv in ((s_hi, m_hi), (s_hi, m_lo), (s_lo, m_hi)):
                                last = nc.tensor.matmul(out_ap, st, mv, start=(at == 0), stop=(at == n - 1))
                                at += 1
                        return last

                    pe.wait_ge(prep_loaded, 16 * N_PREP)
                    pe.wait_ge(consts_ready, 2)
                    for b in range(B):
                        for k in range(KI):
                            nc.tensor.transpose(bank[b][:, k * P:(k + 1) * P], row[:, b, k * P:(k + 1) * P], ident[:, :])
                    for k in range(KD):
                        a, c = divmod(k, KD // 2)
                        last = nc.tensor.transpose(bank[2][:, k * E:(k + 1) * E],
                                                   row[0:E, a, DI + c * P:DI + (c + 1) * P], ident[0:E, 0:E])
                    last.then_inc(prep_pe, 1)
                    pe.wait_ge(prep_dve, 1)
                    ctxT = xnT
                    for b in range(B):
                        for m in range(KD):
                            for k in range(KI):
                                nc.tensor.matmul(bank[4 + b][:, m * LKV:(m + 1) * LKV], xin[:, k, m * P:(m + 1) * P],
                                                 ctxT[:, b, k, :], start=(k == 0), stop=(k == KI - 1))
                        for k in range(KI):
                            nc.tensor.matmul(bank[6 + b][:, :], ctxT[:, b, k, :], xres[:, k, :], start=(k == 0), stop=False)
                        last = nc.tensor.matmul(bank[6 + b][:, :], ones[0:1, :], bv_row[:, :], start=False, stop=True)
                    last.then_inc(prep_pe, 1)
                    pe.wait_ge(prep_dve, 3)

                    def transposes_x(blk, at):
                        pe.wait_ge(xn_ready, 2 * blk + 2)
                        for i in range(2):
                            if at is not None:
                                pe.wait_ge(w_free[i], at)
                            for kk in range(2):
                                for a in range(2):
                                    last = nc.tensor.transpose(bank[6 + i][:, kk * TB + a * P:kk * TB + (a + 1) * P],
                                                               xin[:, a, (2 * i + kk) * P:(2 * i + kk + 1) * P], ident[:, :])
                            last.then_inc(w_ready[i], 1)

                    def queries(blk, at):
                        pe.wait_ge(w_free[0], at)
                        pe.wait_ge(w_free[1], at)
                        for m in range(KD):
                            i, cols = m // 2, slice((m % 2) * TB, (m % 2 + 1) * TB)
                            last = passes(bank[6 + i][:, cols],
                                          [((wq_hi[:, k, m * P:(m + 1) * P], wq_lo[:, k, m * P:(m + 1) * P]),
                                            (xT_hi[:, k, :], xT_lo[:, k, :])) for k in range(KD)])
                            if m % 2:
                                last.then_inc(w_ready[i], 1)

                    transposes_x(0, None)
                    queries(0, 1)

                    def scores(n, a, b):
                        for g in range(KD):
                            if not isinstance(n, int) or 8 * n + 4 * a >= 4:
                                pe.wait_ge(s_free, 8 * n + 4 * a + g - 3)
                            passes(bank[g][:, :], [((qT_hi[:, g, a * P:(a + 1) * P], qT_lo[:, g, a * P:(a + 1) * P]),
                                                    (k_hi[b][:, g, :], k_lo[b][:, g, :]))]).then_inc(s_ready, 1)

                    def probs_T(n, a):
                        pe.wait_ge(pn_ready, 2 * n + a + 1)
                        for g in range(KD):
                            if not isinstance(n, int) or 8 * n + 4 * a + g >= 2:
                                pe.wait_ge(pt_free, 8 * n + 4 * a + g - 1)
                            for hh in range(HG):
                                last = nc.tensor.transpose(bank[4 + g % 2][:, hh * P:(hh + 1) * P],
                                                           probs[a][:, HG * g + hh, :], ident[:, :])
                            last.then_inc(pt_ready, 1)

                    def step(n, b_s, b_v):
                        prior = has(n, -1)
                        if has(n, 0):
                            for i in range(2):
                                pe.wait_ge(w_free[i], 2 if isinstance(n, int) and n == 0 else
                                           4 if isinstance(n, int) and n == 1 else unit(n - 1, Q) + 1)
                            scores(n, 0, b_s)
                        if prior:
                            pe.wait_ge(pt_free, 8 * n)
                            for i in range(2):
                                pe.wait_ge(w_free[i], unit(n, V))
                                for gg in range(2):
                                    g = 2 * i + gg
                                    last = passes(bank[6 + i][:, gg * TB:(gg + 1) * TB],
                                                  [((v_hi[b_v][:, h, :], v_lo[b_v][:, h, :]), (pT_hi[:, h, :], pT_lo[:, h, :]))
                                                   for h in range(HG * g, HG * (g + 1))])
                                last.then_inc(w_ready[i], 1)
                        if has(n, 1):
                            transposes_x(n + 1, unit(n, X))
                        if has(n, 0):
                            scores(n, 1, b_s)
                        if prior:
                            for i in range(2):
                                pe.wait_ge(w_free[i], unit(n, O))
                            if isinstance(n, int) and n == 1 or not isinstance(n, int):
                                pe.wait_ge(prep_dve, 4)
                            for a in range(2):
                                passes(bank[6 + a][:, :],
                                       [((aT_hi[:, k, a * P:(a + 1) * P], aT_lo[:, k, a * P:(a + 1) * P]),
                                         (wo_hi[:, k, :], wo_lo[:, k, :])) for k in range(KD)]).then_inc(w_ready[a], 1)
                        if has(n, 1):
                            queries(n + 1, unit(n, Q))
                        if has(n, 0):
                            probs_T(n, 0)
                        if prior:
                            for a in range(2):
                                pe.wait_ge(row_ready, 2 * (n - 1) + a + 1)
                                pe.wait_ge(w_free[a], unit(n, N))
                                for k in range(KD):
                                    last = nc.tensor.transpose(bank[6 + a][:, k * P:(k + 1) * P],
                                                               row[:, a, k * P:(k + 1) * P], ident[:, :])
                                last.then_inc(w_ready[a], 1)
                            for a in range(2):
                                pe.wait_ge(w_free[a], unit(n, L))
                                for k in range(KD):
                                    last = nc.tensor.matmul(bank[6 + a][:, 0:E], xnT[:, a, k, :], rwT[:, k, :],
                                                            start=(k == 0), stop=(k == KD - 1))
                                last.then_inc(w_ready[a], 1)
                        if has(n, 0):
                            probs_T(n, 1)
                        if prior:
                            pe.wait_ge(chosen_ready, n)
                            for a in range(2):
                                pe.wait_ge(w_free[a], unit(n, C))
                                nc.tensor.matmul(bank[6 + a][:, 0:E], upper[:, :], chosen[:, a, :], start=True, stop=False)
                                nc.tensor.matmul(bank[6 + a][:, 0:E], ones[:, :], before[:, a, :], start=False, stop=True)\
                                  .then_inc(w_ready[a], 1)

                    steps(pe, step)

        with ExitStack() as stage:
            def sb(name, shape, dt=fp32):
                return stage.enter_context(nc.sbuf_tensor(name, shape, dt))

            raw12 = [sb(f"raw12_{i}", [P, NU12, D]) for i in range(2)]
            raw3 = [sb(f"raw3_{i}", [P, KD, FC]) for i in range(2)]
            w12_hi, w12_lo = ([sb(f"w12_{h}{i}", [P, KD, NU12, P], f32r) for i in range(2)] for h in ("hi", "lo"))
            w3_hi, w3_lo = ([sb(f"w3_{h}{i}", [P, NU3, D], f32r) for i in range(2)] for h in ("hi", "lo"))
            xrow = [sb(f"xrow{i}", [P, D]) for i in range(XR)]
            xT_hi, xT_lo = (sb(f"slotsT_{h}", [P, KD, CAP], f32r) for h in ("hi", "lo"))
            silu = [sb(f"silu{i}", [P, SB]) for i in range(2)]
            h32 = [sb(f"h32_{i}", [P, SB]) for i in range(2)]
            h_hi, h_lo = ([sb(f"h_{h}{i}", [P, NU3, SB], f32r) for i in range(2)] for h in ("hi", "lo"))
            yacc = sb("yacc", [P, NT, D])
            yout = sb("yout", [P, NT, D])
            meta = sb("meta", [P, NT, 4])
            first_is_e = sb("first_is_e", [P, NT])
            wdiff = sb("wdiff", [P, NT])
            wslot = sb("wslot", [P, NT])
            token = sb("token", [P, NT], i32)
            e_now = sb("e_now", [P, 1])

            raw12_loaded, raw3_loaded = ([sem(f"{n}_loaded{i}") for i in range(2)] for n in ("raw12", "raw3"))
            xrow_loaded = [sem(f"xrow_loaded{i}") for i in range(XR)]
            tp_ready = sem("tp_ready")
            whi_ready, wlo_ready = sem("whi_ready"), sem("wlo_ready")
            xThi_ready, xTlo_ready = sem("slotsT_hi_ready"), sem("slotsT_lo_ready")
            g_ready, u_ready = sem("g_ready"), sem("u_ready")
            silu_ready, h32_ready = sem("silu_ready"), sem("h32_ready")
            hhi_ready, hlo_ready = sem("hhi_ready"), sem("hlo_ready")
            y_ready, y_added = sem("y_ready"), sem("y_added")
            yout_ready, yout_free = sem("yout_ready"), sem("yout_free")
            meta_loaded, weights_ready, added = sem("meta_loaded"), sem("weights_ready"), sem("added")
            idx_done = sem("idx_done")

            GB, UB, YB, TBK = bank[0:2], bank[2:4], bank[4:6], bank[6:8]
            STEPS = NSB * NU3
            UNITS = NU * NCH + NT
            ECH = E * NCH

            def chunk_order(c):
                order = []
                for s in range(NSB):
                    for j in range(NU3):
                        order.append(("G1", s, j))
                        if s == 0:
                            order += [("U", 2 * j, 0), ("U", 2 * j + 1, 0)]
                        if s == 1:
                            order.append(("U", NU12 + j, 0))
                    if c == NCH - 1:
                        order += [("X", 2 * s, 0), ("X", 2 * s + 1, 0)]
                    if s:
                        order.append(("G2", s - 1, 0))
                order.append(("G2", NSB - 1, 0))
                return order

            steps_before = lambda e, c: (e * NCH + c) * STEPS
            tiles_before = lambda e, c: (e * NCH + c) * NT

            def tp_at(e, c, u=None, t=None):
                at = NU + NT + e * UNITS + c * NU
                if t is None:
                    return at + u + (2 if c == NCH - 1 and u >= NU12 else 0)
                return at + t + (NU12 if t < 2 else NU)

            with nc.Block() as block:

                @block.sync
                def _(sp):
                    def load_weights(e, c, par):
                        src12 = w12.rearrange("e (h c r p) d -> h e c p r d", h=2, c=NCH, p=P)
                        for half in range(2):
                            sp.dma_start(raw12[par][:, half * NU3:(half + 1) * NU3, :],
                                         src12[half, bass.ds(e, 1), c, :, :, :].rearrange("e p r d -> (e p) r d"))\
                              .then_inc(raw12_loaded[par], 16)
                        src3 = w3.rearrange("e (k p) (c f) -> e c p k f", p=P, f=FC)[bass.ds(e, 1), c, :, :, :]
                        sp.dma_start(raw3[par][:, :, :], src3.rearrange("e p k f -> (e p) k f"))\
                          .then_inc(raw3_loaded[par], 16)

                    load_weights(0, 0, 0)
                    load_weights(0, 1, 1)
                    with sp.Fori(0, E - 1) as e:
                        for c in range(NCH):
                            sp.wait_ge(whi_ready, (e * NCH + c + 1) * NU)
                            load_weights(e + (c + 2) // NCH, (c + 2) % NCH, c % 2)
                    for c in range(NCH - 1):
                        sp.wait_ge(whi_ready, ((E - 1) * NCH + c + 1) * NU)
                        load_weights(E - 1 if c + 2 < NCH else 0, (c + 2) % NCH, c % 2)

                @block.gpsimd
                def _(pool):
                    def load_slots(e, t):
                        r = t % XR
                        pool.dma_start(xrow[r][:, :], xbuf[bass.ds(e * CAP + t * P, P), 0:D]).then_inc(xrow_loaded[r], 16)

                    nc.gpsimd.memset(e_now[:, :], 0.0).then_inc(idx_done, 1)
                    pool.sem_inc(yout_free, NT)
                    for t in range(NT):
                        if t >= XR:
                            wait_apart(pool, "pool", xTlo_ready, t - XR + 1)
                        load_slots(0, t)

                    def expert(e, nxt):
                        pool.dma_start(meta[:, :, :],
                                       xbuf[bass.ds(e * CAP, CAP), D:D + 4].rearrange("(t p) c -> p t c", p=P))\
                            .then_inc(meta_loaded, 16)
                        wait_apart(pool, "pool", xTlo_ready, NT * (e + 1))
                        for t in range(XR):
                            load_slots(nxt, t)
                        wait_apart(pool, "pool", meta_loaded, 16 * (e + 1))
                        wait_apart(pool, "pool", idx_done, 3 * e + 1)
                        nc.gpsimd.tensor_scalar(token[:, :], meta[:, :, 0], -1.0, float(T), ALU.mult, ALU.add)
                        nc.gpsimd.tensor_scalar(first_is_e[:, :], meta[:, :, 3], e_now[:, 0:1], None, ALU.is_equal)
                        nc.gpsimd.tensor_tensor(wdiff[:, :], meta[:, :, 1], meta[:, :, 2], ALU.subtract).then_inc(idx_done, 1)
                        pool.wait_ge(idx_done, 3 * e + 2)
                        nc.gpsimd.tensor_tensor(wdiff[:, :], wdiff[:, :], first_is_e[:, :], ALU.mult).then_inc(idx_done, 1)
                        pool.wait_ge(idx_done, 3 * e + 3)
                        nc.gpsimd.tensor_tensor(wslot[:, :], wdiff[:, :], meta[:, :, 2], ALU.add).then_inc(weights_ready, 1)
                        nc.gpsimd.tensor_scalar_add(e_now[:, :], e_now[:, :], 1.0).then_inc(idx_done, 1)
                        for t in range(NT):
                            if t < XR:
                                wait_apart(pool, "pool", xTlo_ready, NT * (e + 1) + t + 1)
                                load_slots(nxt, t + XR)
                        wait_apart(pool, "pool", idx_done, 3 * e + 4)
                        for t in range(NT):
                            wait_apart(pool, "pool", yout_ready, NT * (e + 1) + t + 1)
                            nc.gpsimd.indirect_dma_start(
                                out=out_tok, out_offset=bass.IndirectOffsetOnAxis(ap=token[:, t:t + 1], axis=0),
                                in_=yout[:, t, :], in_offset=None, bounds_check=T - 1, oob_is_err=False,
                                compute_op=ALU.add).then_inc(added, 16)
                        wait_apart(pool, "pool", added, 16 * NT * (e + 1))
                        pool.sem_inc(yout_free, NT)

                    with pool.Fori(0, E - 1) as e:
                        expert(e, e + 1)
                    expert(E - 1, 0)

                @block.scalar
                def _(act):
                    def w_hi(par, u, at):
                        act.wait_ge(tp_ready, at + 1)
                        if u < NU12:
                            dst, src = w12_hi[par][:, :, u, :], TBK[u % 2][:, :].rearrange("p (k f) -> p k f", k=KD)
                        else:
                            dst, src = w3_hi[par][:, u - NU12, :], TBK[u % 2][:, :]
                        nc.scalar.copy(dst, src).then_inc(whi_ready, 1)

                    def slots_hi(t, at):
                        act.wait_ge(tp_ready, at + 1)
                        nc.scalar.copy(xT_hi[:, :, t * P:(t + 1) * P], TBK[t % 2][:, :].rearrange("p (k t) -> p k t", k=KD))\
                          .then_inc(xThi_ready, 1)

                    act.sem_inc(yout_ready, NT)
                    for u in range(NU):
                        w_hi(0, u, u)
                    for t in range(NT):
                        slots_hi(t, NU + t)

                    with act.Fori(0, E) as e:
                        for c in range(NCH):
                            for what, i, j in chunk_order(c):
                                q = i * NU3 + j
                                if what == "G1":
                                    at = steps_before(e, c) + q
                                    act.wait_ge(g_ready, at + 1)
                                    if c or q >= 2:
                                        act.wait_ge(h32_ready, at - 1)
                                    nc.scalar.activation(silu[q % 2][:, :], GB[q % 2][:, 0:SB], ACT.Silu).then_inc(silu_ready, 1)
                                    act.wait_ge(h32_ready, at + 1)
                                    nc.scalar.copy(h_hi[i % 2][:, j, :], h32[q % 2][:, :]).then_inc(hhi_ready, 1)
                                elif what == "U":
                                    w_hi((c + 1) % 2, i, tp_at(e, c, u=i))
                                elif what == "X":
                                    slots_hi(i, tp_at(e, c, t=i))
                                elif c == NCH - 1:
                                    if i == 0:
                                        act.wait_ge(weights_ready, e + 1)
                                        act.wait_ge(yout_free, NT * (e + 1))
                                    for t in (2 * i, 2 * i + 1):
                                        act.wait_ge(y_added, tiles_before(e, c) + t + 3)
                                        nc.scalar.activation(yout[:, t, :], yacc[:, t, :], ACT.Copy,
                                                             scale=wslot[:, t:t + 1]).then_inc(yout_ready, 1)

                @block.vector
                def _(dve):
                    def w_lo(par, u, count):
                        dve.wait_ge(whi_ready, count)
                        if u < NU12:
                            dst, src = w12_lo[par][:, :, u, :], TBK[u % 2][:, :].rearrange("p (k f) -> p k f", k=KD)
                            hi = w12_hi[par][:, :, u, :]
                        else:
                            dst, src, hi = w3_lo[par][:, u - NU12, :], TBK[u % 2][:, :], w3_hi[par][:, u - NU12, :]
                        nc.vector.tensor_tensor(dst, src, hi.bitcast(fp32), ALU.subtract).then_inc(wlo_ready, 1)

                    def slots_lo(t, count):
                        dve.wait_ge(xThi_ready, count)
                        cols = slice(t * P, (t + 1) * P)
                        nc.vector.tensor_tensor(xT_lo[:, :, cols], TBK[t % 2][:, :].rearrange("p (k t) -> p k t", k=KD),
                                                xT_hi[:, :, cols].bitcast(fp32), ALU.subtract).then_inc(xTlo_ready, 1)

                    dve.sem_inc(y_added, 2)
                    for u in range(NU):
                        w_lo(0, u, u + 1)
                    for t in range(NT):
                        slots_lo(t, t + 1)

                    with dve.Fori(0, E) as e:
                        for c in range(NCH):
                            for what, i, j in chunk_order(c):
                                q = i * NU3 + j
                                if what == "G1":
                                    at = steps_before(e, c) + q
                                    dve.wait_ge(u_ready, at + 1)
                                    dve.wait_ge(silu_ready, at + 1)
                                    nc.vector.tensor_tensor(h32[q % 2][:, :], silu[q % 2][:, :], UB[q % 2][:, 0:SB], ALU.mult)\
                                      .then_inc(h32_ready, 1)
                                    dve.wait_ge(hhi_ready, at + 1)
                                    nc.vector.tensor_tensor(h_lo[i % 2][:, j, :], h32[q % 2][:, :],
                                                            h_hi[i % 2][:, j, :].bitcast(fp32), ALU.subtract).then_inc(hlo_ready, 1)
                                elif what == "U":
                                    w_lo((c + 1) % 2, i, (e * NCH + c + 1) * NU + i + 1)
                                elif what == "X":
                                    slots_lo(i, NT * (e + 1) + i + 1)
                                else:
                                    for t in (2 * i, 2 * i + 1):
                                        dve.wait_ge(y_ready, tiles_before(e, c) + t + 1)
                                        if c == 0:
                                            dve.wait_ge(yout_ready, NT * e + t + 1)
                                            nc.vector.tensor_copy(yacc[:, t, :], YB[t % 2][:, :]).then_inc(y_added, 1)
                                        else:
                                            dve.wait_ge(y_added, tiles_before(e, c) + t + 3 - NT)
                                            nc.vector.tensor_tensor(yacc[:, t, :], YB[t % 2][:, :], yacc[:, t, :], ALU.add)\
                                              .then_inc(y_added, 1)

                @block.tensor
                def _(pe):
                    def passes(out_ap, pairs):
                        n, at = 3 * len(pairs), 0
                        for (s_hi, s_lo), (m_hi, m_lo) in pairs:
                            for st, mv in ((s_hi, m_hi), (s_hi, m_lo), (s_lo, m_hi)):
                                last = nc.tensor.matmul(out_ap, st, mv, start=(at == 0), stop=(at == n - 1))
                                at += 1
                        return last

                    def weight_unit(par, u):
                        for k in range(KD):
                            src = raw12[par][:, u, k * P:(k + 1) * P] if u < NU12 else \
                                raw3[par][:, k, (u - NU12) * P:(u - NU12 + 1) * P]
                            last = nc.tensor.transpose(TBK[u % 2][:, k * P:(k + 1) * P], src, ident[:, :])
                        last.then_inc(tp_ready, 1)

                    def slot_unit(t):
                        for k in range(KD):
                            last = nc.tensor.transpose(TBK[t % 2][:, k * P:(k + 1) * P],
                                                       xrow[t % XR][:, k * P:(k + 1) * P], ident[:, :])
                        last.then_inc(tp_ready, 1)

                    pe.wait_ge(raw12_loaded[0], 32)
                    pe.wait_ge(raw3_loaded[0], 16)
                    for u in range(NU):
                        if u >= 2:
                            pe.wait_ge(wlo_ready, u - 1)
                        weight_unit(0, u)
                    for t in range(NT):
                        if t < 2:
                            pe.wait_ge(wlo_ready, NU - 1 + t)
                        else:
                            pe.wait_ge(xTlo_ready, t - 1)
                        pe.wait_ge(xrow_loaded[t % XR], 16 * (t // XR + 1))
                        slot_unit(t)

                    with pe.Fori(0, E) as e:
                        for c in range(NCH):
                            par = c % 2
                            order = chunk_order(c)
                            units = [w for w in order if w[0] in "UX"]
                            for what, i, j in order:
                                q = i * NU3 + j
                                if what == "G1":
                                    at = steps_before(e, c) + q
                                    if q == 0:
                                        pe.wait_ge(wlo_ready, (e * NCH + c) * NU + NU12)
                                    if c == 0 and j == 0:
                                        pe.wait_ge(xTlo_ready, NT * e + 2 * i + 2)
                                    slots = slice(i * SB, (i + 1) * SB)
                                    moving = [(xT_hi[:, k, slots], xT_lo[:, k, slots]) for k in range(KD)]
                                    stat = lambda r: [(w12_hi[par][:, k, r, :], w12_lo[par][:, k, r, :]) for k in range(KD)]
                                    if c or q >= 2:
                                        pe.wait_ge(silu_ready, at - 1)
                                    passes(GB[q % 2][:, 0:SB], list(zip(stat(j), moving))).then_inc(g_ready, 1)
                                    if c or q >= 2:
                                        pe.wait_ge(h32_ready, at - 1)
                                    passes(UB[q % 2][:, 0:SB], list(zip(stat(NU3 + j), moving))).then_inc(u_ready, 1)
                                elif what in "UX":
                                    n = units.index((what, i, j))
                                    if n >= 2:
                                        k0, i0, _ = units[n - 2]
                                    elif c:
                                        k0, i0 = "U", n - 2
                                    else:
                                        k0, i0 = None, None
                                    if k0 == "U":
                                        pe.wait_ge(wlo_ready, (e * NCH + c + 1) * NU + i0 + 1)
                                    elif k0 == "X":
                                        pe.wait_ge(xTlo_ready, NT * (e + 1) + i0 + 1)
                                    else:
                                        pe.wait_ge(xTlo_ready, NT * (e + 1) - 1 + n)
                                    if what == "U":
                                        if i == 0:
                                            pe.wait_ge(raw12_loaded[(c + 1) % 2], 32 * (e * (NCH // 2) + (c + 1) // 2 + 1))
                                        if i == NU12:
                                            pe.wait_ge(raw3_loaded[(c + 1) % 2], 16 * (e * (NCH // 2) + (c + 1) // 2 + 1))
                                        weight_unit((c + 1) % 2, i)
                                    else:
                                        pe.wait_ge(xrow_loaded[i % XR], 16 * ((e + 1) * (NT // XR) + i // XR + 1))
                                        slot_unit(i)
                                else:
                                    pe.wait_ge(hlo_ready, steps_before(e, c) + (i + 1) * NU3)
                                    if i == 0:
                                        pe.wait_ge(wlo_ready, (e * NCH + c + 1) * NU)
                                    for tt in range(2):
                                        t = 2 * i + tt
                                        pe.wait_ge(y_added, tiles_before(e, c) + t + 1)
                                        cols = slice(tt * P, (tt + 1) * P)
                                        passes(YB[tt][:, :], [((h_hi[i % 2][:, f, cols], h_lo[i % 2][:, f, cols]),
                                                               (w3_hi[par][:, f, :], w3_lo[par][:, f, :]))
                                                              for f in range(NU3)]).then_inc(y_ready, 1)


_INS = ['x', 'ctx_512', 'g_xattn', 'g_ffn', 'L0_xattn_Wq', 'L0_xattn_bq', 'L0_xattn_Wk', 'L0_xattn_bk', 'L0_xattn_Wv',
        'L0_xattn_bv', 'L0_xattn_Wo', 'L0_xattn_bo', 'L0_ffn_ln_gamma', 'L0_ffn_ln_beta', 'L0_ffn_router_w',
        'L0_ffn_w12', 'L0_ffn_w3']
_OUTS = [((2, 2048, 512), 'float32')]


def kernel(**inputs):
    import numpy as _np
    import concourse.bacc as _bacc
    from concourse import mybir as _mybir
    from concourse.bass_utils import run_bass_kernel_spmd as _run

    nc = _bacc.Bacc("TRN2", target_bir_lowering=False, num_devices=1)
    arrays, args = {}, []
    for name in _INS:
        a = _np.ascontiguousarray(inputs[name])
        arrays[f"in_{name}_dram"] = a
        args.append(nc.dram_tensor(f"in_{name}_dram", a.shape, _mybir.dt.from_np(a.dtype), kind="ExternalInput").ap())
    for i, (shape, dtype) in enumerate(_OUTS):
        dt = _mybir.dt.from_np(_np.dtype(dtype))
        args.append(nc.dram_tensor(f"out_{i}_dram", shape, dt, kind="ExternalOutput").ap())
    flamingo_gated_layer(nc, *args)
    r = _run(nc, [arrays], core_ids=[0])
    return r.results[0]["out_0_dram"]
```

```python
import concourse.bass as bass
from concourse import mybir
from contextlib import ExitStack


def flamingo_gated_layer(
    nc: bass.Bass,
    x: bass.AP,
    ctx_img: bass.AP,
    g_xattn: bass.AP,
    g_ffn: bass.AP,
    Wq: bass.AP,
    bq: bass.AP,
    Wk: bass.AP,
    bk: bass.AP,
    Wv: bass.AP,
    bv: bass.AP,
    Wo: bass.AP,
    bo: bass.AP,
    ln_gamma: bass.AP,
    ln_beta: bass.AP,
    router_w: bass.AP,
    w12: bass.AP,
    w3: bass.AP,
    out: bass.AP,
):
    fp32, f32r = mybir.dt.float32, mybir.dt.float32r
    i32, u32 = mybir.dt.int32, mybir.dt.uint32
    ALU = mybir.AluOpType
    ACT = mybir.ActivationFunctionType
    AX = mybir.AxisListType

    P = 128
    B, S, D = x.shape
    LKV, DI = ctx_img.shape[1], ctx_img.shape[2]
    H = 16
    DK = D // H
    SCALE = float(DK) ** -0.5
    E, F2, _ = w12.shape
    F = F2 // 2
    TOPK = 2
    T = B * S
    CAP = -(-T * TOPK * 5 // (4 * E))
    EPS = 1e-5
    CLAMP = 10000.0

    KD = D // P
    KI = DI // P
    HG = H // KD
    TB = 2 * P
    NB = T // TB
    NBB = NB // B
    NT = CAP // P
    SB = 2 * P
    NSB = CAP // SB
    FC = 2 * P
    NCH = F // FC
    NU12 = 2 * FC // P
    NU3 = FC // P
    NU = NU12 + NU3
    ROW = D + 8
    C_TOK, C_W0, C_W1, C_IDX = D, D + 1, D + 2, D + 3

    x_tok = x.rearrange("b s d -> (b s) d")
    out_tok = out.rearrange("b s d -> (b s) d")
    xbuf = nc.dram_tensor("expert_rows", [E * CAP, ROW], fp32, kind="Internal").ap()

    with ExitStack() as whole:
        def sem(name):
            return whole.enter_context(nc.semaphore(name))

        stepped = {name: sem(f"stepped_{name}") for name in ("pool", "dve", "sp")}

        def wait_apart(eng, name, semaphore, value):
            eng.wait_ge(semaphore, value)
            eng.sem_inc(stepped[name], 1)

        ident = whole.enter_context(nc.sbuf_tensor("ident", [P, P], fp32))
        counts = whole.enter_context(nc.sbuf_tensor("counts", [1, E], i32))
        bank = [whole.enter_context(nc.psum_tensor(f"bank{i}", [P, 512], fp32)) for i in range(8)]

        with ExitStack() as stage:
            def sb(name, shape, dt=fp32):
                return stage.enter_context(nc.sbuf_tensor(name, shape, dt))

            upper = sb("upper", [P, P])
            ones = sb("ones", [P, P])
            zeros = sb("zeros", [P, 2 * ROW])
            expert_id = sb("expert_id", [P, E])
            neg_half = sb("neg_half", [P, 2])
            tok_count = sb("tok_count", [P, 2])
            gates = sb("gates", [P, 2])
            bqT = sb("bqT", [P, KD])
            bkT = sb("bkT", [P, KD])
            bv_row = sb("bv_row", [1, D])
            gamma_b = sb("gamma_b", [P, D])
            beta_b = sb("beta_b", [P, D])
            gbo_b = sb("gbo_b", [P, D])
            rwT = sb("rwT", [P, KD, E])
            wq_hi, wq_lo = (sb(f"wq_{h}", [P, KD, D], f32r) for h in ("hi", "lo"))
            wo_hi, wo_lo = (sb(f"wo_{h}", [P, KD, D], f32r) for h in ("hi", "lo"))
            k_hi, k_lo = ([sb(f"k_{h}{b}", [P, KD, HG * LKV], f32r) for b in range(B)] for h in ("hi", "lo"))
            v_hi, v_lo = ([sb(f"v_{h}{b}", [P, H, P], f32r) for b in range(B)] for h in ("hi", "lo"))
            xin = sb("xin", [P, 2, D])
            xT_hi, xT_lo = (sb(f"xT_{h}", [P, KD, TB], f32r) for h in ("hi", "lo"))
            qT_hi, qT_lo = (sb(f"qT_{h}", [P, KD, TB], f32r) for h in ("hi", "lo"))
            probs = sb("probs", [P, 2, H, LKV])
            pT_hi, pT_lo = (sb(f"pT_{h}", [P, H, TB], f32r) for h in ("hi", "lo"))
            aT_hi, aT_lo = (sb(f"aT_{h}", [P, KD, TB], f32r) for h in ("hi", "lo"))
            xres = sb("xres", [P, 2, D])
            row = sb("row", [P, 2, ROW])
            xnT = sb("xnT", [P, 2, KD, P])
            neg_max = sb("neg_max", [P, 2, H])
            sums = sb("sums", [P, 2, H])
            rsums = sb("rsums", [P, 2, H])
            bn1, bn2 = (sb(f"bn{i}", [P, 2, 6]) for i in (1, 2))
            mv1, mv2 = (sb(f"mv{i}", [P, 2, 2]) for i in (1, 2))
            var1, var2 = (sb(f"var{i}", [P, 2]) for i in (1, 2))
            rstd1, rstd2 = (sb(f"rstd{i}", [P, 2]) for i in (1, 2))
            shift1 = sb("shift1", [P, 2])
            logits = sb("logits", [P, 2, E])
            top8 = sb("top8", [P, 2, 8])
            topi = sb("topi", [P, 2, 8], u32)
            idxf = sb("idxf", [P, 2, TOPK])
            gap = sb("gap", [P, 2, 1])
            e1 = sb("e1", [P, 2, 1])
            zsum = sb("zsum", [P, 2, 1])
            zinv = sb("zinv", [P, 2, 1])
            onehot = sb("onehot", [P, 2, TOPK, E])
            chosen = sb("chosen", [P, 2, E])
            before = sb("before", [P, 2, E])
            prod = sb("prod", [P, 2, TOPK, E])
            pos = sb("pos", [P, 2, TOPK])
            over = sb("over", [P, 2, TOPK])
            slotf = sb("slotf", [P, 2, TOPK])
            slot = sb("slot", [P, 2, TOPK], i32)

            prep_loaded = sem("prep_loaded")
            consts_ready, prep_pe, prep_act, prep_dve, prep_pool = (
                sem(n) for n in ("consts_ready", "prep_pe", "prep_act", "prep_dve", "prep_pool"))
            zero_filled = sem("zero_filled")
            cleared, prep_split = sem("cleared"), sem("prep_split")
            xin_loaded, xres_loaded, x1_stored = sem("xin_loaded"), sem("xres_loaded"), sem("x1_stored")
            stats1_done, stats1_ready, var1_ready, rstd1_ready, xn_ready = (
                sem(n) for n in ("stats1_done", "stats1_ready", "var1_ready", "rstd1_ready", "xn_ready"))
            shift1_mean, shift1_ready = sem("shift1_mean"), sem("shift1_ready")
            x_ready, x_hi, x_lo = sem("x_ready"), sem("x_hi"), sem("x_lo")
            q_ready, q_hi, q_lo = sem("q_ready"), sem("q_hi"), sem("q_lo")
            s_ready, max_ready, exp_done = sem("s_ready"), sem("max_ready"), sem("exp_done")
            rs_ready, pn_ready = sem("rs_ready"), sem("pn_ready")
            pt_ready, pt_hi, pt_lo = sem("pt_ready"), sem("pt_hi"), sem("pt_lo")
            v_ready, a_hi, a_lo = sem("v_ready"), sem("a_hi"), sem("a_lo")
            xb_ready, o_ready, x1_ready = sem("xb_ready"), sem("o_ready"), sem("x1_ready")
            stats2_ready, var2_ready, rstd2_ready, row_ready = (
                sem(n) for n in ("stats2_ready", "var2_ready", "rstd2_ready", "row_ready"))
            n_ready, xnT_ready = sem("n_ready"), sem("xnT_ready")
            l_ready, logits_ready, gap_ready, e1_ready = (
                sem(n) for n in ("l_ready", "logits_ready", "gap_ready", "e1_ready"))
            chosen_ready, c_ready, c_read, slot_ready, scattered = (
                sem(n) for n in ("chosen_ready", "c_ready", "c_read", "slot_ready", "scattered"))
            sums_ready, counts_ready = sem("sums_ready"), sem("counts_ready")
            rows_done = sem("rows_done")

            N_PREP = 14
            S_BANK, PT_BANK = bank[0:2], bank[2:4]
            X_BANK = bank[6:8]
            Q_BANK = [bank[7], bank[5]]
            V_BANK = [bank[4], bank[4]]
            O_BANK = bank[6:8]
            N_BANK = [bank[6], bank[5]]
            L_BANK = C_BANK = bank[5]

            def steps(eng, step):
                for n in range(3):
                    step(n, 0, 0)
                with eng.Fori(3, NBB) as n:
                    step(n, 0, 0)
                step(NBB, 1, 0)
                with eng.Fori(NBB + 1, NB - 2) as n:
                    step(n, 1, 1)
                for n in range(NB - 2, NB + 2):
                    step(n, 1, 1)

            def has(n, ahead):
                return not isinstance(n, int) or 0 <= n + ahead < NB

            with nc.Block() as block:

                @block.sync
                def _(sp):
                    def prep(dst, src, **kw):
                        sp.dma_start(dst, src, **kw).then_inc(prep_loaded, 16)

                    wide = lambda w: w.rearrange("(k p) n -> p k n", p=P)
                    prep(row[:, :, 0:DI], ctx_img.rearrange("b s d -> s b d"))
                    prep(xin[:, :, :], wide(Wk))
                    prep(xres[:, :, :], wide(Wv))
                    prep(row[0:E, 0, DI:DI + D // 2], router_w[:, 0:D // 2])
                    prep(row[0:E, 1, DI:DI + D // 2], router_w[:, D // 2:D])
                    prep(bkT[:, :], bk.rearrange("(m p) -> p m", p=P), allow_slow_non_contiguous=True)
                    prep(bv_row[:, :], bv.rearrange("(a n) -> a n", a=1))
                    prep(gates[:, 0:1], g_xattn.partition_broadcast(P))
                    prep(gates[:, 1:2], g_ffn.partition_broadcast(P))
                    prep(bqT[:, :], bq.rearrange("(m p) -> p m", p=P), allow_slow_non_contiguous=True)
                    prep(gbo_b[:, :], bo.partition_broadcast(P))
                    prep(gamma_b[:, :], ln_gamma.partition_broadcast(P))
                    prep(beta_b[:, :], ln_beta.partition_broadcast(P))
                    prep(probs[:, 0, :, :].rearrange("p (k a) n -> p k (a n)", k=KD), wide(Wq))

                    def load_xin(blk):
                        sp.dma_start(xin[:, :, :], x_tok[bass.ds(blk * TB, TB), :].rearrange("(a p) d -> p a d", p=P))\
                          .then_inc(xin_loaded, 16)

                    def load_xres(blk):
                        sp.dma_start(xres[:, :, :], x_tok[bass.ds(blk * TB, TB), :].rearrange("(a p) d -> p a d", p=P))\
                          .then_inc(xres_loaded, 16)

                    sp.wait_ge(prep_pe, 2)
                    load_xin(0)
                    load_xres(0)
                    sp.wait_ge(consts_ready, 1)
                    flat = xbuf.rearrange("(p r) n -> p (r n)", p=P)
                    FILLS = E * CAP // P // 2

                    def fill(first, last):
                        for i in range(first * FILLS // 4, last * FILLS // 4):
                            sp.dma_start(flat[:, i * 2 * ROW:(i + 1) * 2 * ROW], zeros[:, :]).then_inc(zero_filled, 16)

                    fill(0, 1)
                    sp.wait_ge(x_ready, 2)
                    load_xin(1)
                    fill(1, 2)

                    def step(n, b_s, b_v):
                        if has(n, 2):
                            sp.wait_ge(x_ready, 2 * (n + 1) + 2)
                            load_xin(n + 2)
                        if isinstance(n, int) and n < 2:
                            fill(n + 2, n + 3)
                        if has(n, -2) and has(n, -1):
                            wait_apart(sp, "sp", x1_stored, 16 * (n - 1))
                            sp.wait_ge(row_ready, 2 * (n - 2) + 2)
                            load_xres(n - 1)
                        if has(n, -1):
                            sp.wait_ge(x1_ready, 2 * (n - 1) + 2)
                            sp.dma_start(out_tok[bass.ds((n - 1) * TB, TB), :].rearrange("(a p) d -> p a d", p=P),
                                         xres[:, :, :]).then_inc(x1_stored, 16)

                    steps(sp, step)
                    sp.wait_ge(x1_stored, 16 * NB)

                @block.gpsimd
                def _(pool):
                    nc.gpsimd.memset(zeros[:, :], 0.0).then_inc(consts_ready, 1)
                    nc.gpsimd.memset(ident[:, :], 0.0)
                    nc.gpsimd.memset(upper[:, :], 0.0)
                    nc.gpsimd.memset(ones[:, :], 1.0)
                    nc.gpsimd.memset(neg_half[:, :], -0.5)
                    nc.gpsimd.memset(before[:, 0, :], 0.0).then_inc(cleared, 1)
                    pool.wait_ge(cleared, 1)
                    nc.gpsimd.affine_select(out=ident[:, :], in_=ident[:, :], compare_op=ALU.not_equal, fill=1.0,
                                            base=0, pattern=[[-1, P]], channel_multiplier=1)
                    nc.gpsimd.affine_select(out=upper[:, :], in_=upper[:, :], compare_op=ALU.is_ge, fill=1.0,
                                            base=0, pattern=[[-1, P]], channel_multiplier=1)
                    nc.gpsimd.iota(expert_id[:, :], pattern=[[1, E]], base=0, channel_multiplier=0,
                                   allow_small_or_imprecise_dtypes=True)
                    nc.gpsimd.iota(tok_count[:, :], pattern=[[-P, 2]], base=T, channel_multiplier=-1,
                                   allow_small_or_imprecise_dtypes=True).then_inc(consts_ready, 1)
                    for b in range(B):
                        for t in (k_hi[b], k_lo[b], v_hi[b], v_lo[b]):
                            last = nc.gpsimd.memset(t[:, :, :].bitcast(fp32), 0.0)
                    last.then_inc(prep_pool, 1)

                    def rstd_x(blk):
                        wait_apart(pool, "pool", stats1_ready, blk + 1)
                        nc.gpsimd.tensor_scalar_add(var1[:, :], mv1[:, :, 1], EPS).then_inc(var1_ready, 1)
                        pool.wait_ge(var1_ready, blk + 1)
                        nc.gpsimd.tensor_tensor(rstd1[:, :], var1[:, :], neg_half[:, :], ALU.pow)\
                          .then_inc(rstd1_ready, 1)
                        pool.wait_ge(rstd1_ready, blk + 1)
                        nc.gpsimd.tensor_tensor(shift1[:, :], mv1[:, :, 0], rstd1[:, :], ALU.mult).then_inc(shift1_mean, 1)
                        wait_apart(pool, "pool", shift1_mean, blk + 1)
                        nc.gpsimd.tensor_scalar(shift1[:, :], shift1[:, :], -1.0, None, ALU.mult).then_inc(shift1_ready, 1)

                    def norm(blk, g):
                        heads = slice(HG * g, HG * (g + 1))
                        pool.wait_ge(rs_ready, KD * blk + g + 1)
                        nc.gpsimd.tensor_tensor(probs[:, :, heads, :], probs[:, :, heads, :],
                                                rsums[:, :, heads].unsqueeze(3).to_broadcast([P, 2, HG, LKV]),
                                                ALU.mult).then_inc(pn_ready, 1)

                    def rstd_x1(blk):
                        wait_apart(pool, "pool", stats2_ready, blk + 1)
                        nc.gpsimd.tensor_scalar(var2[:, :], mv2[:, :, 1], 1.0 + EPS, EPS * EPS,
                                                ALU.mult, ALU.add).then_inc(var2_ready, 1)
                        pool.wait_ge(var2_ready, blk + 1)
                        nc.gpsimd.tensor_tensor(rstd2[:, :], var2[:, :], neg_half[:, :], ALU.pow)\
                          .then_inc(rstd2_ready, 1)

                    def add_bias(blk):
                        if isinstance(blk, int) and blk == 0:
                            pool.wait_ge(prep_dve, 3)
                        pool.wait_ge(xres_loaded, 16 * blk + 16)
                        nc.gpsimd.tensor_tensor(xres[:, :, :], xres[:, :, :],
                                                gbo_b[:, :].unsqueeze(1).to_broadcast([P, 2, D]),
                                                ALU.add).then_inc(xb_ready, 1)

                    def scatter(blk):
                        wait_apart(pool, "pool", slot_ready, blk + 1)
                        if isinstance(blk, int) and blk == 0:
                            pool.wait_ge(zero_filled, 16 * (E * CAP // P // 2))
                        for a in range(2):
                            for k in range(TOPK):
                                nc.gpsimd.indirect_dma_start(
                                    out=xbuf[:, :],
                                    out_offset=bass.IndirectOffsetOnAxis(ap=slot[:, a, k:k + 1], axis=0),
                                    in_=row[:, a, :], in_offset=None,
                                    bounds_check=E * CAP - 1, oob_is_err=False).then_inc(scattered, 16)

                    rstd_x(0)
                    pool.wait_ge(xn_ready, 2)
                    rstd_x(1)

                    def step(n, b_s, b_v):
                        if has(n, -1):
                            norm(n - 1, 3)
                        if has(n, -2):
                            rstd_x1(n - 2)
                        if has(n, 0):
                            norm(n, 0)
                            norm(n, 1)
                        if has(n, -1):
                            add_bias(n - 1)
                        if has(n, 2):
                            rstd_x(n + 2)
                        if has(n, 0):
                            norm(n, 2)
                        if has(n, -2):
                            scatter(n - 2)

                    steps(pool, step)
                    pool.wait_ge(scattered, 64 * NB)

                @block.scalar
                def _(act):
                    act.wait_ge(prep_loaded, 16 * N_PREP)
                    nc.scalar.activation(gates[:, :], gates[:, :], ACT.Tanh).then_inc(prep_act, 1)
                    nc.scalar.mul(bkT[:, :], bkT[:, :], SCALE).then_inc(prep_act, 1)
                    wq_raw = probs[:, 0, :, :].rearrange("p (k a) n -> p k (a n)", k=KD)
                    wo_raw = probs[:, 1, :, :].rearrange("p (k a) n -> p k (a n)", k=KD)
                    act.dma_start(wo_raw, Wo.rearrange("(k p) n -> p k n", p=P)).then_inc(prep_loaded, 16)
                    nc.scalar.copy(wq_hi[:, :, :], wq_raw).then_inc(prep_act, 1)
                    act.wait_ge(prep_act, 2)
                    act.wait_ge(prep_pe, 2)
                    for b in range(B):
                        for m in range(KD):
                            nc.scalar.activation(row[:, b, m * LKV:(m + 1) * LKV], bank[4 + b][:, m * LKV:(m + 1) * LKV],
                                                 ACT.Identity, bias=bkT[:, m:m + 1], scale=SCALE).then_inc(prep_act, 1)
                    act.wait_ge(prep_loaded, 16 * (N_PREP + 1))
                    nc.scalar.copy(wo_hi[:, :, :], wo_raw).then_inc(prep_act, 1)

                    def x_halves(blk):
                        for i in range(2):
                            act.wait_ge(x_ready, 2 * blk + i + 1)
                            nc.scalar.copy(xT_hi[:, 2 * i:2 * i + 2, :],
                                           X_BANK[i][:, :].rearrange("p (k t) -> p k t", k=2)).then_inc(x_hi, 1)

                    def q_halves(blk, i):
                        act.wait_ge(q_ready, 2 * blk + i + 1)
                        for m in (2 * i, 2 * i + 1):
                            nc.scalar.activation(qT_hi[:, m, :], Q_BANK[i][:, (m % 2) * TB:(m % 2 + 1) * TB],
                                                 ACT.Identity, bias=bqT[:, m:m + 1]).then_inc(q_hi, 1)

                    def exps(blk, idx):
                        g, t = divmod(idx, 2)
                        act.wait_ge(max_ready, 2 * KD * blk + idx + 1)
                        if not isinstance(blk, int) or blk > 0:
                            act.wait_ge(pt_ready, 2 * KD * (blk - 1) + idx + 1)
                        for hh in range(HG):
                            h = HG * g + hh
                            ins = nc.scalar.activation(probs[:, t, h, :], S_BANK[t][:, hh * LKV:(hh + 1) * LKV], ACT.Exp,
                                                       bias=neg_max[:, t, h:h + 1], accum_out=sums[:, t, h:h + 1])
                        ins.then_inc(exp_done, 1)

                    def pT_halves(blk, g):
                        for t in range(2):
                            act.wait_ge(pt_ready, 2 * KD * blk + 2 * g + t + 1)
                            nc.scalar.copy(pT_hi[:, HG * g:HG * (g + 1), t * P:(t + 1) * P],
                                           PT_BANK[t][:, :].rearrange("p (h t) -> p h t", h=HG)).then_inc(pt_hi, 1)

                    def a_halves(blk, i):
                        act.wait_ge(v_ready, 2 * blk + i + 1)
                        nc.scalar.copy(aT_hi[:, 2 * i:2 * i + 2, :],
                                       V_BANK[i][:, :].rearrange("p (k t) -> p k t", k=2)).then_inc(a_hi, 1)

                    def norm_x(blk):
                        act.wait_ge(shift1_ready, blk + 1)
                        for a in range(2):
                            nc.scalar.activation(xin[:, a, :], xin[:, a, :], ACT.Identity, bias=shift1[:, a:a + 1],
                                                 scale=rstd1[:, a:a + 1]).then_inc(xn_ready, 1)

                    norm_x(0)
                    x_halves(0)
                    q_halves(0, 0)
                    act.wait_ge(prep_dve, 4)

                    def step(n, b_s, b_v):
                        for slot_no in range(2 * KD):
                            if slot_no == 0 and has(n, -1):
                                exps(n - 1, 2 * KD - 1)
                            if slot_no > 0 and has(n, 0):
                                exps(n, slot_no - 1)
                            if slot_no == 0:
                                if has(n, -1):
                                    pT_halves(n - 1, 2)
                                if has(n, 1):
                                    norm_x(n + 1)
                            if slot_no == 1 and has(n, -1):
                                a_halves(n - 1, 0)
                            if slot_no == 2:
                                if has(n, 0):
                                    q_halves(n, 1)
                                if has(n, -1):
                                    pT_halves(n - 1, 3)
                            if slot_no == 3:
                                if has(n, 1):
                                    x_halves(n + 1)
                            if slot_no == 4:
                                if has(n, -1):
                                    a_halves(n - 1, 1)
                                if has(n, 0):
                                    pT_halves(n, 0)
                                if has(n, -2):
                                    for a in range(2):
                                        act.wait_ge(n_ready, 2 * (n - 2) + a + 1)
                                        nc.scalar.copy(xnT[:, a, :, :], N_BANK[a][:, :].rearrange("p (k t) -> p k t", k=KD))\
                                          .then_inc(xnT_ready, 1)
                            if slot_no == 6:
                                if has(n, 1):
                                    q_halves(n + 1, 0)
                                if has(n, 0):
                                    pT_halves(n, 1)
                                if has(n, -2):
                                    act.wait_ge(gap_ready, n - 1)
                                    nc.scalar.activation(e1[:, :, :], gap[:, :, :], ACT.Exp).then_inc(e1_ready, 1)

                    steps(act, step)

                @block.vector
                def _(dve):
                    ROWS = 18
                    state = {"k": 0}

                    def done(ins):
                        ins.then_inc(rows_done, 1)
                        state["k"] += 1

                    def settle(blk):
                        wait_apart(dve, "dve", rows_done, ROWS * blk + state["k"])

                    def stats_x(blk):
                        dve.wait_ge(xin_loaded, 16 * blk + 16)
                        for a in range(2):
                            nc.vector.bn_stats(bn1[:, a, :], xin[:, a, :]).then_inc(stats1_done, 1)
                        wait_apart(dve, "dve", stats1_done, 2 * blk + 2)
                        for a in range(2):
                            ins = nc.vector.bn_aggr(mv1[:, a, :], bn1[:, a, :])
                        ins.then_inc(stats1_ready, 1)

                    def x_rest(blk):
                        for i in range(2):
                            dve.wait_ge(x_hi, 2 * blk + i + 1)
                            nc.vector.tensor_tensor(xT_lo[:, 2 * i:2 * i + 2, :],
                                                    X_BANK[i][:, :].rearrange("p (k t) -> p k t", k=2),
                                                    xT_hi[:, 2 * i:2 * i + 2, :].bitcast(fp32), ALU.subtract)\
                              .then_inc(x_lo, 1)

                    def q_rest(blk, i):
                        dve.wait_ge(q_hi, KD * blk + 2 * i + 2)
                        for m in (2 * i, 2 * i + 1):
                            nc.vector.scalar_tensor_tensor(
                                out=qT_lo[:, m, :], in0=Q_BANK[i][:, (m % 2) * TB:(m % 2 + 1) * TB],
                                scalar=bqT[:, m:m + 1], in1=qT_hi[:, m, :].bitcast(fp32),
                                op0=ALU.add, op1=ALU.subtract).then_inc(q_lo, 1)

                    dve.wait_ge(prep_pe, 1)
                    dve.wait_ge(consts_ready, 2)
                    ctxT = xnT
                    for b in range(B):
                        nc.vector.tensor_copy(ctxT[:, b, 0:KI, :], bank[b][:, 0:KI * P].rearrange("p (k t) -> p k t", k=KI))
                    nc.vector.tensor_copy(rwT[:, :, :], bank[2][:, 0:KD * E].rearrange("p (k e) -> p k e", k=KD))\
                      .then_inc(prep_dve, 1)
                    dve.wait_ge(prep_act, 3)
                    nc.vector.tensor_tensor(wq_lo[:, :, :], probs[:, 0, :, :].rearrange("p (k a) n -> p k (a n)", k=KD),
                                            wq_hi[:, :, :].bitcast(fp32), ALU.subtract).then_inc(prep_dve, 1)
                    nc.vector.tensor_scalar(gbo_b[:, :], gbo_b[:, :], gates[:, 0:1], None, ALU.mult)
                    dve.wait_ge(prep_pool, 1)
                    dve.wait_ge(prep_act, 3 + B * KD)
                    dve.wait_ge(prep_pe, 2)
                    for b in range(B):
                        for hh in range(HG):
                            rows = slice(DK * hh, DK * (hh + 1))
                            cols = slice(LKV * hh, LKV * (hh + 1))
                            nc.vector.tensor_copy(k_hi[b][rows, :, cols],
                                                  row[rows, b, 0:KD * LKV].rearrange("p (m t) -> p m t", m=KD))
                            vals = bank[6 + b][:, :].rearrange("p (g h d) -> p g h d", g=KD, h=HG)[:, :, hh, :]
                            last = nc.vector.tensor_copy(
                                v_hi[b][:, :, :].rearrange("p (g h) n -> p g h n", g=KD)[:, :, hh, DK * hh:DK * (hh + 1)],
                                vals)
                    last.then_inc(prep_split, 1)
                    dve.wait_ge(prep_split, 1)
                    for b in range(B):
                        for hh in range(HG):
                            rows = slice(DK * hh, DK * (hh + 1))
                            cols = slice(LKV * hh, LKV * (hh + 1))
                            nc.vector.tensor_tensor(k_lo[b][rows, :, cols],
                                                    row[rows, b, 0:KD * LKV].rearrange("p (m t) -> p m t", m=KD),
                                                    k_hi[b][rows, :, cols].bitcast(fp32), ALU.subtract)
                            vals = bank[6 + b][:, :].rearrange("p (g h d) -> p g h d", g=KD, h=HG)[:, :, hh, :]
                            mine = lambda t: t[b][:, :, :].rearrange("p (g h) n -> p g h n", g=KD)[:, :, hh, DK * hh:DK * (hh + 1)]
                            last = nc.vector.tensor_tensor(mine(v_lo), vals, mine(v_hi).bitcast(fp32), ALU.subtract)
                    last.then_inc(prep_dve, 1)
                    dve.wait_ge(prep_act, 4 + B * KD)
                    nc.vector.tensor_tensor(wo_lo[:, :, :], probs[:, 1, :, :].rearrange("p (k a) n -> p k (a n)", k=KD),
                                            wo_hi[:, :, :].bitcast(fp32), ALU.subtract).then_inc(prep_dve, 1)
                    dve.wait_ge(prep_dve, 3)
                    for a in range(2):
                        nc.vector.memset(row[:, a, D:ROW], 0.0)

                    stats_x(0)
                    x_rest(0)
                    q_rest(0, 0)
                    stats_x(1)

                    def maxima(n, idx):
                        g, t = divmod(idx, 2)
                        dve.wait_ge(s_ready, 2 * KD * n + idx + 1)
                        nc.vector.tensor_reduce(neg_max[:, t, HG * g:HG * (g + 1)],
                                                S_BANK[t][:, :].rearrange("p (h t) -> p h t", h=HG),
                                                AX.X, ALU.max, negate=True).then_inc(max_ready, 1)

                    def recips(blk, g):
                        heads = slice(HG * g, HG * (g + 1))
                        dve.wait_ge(exp_done, 2 * KD * blk + 2 * g + 2)
                        nc.vector.reciprocal(rsums[:, :, heads], sums[:, :, heads]).then_inc(rs_ready, 1)

                    def pT_rest(blk, g):
                        for t in range(2):
                            heads, cols = slice(HG * g, HG * (g + 1)), slice(t * P, (t + 1) * P)
                            dve.wait_ge(pt_hi, 2 * KD * blk + 2 * g + t + 1)
                            nc.vector.tensor_tensor(pT_lo[:, heads, cols], PT_BANK[t][:, :].rearrange("p (h t) -> p h t", h=HG),
                                                    pT_hi[:, heads, cols].bitcast(fp32), ALU.subtract).then_inc(pt_lo, 1)

                    def a_rest(blk, i):
                        dve.wait_ge(a_hi, 2 * blk + i + 1)
                        nc.vector.tensor_tensor(aT_lo[:, 2 * i:2 * i + 2, :],
                                                V_BANK[i][:, :].rearrange("p (k t) -> p k t", k=2),
                                                aT_hi[:, 2 * i:2 * i + 2, :].bitcast(fp32), ALU.subtract).then_inc(a_lo, 1)

                    def x1(blk, a):
                        dve.wait_ge(xb_ready, blk + 1)
                        dve.wait_ge(o_ready, 2 * blk + a + 1)
                        nc.vector.scalar_tensor_tensor(out=xres[:, a, :], in0=O_BANK[a][:, :],
                                                       scalar=gates[:, 0:1], in1=xres[:, a, :],
                                                       op0=ALU.mult, op1=ALU.add).then_inc(x1_ready, 1)

                    def stats_x1(blk):
                        dve.wait_ge(x1_ready, 2 * blk + 2)
                        for a in range(2):
                            done(nc.vector.bn_stats(bn2[:, a, :], xres[:, a, :]))
                        settle(blk)
                        for a in range(2):
                            ins = nc.vector.bn_aggr(mv2[:, a, :], bn2[:, a, :])
                        ins.then_inc(stats2_ready, 1)

                    def rows(blk):
                        dve.wait_ge(rstd2_ready, blk + 1)
                        if not isinstance(blk, int) or blk > 0:
                            dve.wait_ge(scattered, 64 * blk)
                        dve.wait_ge(stats2_ready, blk + 1)
                        for a in range(2):
                            done(nc.vector.scalar_tensor_tensor(out=row[:, a, 0:D], in0=xres[:, a, :],
                                                                scalar=mv2[:, a, 0:1], in1=gamma_b[:, :],
                                                                op0=ALU.subtract, op1=ALU.mult))
                        settle(blk)
                        for a in range(2):
                            nc.vector.scalar_tensor_tensor(out=row[:, a, 0:D], in0=row[:, a, 0:D],
                                                           scalar=rstd2[:, a:a + 1], in1=beta_b[:, :],
                                                           op0=ALU.mult, op1=ALU.add).then_inc(row_ready, 1)

                    def route(blk):
                        dve.wait_ge(l_ready, blk + 1)
                        nc.vector.tensor_scalar(logits[:, :, :], L_BANK[:, 0:2 * E].rearrange("p (a e) -> p a e", a=2),
                                                CLAMP, -CLAMP, ALU.min, ALU.max).then_inc(logits_ready, 1)
                        wait_apart(dve, "dve", logits_ready, blk + 1)
                        for a in range(2):
                            done(nc.vector.max(top8[:, a, :], logits[:, a, :]))
                        settle(blk)
                        for a in range(2):
                            done(nc.vector.max_index(topi[:, a, :], top8[:, a, :], logits[:, a, :]))
                        nc.vector.tensor_tensor(gap[:, :, :], top8[:, :, 1:2], top8[:, :, 0:1], ALU.subtract)\
                          .then_inc(gap_ready, 1)
                        settle(blk)
                        done(nc.vector.tensor_copy(idxf[:, :, :], topi[:, :, 0:TOPK]))
                        settle(blk)
                        done(nc.vector.tensor_tensor(
                            onehot[:, :, :, :],
                            expert_id[:, :].unsqueeze(1).unsqueeze(1).to_broadcast([P, 2, TOPK, E]),
                            idxf[:, :, :].unsqueeze(3).to_broadcast([P, 2, TOPK, E]), ALU.is_equal))
                        settle(blk)
                        done(nc.vector.tensor_tensor(chosen[:, :, :], onehot[:, :, 0, :], onehot[:, :, 1, :], ALU.add))
                        settle(blk)
                        nc.vector.tensor_tensor(before[:, 1, :], before[:, 0, :], chosen[:, 0, :], ALU.add)\
                          .then_inc(chosen_ready, 1)

                    def place(blk):
                        dve.wait_ge(chosen_ready, blk + 1)
                        dve.wait_ge(c_ready, blk + 1)
                        nc.vector.tensor_tensor(
                            prod[:, :, :, :], onehot[:, :, :, :],
                            C_BANK[:, 0:2 * E].rearrange("p (a e) -> p a e", a=2).unsqueeze(2).to_broadcast([P, 2, TOPK, E]),
                            ALU.mult).then_inc(c_read, 1)
                        done(nc.vector.tensor_tensor(before[:, 0, :], before[:, 1, :], chosen[:, 1, :], ALU.add))
                        dve.wait_ge(e1_ready, blk + 1)
                        done(nc.vector.tensor_scalar(zsum[:, :, :], e1[:, :, :], 1.0, 1e-12, ALU.add, ALU.add))
                        settle(blk)
                        dve.wait_ge(c_read, blk + 1)
                        done(nc.vector.tensor_reduce(pos[:, :, :], prod[:, :, :, :], AX.X, ALU.add))
                        done(nc.vector.reciprocal(zinv[:, :, :], zsum[:, :, :]))
                        settle(blk)
                        done(nc.vector.tensor_scalar(over[:, :, :], pos[:, :, :], float(CAP), float(E * CAP),
                                                     ALU.is_ge, ALU.mult))
                        done(nc.vector.scalar_tensor_tensor(out=slotf[:, :, :], in0=idxf[:, :, :], scalar=float(CAP),
                                                            in1=pos[:, :, :], op0=ALU.mult, op1=ALU.add))
                        nc.vector.tensor_scalar(row[:, :, C_W0], zinv[:, :, 0], gates[:, 1:2], None, ALU.mult)
                        nc.vector.scalar_tensor_tensor(out=row[:, :, C_W1], in0=e1[:, :, 0], scalar=gates[:, 1:2],
                                                       in1=zinv[:, :, 0], op0=ALU.mult, op1=ALU.mult)
                        nc.vector.tensor_copy(row[:, :, C_TOK], tok_count[:, :])
                        nc.vector.tensor_copy(row[:, :, C_IDX], idxf[:, :, 0])
                        settle(blk)
                        nc.vector.tensor_tensor(slot[:, :, :], slotf[:, :, :], over[:, :, :], ALU.add)\
                          .then_inc(slot_ready, 1)
                        done(nc.vector.tensor_scalar(tok_count[:, :], tok_count[:, :], float(-TB), None, ALU.add))

                    def step(n, b_s, b_v):
                        state["k"] = 0
                        for slot_no in range(2 * KD):
                            if has(n, 0):
                                maxima(n, slot_no)
                            if slot_no == 0:
                                if has(n, -2):
                                    x1(n - 2, 1)
                                if has(n, -1):
                                    pT_rest(n - 1, 2)
                                    recips(n - 1, 3)
                                if has(n, -2):
                                    stats_x1(n - 2)
                            if slot_no == 1 and has(n, -1):
                                a_rest(n - 1, 0)
                            if slot_no == 2:
                                if has(n, 0):
                                    recips(n, 0)
                                    q_rest(n, 1)
                                if has(n, -1):
                                    pT_rest(n - 1, 3)
                            if slot_no == 3:
                                if has(n, 1):
                                    x_rest(n + 1)
                                if has(n, -2):
                                    rows(n - 2)
                            if slot_no == 4:
                                if has(n, -1):
                                    a_rest(n - 1, 1)
                                if has(n, 0):
                                    recips(n, 1)
                                    pT_rest(n, 0)
                            if slot_no == 5:
                                if has(n, 2):
                                    stats_x(n + 2)
                                if has(n, -2):
                                    route(n - 2)
                            if slot_no == 6:
                                if has(n, 0):
                                    recips(n, 2)
                                if has(n, 1):
                                    q_rest(n + 1, 0)
                                if has(n, 0):
                                    pT_rest(n, 1)
                            if slot_no == 7:
                                if has(n, -1):
                                    x1(n - 1, 0)
                                if has(n, -2):
                                    place(n - 2)
                        assert state["k"] in (0, ROWS), state["k"]

                    steps(dve, step)
                    dve.wait_ge(rows_done, ROWS * NB)
                    nc.vector.tensor_copy(chosen[:, 0, :], before[:, 0, :]).then_inc(sums_ready, 1)
                    dve.wait_ge(counts_ready, 1)
                    nc.vector.tensor_copy(counts[:, :], bank[0][0:1, 0:E])

                @block.tensor
                def _(pe):
                    def passes(out_ap, pairs):
                        n, at = 3 * len(pairs), 0
                        for (s_hi, s_lo), (m_hi, m_lo) in pairs:
                            for st, mv in ((s_hi, m_hi), (s_hi, m_lo), (s_lo, m_hi)):
                                last = nc.tensor.matmul(out_ap, st, mv, start=(at == 0), stop=(at == n - 1))
                                at += 1
                        return last

                    pe.wait_ge(prep_loaded, 16 * N_PREP)
                    pe.wait_ge(consts_ready, 2)
                    for b in range(B):
                        for k in range(KI):
                            nc.tensor.transpose(bank[b][:, k * P:(k + 1) * P], row[:, b, k * P:(k + 1) * P], ident[:, :])
                    for k in range(KD):
                        a, c = divmod(k, KD // 2)
                        last = nc.tensor.transpose(bank[2][:, k * E:(k + 1) * E],
                                                   row[0:E, a, DI + c * P:DI + (c + 1) * P], ident[0:E, 0:E])
                    last.then_inc(prep_pe, 1)
                    pe.wait_ge(prep_dve, 1)
                    ctxT = xnT
                    for b in range(B):
                        for m in range(KD):
                            for k in range(KI):
                                nc.tensor.matmul(bank[4 + b][:, m * LKV:(m + 1) * LKV], xin[:, k, m * P:(m + 1) * P],
                                                 ctxT[:, b, k, :], start=(k == 0), stop=(k == KI - 1))
                        for k in range(KI):
                            nc.tensor.matmul(bank[6 + b][:, :], ctxT[:, b, k, :], xres[:, k, :], start=(k == 0), stop=False)
                        last = nc.tensor.matmul(bank[6 + b][:, :], ones[0:1, :], bv_row[:, :], start=False, stop=True)
                    last.then_inc(prep_pe, 1)
                    pe.wait_ge(prep_dve, 3)

                    def transposes_x(blk):
                        pe.wait_ge(xn_ready, 2 * blk + 2)
                        for i in range(2):
                            for kk in range(2):
                                for a in range(2):
                                    last = nc.tensor.transpose(X_BANK[i][:, kk * TB + a * P:kk * TB + (a + 1) * P],
                                                               xin[:, a, (2 * i + kk) * P:(2 * i + kk + 1) * P], ident[:, :])
                            last.then_inc(x_ready, 1)

                    def queries(blk, i):
                        pe.wait_ge(x_lo, 2 * blk + 2)
                        for m in (2 * i, 2 * i + 1):
                            last = passes(Q_BANK[i][:, (m % 2) * TB:(m % 2 + 1) * TB],
                                          [((wq_hi[:, k, m * P:(m + 1) * P], wq_lo[:, k, m * P:(m + 1) * P]),
                                            (xT_hi[:, k, :], xT_lo[:, k, :])) for k in range(KD)])
                        last.then_inc(q_ready, 1)

                    def scores(n, idx, b):
                        g, t = divmod(idx, 2)
                        pe.wait_ge(q_lo, KD * n + g + 1)
                        if not isinstance(n, int) or 2 * KD * n + idx >= 2:
                            pe.wait_ge(exp_done, 2 * KD * n + idx - 1)
                        passes(S_BANK[t][:, :], [((qT_hi[:, g, t * P:(t + 1) * P], qT_lo[:, g, t * P:(t + 1) * P]),
                                                  (k_hi[b][:, g, :], k_lo[b][:, g, :]))]).then_inc(s_ready, 1)

                    def probs_T(blk, g):
                        pe.wait_ge(pn_ready, KD * blk + g + 1)
                        for t in range(2):
                            at = 2 * KD * blk + 2 * g + t
                            if not isinstance(at, int) or at >= 2:
                                pe.wait_ge(pt_lo, at - 1)
                            for hh in range(HG):
                                last = nc.tensor.transpose(PT_BANK[t][:, hh * P:(hh + 1) * P],
                                                           probs[:, t, HG * g + hh, :], ident[:, :])
                            last.then_inc(pt_ready, 1)

                    def heads(blk, i, b):
                        pe.wait_ge(pt_lo, 2 * KD * blk + 4 * i + 4)
                        for gg in range(2):
                            g = 2 * i + gg
                            last = passes(V_BANK[i][:, gg * TB:(gg + 1) * TB],
                                          [((v_hi[b][:, h, :], v_lo[b][:, h, :]), (pT_hi[:, h, :], pT_lo[:, h, :]))
                                           for h in range(HG * g, HG * (g + 1))])
                        last.then_inc(v_ready, 1)

                    def attention_out(blk, a):
                        pe.wait_ge(a_lo, 2 * blk + 2)
                        passes(O_BANK[a][:, :],
                               [((aT_hi[:, k, a * P:(a + 1) * P], aT_lo[:, k, a * P:(a + 1) * P]),
                                 (wo_hi[:, k, :], wo_lo[:, k, :])) for k in range(KD)]).then_inc(o_ready, 1)

                    transposes_x(0)
                    queries(0, 0)

                    def step(n, b_s, b_v):
                        for slot_no in range(2 * KD):
                            if has(n, 0):
                                scores(n, slot_no, b_s)
                            if slot_no == 0 and has(n, -1):
                                probs_T(n - 1, 2)
                                heads(n - 1, 0, b_v)
                            if slot_no == 1 and has(n, 0):
                                if has(n, -3):
                                    pe.wait_ge(c_read, n - 2)
                                queries(n, 1)
                            if slot_no == 2:
                                if has(n, -1):
                                    probs_T(n - 1, 3)
                                if has(n, 1):
                                    if has(n, -2):
                                        pe.wait_ge(x1_ready, 2 * (n - 2) + 2)
                                    transposes_x(n + 1)
                            if slot_no == 3:
                                if has(n, -1):
                                    pe.wait_ge(a_lo, 2 * (n - 1) + 1)
                                    heads(n - 1, 1, b_v)
                            if slot_no == 4:
                                if has(n, 0):
                                    probs_T(n, 0)
                                if has(n, -2):
                                    if has(n, 1):
                                        pe.wait_ge(x_lo, 2 * (n + 1) + 1)
                                    else:
                                        pe.wait_ge(x1_ready, 2 * (n - 2) + 1)
                                    if has(n, 0):
                                        pe.wait_ge(q_lo, KD * n + 4)
                                    else:
                                        pe.wait_ge(c_read, n - 2)
                                    for a in range(2):
                                        pe.wait_ge(row_ready, 2 * (n - 2) + a + 1)
                                        for k in range(KD):
                                            last = nc.tensor.transpose(N_BANK[a][:, k * P:(k + 1) * P],
                                                                       row[:, a, k * P:(k + 1) * P], ident[:, :])
                                        last.then_inc(n_ready, 1)
                            if slot_no == 5:
                                if has(n, -2):
                                    pe.wait_ge(xnT_ready, 2 * (n - 2) + 2)
                                    for a in range(2):
                                        for k in range(KD):
                                            last = nc.tensor.matmul(L_BANK[:, a * E:(a + 1) * E], xnT[:, a, k, :], rwT[:, k, :],
                                                                    start=(k == 0), stop=(k == KD - 1))
                                    last.then_inc(l_ready, 1)
                                if has(n, 1):
                                    queries(n + 1, 0)
                            if slot_no == 6:
                                if has(n, 0):
                                    probs_T(n, 1)
                                if has(n, -1):
                                    if isinstance(n, int) and n == 1:
                                        pe.wait_ge(prep_dve, 4)
                                    attention_out(n - 1, 0)
                            if slot_no == 7:
                                if has(n, -2):
                                    pe.wait_ge(chosen_ready, n - 1)
                                    for a in range(2):
                                        nc.tensor.matmul(C_BANK[:, a * E:(a + 1) * E], upper[:, :], chosen[:, a, :],
                                                         start=True, stop=False)
                                        last = nc.tensor.matmul(C_BANK[:, a * E:(a + 1) * E], ones[:, :], before[:, a, :],
                                                                start=False, stop=True)
                                    last.then_inc(c_ready, 1)
                                if has(n, -1):
                                    if has(n, 1):
                                        pe.wait_ge(q_lo, KD * (n + 1) + 2)
                                    else:
                                        pe.wait_ge(x1_ready, 2 * (n - 2) + 2)
                                    attention_out(n - 1, 1)

                    steps(pe, step)
                    pe.wait_ge(sums_ready, 1)
                    nc.tensor.matmul(bank[0][:, 0:E], ones[:, :], chosen[:, 0, :], start=True, stop=True).then_inc(counts_ready, 1)

        with ExitStack() as stage:
            def sb(name, shape, dt=fp32):
                return stage.enter_context(nc.sbuf_tensor(name, shape, dt))

            raw12 = [sb(f"raw12_{i}", [P, NU12, D]) for i in range(2)]
            raw3 = [sb(f"raw3_{i}", [P, KD, FC]) for i in range(2)]
            w12_hi, w12_lo = ([sb(f"w12_{h}{i}", [P, KD, NU12, P], f32r) for i in range(2)] for h in ("hi", "lo"))
            w3_hi, w3_lo = ([sb(f"w3_{h}{i}", [P, NU3, D], f32r) for i in range(2)] for h in ("hi", "lo"))
            xrow = sb("xrow", [P, NT, ROW])
            xT_hi, xT_lo = (sb(f"slotsT_{h}", [P, KD, CAP], f32r) for h in ("hi", "lo"))
            silu = [sb(f"silu{i}", [P, SB]) for i in range(2)]
            h32 = [sb(f"h32_{i}", [P, SB]) for i in range(2)]
            h_hi, h_lo = ([sb(f"h_{h}{i}", [P, NU3, SB], f32r) for i in range(3)] for h in ("hi", "lo"))
            yacc = sb("yacc", [P, NT, D])
            yout = sb("yout", [P, NT, D])
            first_is_e = sb("first_is_e", [P, NT])
            wdiff = sb("wdiff", [P, NT])
            wslot = sb("wslot", [P, NT])
            token = sb("token", [P, NT], i32)
            e_now = sb("e_now", [P, 1])

            raw12_loaded, raw3_loaded = ([sem(f"{n}_loaded{i}") for i in range(2)] for n in ("raw12", "raw3"))
            xrow_loaded = sem("xrow_loaded")
            tp_ready, hi_done, lo_done = sem("tp_ready"), sem("hi_done"), sem("lo_done")
            g_ready, u_ready = sem("g_ready"), sem("u_ready")
            silu_ready, h32_ready = sem("silu_ready"), sem("h32_ready")
            hhi_ready, hlo_ready = sem("hhi_ready"), sem("hlo_ready")
            y_ready, y_added = sem("y_ready"), sem("y_added")
            yout_ready, yout_free = sem("yout_ready"), sem("yout_free")
            weights_ready, added, idx_done = sem("weights_ready"), sem("added"), sem("idx_done")

            GB, UB, YB, TBK = bank[0:2], bank[2:4], bank[4:6], bank[6:8]
            STEPS = NSB * NU3
            BT = SB // P
            UNITS = NU * NCH + NT
            hbuf = lambda s: 0 if s == 0 else 1 + s % 2

            def blocks(eng, n_e, g1, g2, skip, end):
                g1(0)

                def level(s):
                    def tail():
                        if s < NSB:
                            skip(s, NSB - s)
                        g2(0, max(0, s - 2))
                        if s > 1:
                            g2(s - 1, s - 1)
                        if s < NSB:
                            end(s, NSB - s)

                    if s == NSB:
                        tail()
                        return
                    with eng.If(n_e > s * SB):
                        g1(s)
                        if s >= 2:
                            g2(s - 1, s - 2)
                        level(s + 1)
                    with eng.Else():
                        tail()

                level(1)

            def experts(eng, chunk):
                with eng.Fori(0, E) as e:
                    n_e = eng.value_load(counts[0:1, bass.ds(e, 1)], min_val=0, max_val=T)
                    chunk(e, 0, 0, 0, n_e, True, False)
                    with eng.Fori(0, NCH // 2 - 1) as pair:
                        for i in (1, 2):
                            chunk(e, pair * 2 + i, i % 2, pair + 1, n_e, False, False)
                    chunk(e, NCH - 1, (NCH - 1) % 2, NCH // 2, n_e, False, True)

            steps_before = lambda e, c: e * (NCH * STEPS) + c * STEPS
            tiles_before = lambda e, c: e * (NCH * NT) + c * NT
            units_ahead = NU + BT

            def units_before(e, c, first):
                return e * UNITS + units_ahead if first else e * UNITS + c * NU + (units_ahead + NT - BT)

            def slots_at(t):
                return NU12 + (t if t < BT else t - BT)

            def w3_at(u, first, last):
                return u + (NT - BT if first else BT if last else 0)

            def units_of(s, j, first, last):
                units = []
                if s == 0:
                    units += [("U", u, u) for u in (2 * j, 2 * j + 1)]
                    if j == NU3 - 1 and (first or last):
                        units += [("X", t, slots_at(t)) for t in (range(BT, 2 * BT) if first else range(BT))]
                elif first and s < NSB - 1:
                    t = BT * (s + 1) + j
                    units.append(("X", t, slots_at(t)))
                return units

            ahead = [("U", u) for u in range(NU12)] + [("X", t) for t in range(BT)] + [("U", u) for u in range(NU12, NU)]

            with nc.Block() as block:

                @block.sync
                def _(sp):
                    def load_weights(e, c, par):
                        src12 = w12.rearrange("e (h c r p) d -> h e c p r d", h=2, c=NCH, p=P)
                        for half in range(2):
                            sp.dma_start(raw12[par][:, half * NU3:(half + 1) * NU3, :],
                                         src12[half, bass.ds(e, 1), c, :, :, :].rearrange("e p r d -> (e p) r d"))\
                              .then_inc(raw12_loaded[par], 16)
                        src3 = w3.rearrange("e (k p) (c f) -> e c p k f", p=P, f=FC)[bass.ds(e, 1), c, :, :, :]
                        sp.dma_start(raw3[par][:, :, :], src3.rearrange("e p k f -> (e p) k f"))\
                          .then_inc(raw3_loaded[par], 16)

                    load_weights(0, 0, 0)
                    load_weights(0, 1, 1)
                    with sp.Fori(0, E - 1) as e:
                        for c in range(NCH):
                            sp.wait_ge(lo_done, units_before(e, c, c == 0))
                            load_weights(e + (c + 2) // NCH, (c + 2) % NCH, c % 2)
                    for c in range(NCH - 1):
                        sp.wait_ge(lo_done, units_before(E - 1, c, c == 0))
                        load_weights(E - 1 if c + 2 < NCH else 0, (c + 2) % NCH, c % 2)

                @block.gpsimd
                def _(pool):
                    def load_slots(e):
                        pool.dma_start(xrow[:, :, :], xbuf[bass.ds(e * CAP, CAP), :].rearrange("(t p) c -> p t c", p=P))\
                            .then_inc(xrow_loaded, 16)

                    nc.gpsimd.memset(e_now[:, :], 0.0).then_inc(idx_done, 1)
                    pool.sem_inc(yout_free, 1)
                    load_slots(0)

                    def expert(e, nxt):
                        n_e = pool.value_load(counts[0:1, bass.ds(e, 1)], min_val=0, max_val=T)
                        wait_apart(pool, "pool", xrow_loaded, 16 * (e + 1))
                        wait_apart(pool, "pool", idx_done, 3 * e + 1)
                        nc.gpsimd.tensor_scalar(token[:, :], xrow[:, :, C_TOK], -1.0, float(T), ALU.mult, ALU.add)
                        nc.gpsimd.tensor_scalar(first_is_e[:, :], xrow[:, :, C_IDX], e_now[:, 0:1], None, ALU.is_equal)
                        nc.gpsimd.tensor_tensor(wdiff[:, :], xrow[:, :, C_W0], xrow[:, :, C_W1], ALU.subtract)\
                          .then_inc(idx_done, 1)
                        pool.wait_ge(idx_done, 3 * e + 2)
                        nc.gpsimd.tensor_tensor(wdiff[:, :], wdiff[:, :], first_is_e[:, :], ALU.mult).then_inc(idx_done, 1)
                        pool.wait_ge(idx_done, 3 * e + 3)
                        nc.gpsimd.tensor_tensor(wslot[:, :], wdiff[:, :], xrow[:, :, C_W1], ALU.add).then_inc(weights_ready, 1)
                        nc.gpsimd.tensor_scalar_add(e_now[:, :], e_now[:, :], 1.0).then_inc(idx_done, 1)
                        wait_apart(pool, "pool", lo_done, units_before(e, 0, True) + NU12 + NT - BT)
                        wait_apart(pool, "pool", idx_done, 3 * e + 4)
                        load_slots(nxt)

                        def add_rows(t, rows):
                            nc.gpsimd.indirect_dma_start(
                                out=out_tok, out_offset=bass.IndirectOffsetOnAxis(ap=token[:, t:t + 1], axis=0),
                                in_=yout[:, rows, :], in_offset=None, bounds_check=T - 1, oob_is_err=False,
                                compute_op=ALU.add).then_inc(added, 16)

                        def scatter(s, place):
                            for tt in range(BT):
                                wait_apart(pool, "pool", yout_ready, NT * (e + 1) + BT * place + tt + 1)
                                add_rows(BT * s + tt, BT * s + tt)

                        def end(s, left):
                            pool.sem_inc(yout_ready, BT * left)
                            for t in range(BT * s, NT):
                                add_rows(t, 0)

                        blocks(pool, n_e, lambda s: None, scatter, lambda s, left: None, end)
                        wait_apart(pool, "pool", added, 16 * NT * (e + 1))
                        pool.sem_inc(yout_free, 1)

                    with pool.Fori(0, E - 1) as e:
                        expert(e, e + 1)
                    expert(E - 1, 0)

                @block.scalar
                def _(act):
                    def hi_half(kind, i, par, at):
                        act.wait_ge(tp_ready, at + 1)
                        src = TBK[i % 2][:, :]
                        if kind == "X":
                            dst, src = xT_hi[:, :, i * P:(i + 1) * P], src.rearrange("p (k t) -> p k t", k=KD)
                        elif i < NU12:
                            dst, src = w12_hi[par][:, :, i, :], src.rearrange("p (k f) -> p k f", k=KD)
                        else:
                            dst = w3_hi[par][:, i - NU12, :]
                        nc.scalar.copy(dst, src).then_inc(hi_done, 1)

                    act.sem_inc(yout_ready, NT)
                    for at, (kind, i) in enumerate(ahead):
                        hi_half(kind, i, 0, at)

                    def chunk(e, c, par, half, n_e, first, last):
                        units = units_before(e, c, first)

                        def g1(s):
                            for j in range(NU3):
                                q = s * NU3 + j
                                at = steps_before(e, c) + q
                                act.wait_ge(g_ready, at + 1)
                                nc.scalar.activation(silu[q % 2][:, :], GB[q % 2][:, 0:SB], ACT.Silu).then_inc(silu_ready, 1)
                                act.wait_ge(h32_ready, at + 1)
                                nc.scalar.copy(h_hi[hbuf(s)][:, j, :], h32[q % 2][:, :]).then_inc(hhi_ready, 1)
                                for kind, i, place in units_of(s, j, first, last):
                                    hi_half(kind, i, 1 - par, units + place)

                        def g2(s, place):
                            if last:
                                if place == 0:
                                    act.wait_ge(weights_ready, e + 1)
                                    act.wait_ge(yout_free, e + 1)
                                for tt in range(BT):
                                    t = BT * s + tt
                                    act.wait_ge(y_added, tiles_before(e, c) + BT * place + tt + 3)
                                    nc.scalar.activation(yout[:, t, :], yacc[:, t, :], ACT.Copy,
                                                         scale=wslot[:, t:t + 1]).then_inc(yout_ready, 1)

                        def skip(s, left):
                            act.sem_inc(g_ready, NU3 * left)
                            act.sem_inc(h32_ready, NU3 * left)
                            if first and left > 1:
                                act.sem_inc(tp_ready, BT * (left - 1))

                        blocks(act, n_e, g1, g2, skip, lambda s, left: None)
                        for u in range(NU12, NU):
                            hi_half("U", u, 1 - par, units + w3_at(u, first, last))

                    experts(act, chunk)

                @block.vector
                def _(dve):
                    def lo_half(kind, i, par, at):
                        dve.wait_ge(hi_done, at + 1)
                        src = TBK[i % 2][:, :]
                        if kind == "X":
                            cols = slice(i * P, (i + 1) * P)
                            dst, hi, src = xT_lo[:, :, cols], xT_hi[:, :, cols], src.rearrange("p (k t) -> p k t", k=KD)
                        elif i < NU12:
                            dst, hi, src = w12_lo[par][:, :, i, :], w12_hi[par][:, :, i, :], src.rearrange("p (k f) -> p k f", k=KD)
                        else:
                            dst, hi = w3_lo[par][:, i - NU12, :], w3_hi[par][:, i - NU12, :]
                        nc.vector.tensor_tensor(dst, src, hi.bitcast(fp32), ALU.subtract).then_inc(lo_done, 1)

                    dve.sem_inc(y_added, BT)
                    for at, (kind, i) in enumerate(ahead):
                        lo_half(kind, i, 0, at)

                    def chunk(e, c, par, half, n_e, first, last):
                        units = units_before(e, c, first)

                        def g1(s):
                            for j in range(NU3):
                                q = s * NU3 + j
                                at = steps_before(e, c) + q
                                dve.wait_ge(u_ready, at + 1)
                                dve.wait_ge(silu_ready, at + 1)
                                nc.vector.tensor_tensor(h32[q % 2][:, :], silu[q % 2][:, :], UB[q % 2][:, 0:SB], ALU.mult)\
                                  .then_inc(h32_ready, 1)
                                dve.wait_ge(hhi_ready, at + 1)
                                nc.vector.tensor_tensor(h_lo[hbuf(s)][:, j, :], h32[q % 2][:, :],
                                                        h_hi[hbuf(s)][:, j, :].bitcast(fp32), ALU.subtract).then_inc(hlo_ready, 1)
                                for kind, i, place in units_of(s, j, first, last):
                                    lo_half(kind, i, 1 - par, units + place)

                        def g2(s, place):
                            for tt in range(BT):
                                t = BT * s + tt
                                dve.wait_ge(y_ready, tiles_before(e, c) + BT * place + tt + 1)
                                if first:
                                    dve.wait_ge(yout_ready, NT * (e + 1))
                                    nc.vector.tensor_copy(yacc[:, t, :], YB[tt][:, :]).then_inc(y_added, 1)
                                else:
                                    dve.wait_ge(y_added, tiles_before(e, c) + BT)
                                    nc.vector.tensor_tensor(yacc[:, t, :], YB[tt][:, :], yacc[:, t, :], ALU.add)\
                                      .then_inc(y_added, 1)

                        def skip(s, left):
                            dve.sem_inc(u_ready, NU3 * left)
                            dve.sem_inc(silu_ready, NU3 * left)
                            dve.sem_inc(hhi_ready, NU3 * left)
                            if first and left > 1:
                                dve.sem_inc(hi_done, BT * (left - 1))
                                dve.wait_ge(lo_done, units + NU12 + BT * s)
                                dve.sem_inc(lo_done, BT * (left - 1))

                        def end(s, left):
                            dve.sem_inc(y_ready, BT * left)
                            dve.wait_ge(y_added, tiles_before(e, c) + BT + BT * s)
                            dve.sem_inc(y_added, BT * left)

                        blocks(dve, n_e, g1, g2, skip, end)
                        for u in range(NU12, NU):
                            lo_half("U", u, 1 - par, units + w3_at(u, first, last))

                    experts(dve, chunk)

                @block.tensor
                def _(pe):
                    def passes(out_ap, pairs):
                        n, at = 3 * len(pairs), 0
                        for (s_hi, s_lo), (m_hi, m_lo) in pairs:
                            for st, mv in ((s_hi, m_hi), (s_hi, m_lo), (s_lo, m_hi)):
                                last = nc.tensor.matmul(out_ap, st, mv, start=(at == 0), stop=(at == n - 1))
                                at += 1
                        return last

                    def transpose_unit(kind, i, par, at):
                        if not isinstance(at, int) or at >= 2:
                            pe.wait_ge(lo_done, at - 1)
                        for k in range(KD):
                            if kind == "X":
                                src = xrow[:, i, k * P:(k + 1) * P]
                            elif i < NU12:
                                src = raw12[par][:, i, k * P:(k + 1) * P]
                            else:
                                src = raw3[par][:, k, (i - NU12) * P:(i - NU12 + 1) * P]
                            last = nc.tensor.transpose(TBK[i % 2][:, k * P:(k + 1) * P], src, ident[:, :])
                        last.then_inc(tp_ready, 1)

                    pe.wait_ge(raw12_loaded[0], 32)
                    pe.wait_ge(raw3_loaded[0], 16)
                    pe.wait_ge(xrow_loaded, 16)
                    for at, (kind, i) in enumerate(ahead):
                        transpose_unit(kind, i, 0, at)

                    def chunk(e, c, par, half, n_e, first, last):
                        units = units_before(e, c, first)
                        loads = e * (NCH // 2) + half + 1

                        def g1(s):
                            stat = lambda r: [(w12_hi[par][:, k, r, :], w12_lo[par][:, k, r, :]) for k in range(KD)]
                            slots = slice(s * SB, (s + 1) * SB)
                            moving = [(xT_hi[:, k, slots], xT_lo[:, k, slots]) for k in range(KD)]
                            if s == 0:
                                pe.wait_ge(lo_done, units - NU3)
                            elif first:
                                pe.wait_ge(lo_done, units + slots_at(BT * s + BT - 1) + 1)
                            for j in range(NU3):
                                q = s * NU3 + j
                                at = steps_before(e, c) + q
                                if not first or q >= 2:
                                    pe.wait_ge(silu_ready, at - 1)
                                passes(GB[q % 2][:, 0:SB], list(zip(stat(j), moving))).then_inc(g_ready, 1)
                                if not first or q >= 2:
                                    pe.wait_ge(h32_ready, at - 1)
                                passes(UB[q % 2][:, 0:SB], list(zip(stat(NU3 + j), moving))).then_inc(u_ready, 1)
                                for kind, i, place in units_of(s, j, first, last):
                                    if kind == "U" and i == 0:
                                        pe.wait_ge(raw12_loaded[1 - par], 32 * loads)
                                    if kind == "X" and i == 0:
                                        pe.wait_ge(xrow_loaded, 16 * (e + 2))
                                    transpose_unit(kind, i, 1 - par, units + place)

                        def g2(s, place):
                            pe.wait_ge(hlo_ready, steps_before(e, c) + (s + 1) * NU3)
                            if place == 0:
                                pe.wait_ge(lo_done, units)
                            for tt in range(BT):
                                pe.wait_ge(y_added, tiles_before(e, c) + BT * place + tt + 1)
                                cols = slice(tt * P, (tt + 1) * P)
                                passes(YB[tt][:, :], [((h_hi[hbuf(s)][:, f, cols], h_lo[hbuf(s)][:, f, cols]),
                                                       (w3_hi[par][:, f, :], w3_lo[par][:, f, :]))
                                                      for f in range(NU3)]).then_inc(y_ready, 1)

                        def end(s, left):
                            pe.sem_inc(hlo_ready, NU3 * left)

                        blocks(pe, n_e, g1, g2, lambda s, left: None, end)
                        pe.wait_ge(raw3_loaded[1 - par], 16 * loads)
                        for u in range(NU12, NU):
                            transpose_unit("U", u, 1 - par, units + w3_at(u, first, last))

                    experts(pe, chunk)


_INS = ['x', 'ctx_512', 'g_xattn', 'g_ffn', 'L0_xattn_Wq', 'L0_xattn_bq', 'L0_xattn_Wk', 'L0_xattn_bk', 'L0_xattn_Wv',
        'L0_xattn_bv', 'L0_xattn_Wo', 'L0_xattn_bo', 'L0_ffn_ln_gamma', 'L0_ffn_ln_beta', 'L0_ffn_router_w',
        'L0_ffn_w12', 'L0_ffn_w3']
_OUTS = [((2, 2048, 512), 'float32')]


def kernel(**inputs):
    import numpy as _np
    import concourse.bacc as _bacc
    from concourse import mybir as _mybir
    from concourse.bass_utils import run_bass_kernel_spmd as _run

    nc = _bacc.Bacc("TRN2", target_bir_lowering=False, num_devices=1)
    arrays, args = {}, []
    for name in _INS:
        a = _np.ascontiguousarray(inputs[name])
        arrays[f"in_{name}_dram"] = a
        args.append(nc.dram_tensor(f"in_{name}_dram", a.shape, _mybir.dt.from_np(a.dtype), kind="ExternalInput").ap())
    for i, (shape, dtype) in enumerate(_OUTS):
        dt = _mybir.dt.from_np(_np.dtype(dtype))
        args.append(nc.dram_tensor(f"out_{i}_dram", shape, dt, kind="ExternalOutput").ap())
    flamingo_gated_layer(nc, *args)
    r = _run(nc, [arrays], core_ids=[0])
    return r.results[0]["out_0_dram"]
```

```python
import concourse.bass as bass
from concourse import mybir
from contextlib import ExitStack


def flamingo_gated_layer(
    nc: bass.Bass,
    x: bass.AP,
    ctx_img: bass.AP,
    g_xattn: bass.AP,
    g_ffn: bass.AP,
    Wq: bass.AP,
    bq: bass.AP,
    Wk: bass.AP,
    bk: bass.AP,
    Wv: bass.AP,
    bv: bass.AP,
    Wo: bass.AP,
    bo: bass.AP,
    ln_gamma: bass.AP,
    ln_beta: bass.AP,
    router_w: bass.AP,
    w12: bass.AP,
    w3: bass.AP,
    out: bass.AP,
):
    fp32, f32r = mybir.dt.float32, mybir.dt.float32r
    i32, u32 = mybir.dt.int32, mybir.dt.uint32
    ALU = mybir.AluOpType
    ACT = mybir.ActivationFunctionType
    AX = mybir.AxisListType

    P = 128
    B, S, D = x.shape
    LKV, DI = ctx_img.shape[1], ctx_img.shape[2]
    H = 16
    DK = D // H
    SCALE = float(DK) ** -0.5
    E, F2, _ = w12.shape
    F = F2 // 2
    TOPK = 2
    T = B * S
    CAP = -(-T * TOPK * 5 // (4 * E))
    EPS = 1e-5
    CLAMP = 10000.0

    KD = D // P
    KI = DI // P
    HG = H // KD
    TB = 2 * P
    NB = T // TB
    NBB = NB // B
    NT = CAP // P
    SB = 2 * P
    NSB = CAP // SB
    FC = 2 * P
    NCH = F // FC
    NU12 = 2 * FC // P
    NU3 = FC // P
    NU = NU12 + NU3
    ROW = D + 8
    C_TOK, C_W0, C_W1, C_IDX = D, D + 1, D + 2, D + 3

    x_tok = x.rearrange("b s d -> (b s) d")
    out_tok = out.rearrange("b s d -> (b s) d")
    xbuf = nc.dram_tensor("expert_rows", [E * CAP, ROW], fp32, kind="Internal").ap()

    with ExitStack() as whole:
        def sem(name):
            return whole.enter_context(nc.semaphore(name))

        stepped = {name: sem(f"stepped_{name}") for name in ("pool", "dve", "sp")}

        def wait_apart(eng, name, semaphore, value):
            eng.wait_ge(semaphore, value)
            eng.sem_inc(stepped[name], 1)

        ident = whole.enter_context(nc.sbuf_tensor("ident", [P, P], fp32))
        counts = whole.enter_context(nc.sbuf_tensor("counts", [1, E], i32))
        bank = [whole.enter_context(nc.psum_tensor(f"bank{i}", [P, 512], fp32)) for i in range(8)]

        with ExitStack() as stage:
            def sb(name, shape, dt=fp32):
                return stage.enter_context(nc.sbuf_tensor(name, shape, dt))

            upper = sb("upper", [P, P])
            ones = sb("ones", [P, P])
            zeros = sb("zeros", [P, 2 * ROW])
            expert_id = sb("expert_id", [P, E])
            neg_half = sb("neg_half", [P, 2])
            tok_count = sb("tok_count", [P, 2])
            gates = sb("gates", [P, 2])
            bqT = sb("bqT", [P, KD])
            bkT = sb("bkT", [P, KD])
            bv_row = sb("bv_row", [1, D])
            gamma_b = sb("gamma_b", [P, D])
            beta_b = sb("beta_b", [P, D])
            gbo_b = sb("gbo_b", [P, D])
            rwT = sb("rwT", [P, KD, E])
            wq_hi, wq_lo = (sb(f"wq_{h}", [P, KD, D], f32r) for h in ("hi", "lo"))
            wo_hi, wo_lo = (sb(f"wo_{h}", [P, KD, D], f32r) for h in ("hi", "lo"))
            k_hi, k_lo = ([sb(f"k_{h}{b}", [P, KD, HG * LKV], f32r) for b in range(B)] for h in ("hi", "lo"))
            v_hi, v_lo = ([sb(f"v_{h}{b}", [P, H, P], f32r) for b in range(B)] for h in ("hi", "lo"))
            xin = sb("xin", [P, 2, D])
            xT_hi, xT_lo = (sb(f"xT_{h}", [P, KD, TB], f32r) for h in ("hi", "lo"))
            qT_hi, qT_lo = (sb(f"qT_{h}", [P, KD, TB], f32r) for h in ("hi", "lo"))
            probs = sb("probs", [P, 2, H, LKV])
            pT_hi, pT_lo = (sb(f"pT_{h}", [P, H, TB], f32r) for h in ("hi", "lo"))
            aT_hi, aT_lo = (sb(f"aT_{h}", [P, KD, TB], f32r) for h in ("hi", "lo"))
            xres = sb("xres", [P, 2, D])
            row = sb("row", [P, 2, ROW])
            xnT = sb("xnT", [P, 2, KD, P])
            neg_max = sb("neg_max", [P, 2, H])
            sums = sb("sums", [P, 2, H])
            rsums = sb("rsums", [P, 2, H])
            bn1, bn2 = (sb(f"bn{i}", [P, 2, 6]) for i in (1, 2))
            mv1, mv2 = (sb(f"mv{i}", [P, 2, 2]) for i in (1, 2))
            var1, var2 = (sb(f"var{i}", [P, 2]) for i in (1, 2))
            rstd1, rstd2 = (sb(f"rstd{i}", [P, 2]) for i in (1, 2))
            shift1 = sb("shift1", [P, 2])
            logits = sb("logits", [P, 2, E])
            top8 = sb("top8", [P, 2, 8])
            topi = sb("topi", [P, 2, 8], u32)
            idxf = sb("idxf", [P, 2, TOPK])
            gap = sb("gap", [P, 2, 1])
            e1 = sb("e1", [P, 2, 1])
            zsum = sb("zsum", [P, 2, 1])
            zinv = sb("zinv", [P, 2, 1])
            onehot = sb("onehot", [P, 2, TOPK, E])
            chosen = sb("chosen", [P, 2, E])
            before = sb("before", [P, 2, E])
            prod = sb("prod", [P, 2, TOPK, E])
            pos = sb("pos", [P, 2, TOPK])
            over = sb("over", [P, 2, TOPK])
            slotf = sb("slotf", [P, 2, TOPK])
            slot = sb("slot", [P, 2, TOPK], i32)

            kv_loaded, wq_loaded, wo_loaded, late_loaded = (
                sem(n) for n in ("kv_loaded", "wq_loaded", "wo_loaded", "late_loaded"))
            consts_ready, prep_pe, prep_act, prep_dve, prep_pool = (
                sem(n) for n in ("consts_ready", "prep_pe", "prep_act", "prep_dve", "prep_pool"))
            zero_filled = sem("zero_filled")
            cleared, prep_split = sem("cleared"), sem("prep_split")
            xin_loaded, xres_loaded, x1_stored = sem("xin_loaded"), sem("xres_loaded"), sem("x1_stored")
            stats1_done, stats1_ready, var1_ready, rstd1_ready, xn_ready = (
                sem(n) for n in ("stats1_done", "stats1_ready", "var1_ready", "rstd1_ready", "xn_ready"))
            shift1_mean, shift1_ready = sem("shift1_mean"), sem("shift1_ready")
            x_ready, x_hi, x_lo = sem("x_ready"), sem("x_hi"), sem("x_lo")
            q_ready, q_hi, q_lo = sem("q_ready"), sem("q_hi"), sem("q_lo")
            s_ready, max_ready, exp_done = sem("s_ready"), sem("max_ready"), sem("exp_done")
            rs_ready, pn_ready = sem("rs_ready"), sem("pn_ready")
            pt_ready, pt_hi, pt_lo = sem("pt_ready"), sem("pt_hi"), sem("pt_lo")
            v_ready, a_hi, a_lo = sem("v_ready"), sem("a_hi"), sem("a_lo")
            xb_ready, o_ready, x1_ready = sem("xb_ready"), sem("o_ready"), sem("x1_ready")
            stats2_ready, var2_ready, rstd2_ready, row_ready = (
                sem(n) for n in ("stats2_ready", "var2_ready", "rstd2_ready", "row_ready"))
            n_ready, xnT_ready = sem("n_ready"), sem("xnT_ready")
            l_ready, logits_ready, gap_ready, e1_ready = (
                sem(n) for n in ("l_ready", "logits_ready", "gap_ready", "e1_ready"))
            chosen_ready, c_ready, c_read, slot_ready, scattered = (
                sem(n) for n in ("chosen_ready", "c_ready", "c_read", "slot_ready", "scattered"))
            sums_ready, counts_ready = sem("sums_ready"), sem("counts_ready")
            rows_done = sem("rows_done")

            whole_rows = lambda ap, k: ap.rearrange("p (k a) n -> p k (a n)", k=k)
            DH = D // LKV
            N_KV = 10
            wq_raw, wo_raw = (whole_rows(probs[:, i, :, :], KD) for i in range(2))
            wk_raw, wv_raw = (whole_rows(probs[:, 1, i * KI * DH:(i + 1) * KI * DH, :], KI) for i in range(2))
            S_BANK, PT_BANK = bank[0:2], bank[2:4]
            X_BANK = bank[6:8]
            Q_BANK = [bank[7], bank[5]]
            V_BANK = [bank[4], bank[4]]
            O_BANK = bank[6:8]
            N_BANK = [bank[6], bank[5]]
            L_BANK = C_BANK = bank[5]

            def steps(eng, step):
                for n in range(3):
                    step(n, 0, 0)
                with eng.Fori(3, NBB) as n:
                    step(n, 0, 0)
                step(NBB, 1, 0)
                with eng.Fori(NBB + 1, NB - 2) as n:
                    step(n, 1, 1)
                for n in range(NB - 2, NB + 2):
                    step(n, 1, 1)

            def has(n, ahead):
                return not isinstance(n, int) or 0 <= n + ahead < NB

            with nc.Block() as block:

                @block.sync
                def _(sp):
                    def load_xin(blk):
                        sp.dma_start(xin[:, :, :], x_tok[bass.ds(blk * TB, TB), :].rearrange("(a p) d -> p a d", p=P))\
                          .then_inc(xin_loaded, 16)

                    def load_xres(blk):
                        sp.dma_start(xres[:, :, :], x_tok[bass.ds(blk * TB, TB), :].rearrange("(a p) d -> p a d", p=P))\
                          .then_inc(xres_loaded, 16)

                    wide = lambda w: w.rearrange("(k p) n -> p k n", p=P)
                    kv_parts = [
                        (row[:, :, 0:DI], ctx_img.rearrange("b s d -> s b d")),
                        (row[0:E, 0, DI:DI + D // 2], router_w[:, 0:D // 2]),
                        (row[0:E, 1, DI:DI + D // 2], router_w[:, D // 2:D]),
                        (wk_raw, wide(Wk)),
                        (bkT[:, :], bk.rearrange("(m p) -> p m", p=P)),
                        (bqT[:, :], bq.rearrange("(m p) -> p m", p=P)),
                        (bv_row[:, :], bv.rearrange("(a n) -> a n", a=1)),
                        (gates[:, 0:1], g_xattn.partition_broadcast(P)),
                        (gates[:, 1:2], g_ffn.partition_broadcast(P)),
                        (wv_raw, wide(Wv)),
                    ]
                    assert len(kv_parts) == N_KV
                    for dst, src in kv_parts:
                        sp.dma_start(dst, src, allow_slow_non_contiguous=True).then_inc(kv_loaded, 16)
                    load_xin(0)
                    sp.dma_start(wq_raw, wide(Wq)).then_inc(wq_loaded, 16)
                    load_xres(0)
                    for dst, src in ((gbo_b, bo), (gamma_b, ln_gamma), (beta_b, ln_beta)):
                        sp.dma_start(dst[:, :], src.partition_broadcast(P)).then_inc(late_loaded, 16)
                    sp.wait_ge(x_ready, 2)
                    load_xin(1)
                    sp.wait_ge(prep_pe, 3)
                    sp.dma_start(wo_raw, wide(Wo)).then_inc(wo_loaded, 16)
                    sp.wait_ge(consts_ready, 1)
                    flat = xbuf.rearrange("(p r) n -> p (r n)", p=P)
                    FILLS = E * CAP // P // 2

                    def fill(part, parts=(0, 10, 22, 34, FILLS)):
                        for i in range(parts[part], parts[part + 1]):
                            sp.dma_start(flat[:, i * 2 * ROW:(i + 1) * 2 * ROW], zeros[:, :]).then_inc(zero_filled, 16)

                    fill(0)

                    def step(n, b_s, b_v):
                        if has(n, 2):
                            sp.wait_ge(x_ready, 2 * (n + 1) + 2)
                            load_xin(n + 2)
                        if isinstance(n, int) and n < 3:
                            fill(n + 1)
                        if has(n, -2) and has(n, -1):
                            wait_apart(sp, "sp", x1_stored, 16 * (n - 1))
                            sp.wait_ge(row_ready, 2 * (n - 2) + 2)
                            load_xres(n - 1)
                        if has(n, -1):
                            sp.wait_ge(x1_ready, 2 * (n - 1) + 2)
                            sp.dma_start(out_tok[bass.ds((n - 1) * TB, TB), :].rearrange("(a p) d -> p a d", p=P),
                                         xres[:, :, :]).then_inc(x1_stored, 16)

                    steps(sp, step)
                    sp.wait_ge(x1_stored, 16 * NB)

                @block.gpsimd
                def _(pool):
                    nc.gpsimd.memset(zeros[:, :], 0.0).then_inc(consts_ready, 1)
                    nc.gpsimd.memset(ident[:, :], 0.0)
                    nc.gpsimd.memset(upper[:, :], 0.0)
                    nc.gpsimd.memset(ones[:, :], 1.0)
                    nc.gpsimd.memset(neg_half[:, :], -0.5)
                    nc.gpsimd.memset(before[:, 0, :], 0.0).then_inc(cleared, 1)
                    pool.wait_ge(cleared, 1)
                    nc.gpsimd.affine_select(out=ident[:, :], in_=ident[:, :], compare_op=ALU.not_equal, fill=1.0,
                                            base=0, pattern=[[-1, P]], channel_multiplier=1)
                    nc.gpsimd.affine_select(out=upper[:, :], in_=upper[:, :], compare_op=ALU.is_ge, fill=1.0,
                                            base=0, pattern=[[-1, P]], channel_multiplier=1)
                    nc.gpsimd.iota(expert_id[:, :], pattern=[[1, E]], base=0, channel_multiplier=0,
                                   allow_small_or_imprecise_dtypes=True)
                    nc.gpsimd.iota(tok_count[:, :], pattern=[[-P, 2]], base=T, channel_multiplier=-1,
                                   allow_small_or_imprecise_dtypes=True).then_inc(consts_ready, 1)
                    def rstd_x(blk):
                        wait_apart(pool, "pool", stats1_ready, blk + 1)
                        nc.gpsimd.tensor_scalar_add(var1[:, :], mv1[:, :, 1], EPS).then_inc(var1_ready, 1)
                        pool.wait_ge(var1_ready, blk + 1)
                        nc.gpsimd.tensor_tensor(rstd1[:, :], var1[:, :], neg_half[:, :], ALU.pow)\
                          .then_inc(rstd1_ready, 1)
                        pool.wait_ge(rstd1_ready, blk + 1)
                        nc.gpsimd.tensor_tensor(shift1[:, :], mv1[:, :, 0], rstd1[:, :], ALU.mult).then_inc(shift1_mean, 1)
                        wait_apart(pool, "pool", shift1_mean, blk + 1)
                        nc.gpsimd.tensor_scalar(shift1[:, :], shift1[:, :], -1.0, None, ALU.mult).then_inc(shift1_ready, 1)

                    for parts in (k_hi + k_lo, v_hi + v_lo):
                        for t in parts:
                            last = nc.gpsimd.memset(t[:, :, :].bitcast(fp32), 0.0)
                        last.then_inc(prep_pool, 1)
                        if parts[0] is k_hi[0]:
                            rstd_x(0)

                    def norm(blk, g):
                        heads = slice(HG * g, HG * (g + 1))
                        pool.wait_ge(rs_ready, KD * blk + g + 1)
                        nc.gpsimd.tensor_tensor(probs[:, :, heads, :], probs[:, :, heads, :],
                                                rsums[:, :, heads].unsqueeze(3).to_broadcast([P, 2, HG, LKV]),
                                                ALU.mult).then_inc(pn_ready, 1)

                    def rstd_x1(blk):
                        wait_apart(pool, "pool", stats2_ready, blk + 1)
                        nc.gpsimd.tensor_scalar(var2[:, :], mv2[:, :, 1], 1.0 + EPS, EPS * EPS,
                                                ALU.mult, ALU.add).then_inc(var2_ready, 1)
                        pool.wait_ge(var2_ready, blk + 1)
                        nc.gpsimd.tensor_tensor(rstd2[:, :], var2[:, :], neg_half[:, :], ALU.pow)\
                          .then_inc(rstd2_ready, 1)

                    def add_bias(blk):
                        if isinstance(blk, int) and blk == 0:
                            pool.wait_ge(prep_dve, 5)
                        pool.wait_ge(xres_loaded, 16 * blk + 16)
                        nc.gpsimd.tensor_tensor(xres[:, :, :], xres[:, :, :],
                                                gbo_b[:, :].unsqueeze(1).to_broadcast([P, 2, D]),
                                                ALU.add).then_inc(xb_ready, 1)

                    def scatter(blk):
                        wait_apart(pool, "pool", slot_ready, blk + 1)
                        if isinstance(blk, int) and blk == 0:
                            pool.wait_ge(zero_filled, 16 * (E * CAP // P // 2))
                        for a in range(2):
                            for k in range(TOPK):
                                nc.gpsimd.indirect_dma_start(
                                    out=xbuf[:, :],
                                    out_offset=bass.IndirectOffsetOnAxis(ap=slot[:, a, k:k + 1], axis=0),
                                    in_=row[:, a, :], in_offset=None,
                                    bounds_check=E * CAP - 1, oob_is_err=False).then_inc(scattered, 16)

                    pool.wait_ge(xn_ready, 2)
                    rstd_x(1)

                    def step(n, b_s, b_v):
                        if has(n, -1):
                            norm(n - 1, 3)
                        if has(n, -2):
                            rstd_x1(n - 2)
                        if has(n, 0):
                            norm(n, 0)
                            norm(n, 1)
                        if has(n, -1):
                            add_bias(n - 1)
                        if has(n, 2):
                            rstd_x(n + 2)
                        if has(n, 0):
                            norm(n, 2)
                        if has(n, -2):
                            scatter(n - 2)

                    steps(pool, step)
                    pool.wait_ge(scattered, 64 * NB)

                @block.scalar
                def _(act):
                    act.wait_ge(kv_loaded, 16 * N_KV)
                    nc.scalar.activation(gates[:, :], gates[:, :], ACT.Tanh).then_inc(prep_act, 1)
                    nc.scalar.mul(bkT[:, :], bkT[:, :], SCALE).then_inc(prep_act, 1)

                    def x_halves(blk):
                        for i in range(2):
                            act.wait_ge(x_ready, 2 * blk + i + 1)
                            nc.scalar.copy(xT_hi[:, 2 * i:2 * i + 2, :],
                                           X_BANK[i][:, :].rearrange("p (k t) -> p k t", k=2)).then_inc(x_hi, 1)

                    def q_halves(blk, i):
                        act.wait_ge(q_ready, 2 * blk + i + 1)
                        for m in (2 * i, 2 * i + 1):
                            nc.scalar.activation(qT_hi[:, m, :], Q_BANK[i][:, (m % 2) * TB:(m % 2 + 1) * TB],
                                                 ACT.Identity, bias=bqT[:, m:m + 1]).then_inc(q_hi, 1)

                    def exps(blk, idx):
                        g, t = divmod(idx, 2)
                        act.wait_ge(max_ready, 2 * KD * blk + idx + 1)
                        if not isinstance(blk, int) or blk > 0:
                            act.wait_ge(pt_ready, 2 * KD * (blk - 1) + idx + 1)
                        for hh in range(HG):
                            h = HG * g + hh
                            ins = nc.scalar.activation(probs[:, t, h, :], S_BANK[t][:, hh * LKV:(hh + 1) * LKV], ACT.Exp,
                                                       bias=neg_max[:, t, h:h + 1], accum_out=sums[:, t, h:h + 1])
                        ins.then_inc(exp_done, 1)

                    def pT_halves(blk, g):
                        for t in range(2):
                            act.wait_ge(pt_ready, 2 * KD * blk + 2 * g + t + 1)
                            nc.scalar.copy(pT_hi[:, HG * g:HG * (g + 1), t * P:(t + 1) * P],
                                           PT_BANK[t][:, :].rearrange("p (h t) -> p h t", h=HG)).then_inc(pt_hi, 1)

                    def a_halves(blk, i):
                        act.wait_ge(v_ready, 2 * blk + i + 1)
                        nc.scalar.copy(aT_hi[:, 2 * i:2 * i + 2, :],
                                       V_BANK[i][:, :].rearrange("p (k t) -> p k t", k=2)).then_inc(a_hi, 1)

                    def norm_x(blk):
                        act.wait_ge(shift1_ready, blk + 1)
                        for a in range(2):
                            nc.scalar.activation(xin[:, a, :], xin[:, a, :], ACT.Identity, bias=shift1[:, a:a + 1],
                                                 scale=rstd1[:, a:a + 1]).then_inc(xn_ready, 1)

                    norm_x(0)
                    act.wait_ge(wq_loaded, 16)
                    nc.scalar.copy(wq_hi[:, :, :], wq_raw).then_inc(prep_act, 1)
                    x_halves(0)
                    act.wait_ge(prep_act, 2)
                    act.wait_ge(prep_pe, 2)
                    for b in range(B):
                        for m in range(KD):
                            nc.scalar.activation(row[:, b, m * LKV:(m + 1) * LKV], bank[4 + b][:, m * LKV:(m + 1) * LKV],
                                                 ACT.Identity, bias=bkT[:, m:m + 1], scale=SCALE).then_inc(prep_act, 1)
                    q_halves(0, 0)
                    act.wait_ge(prep_dve, 2)

                    def step(n, b_s, b_v):
                        for slot_no in range(2 * KD):
                            if slot_no == 0 and has(n, -1):
                                exps(n - 1, 2 * KD - 1)
                            if isinstance(n, int) and n == 0 and slot_no == 2:
                                norm_x(1)
                                act.wait_ge(wo_loaded, 16)
                                nc.scalar.copy(wo_hi[:, :, :], wo_raw).then_inc(prep_act, 1)
                                act.wait_ge(prep_dve, 5)
                            if slot_no > 0 and has(n, 0):
                                exps(n, slot_no - 1)
                            if slot_no == 0:
                                if has(n, -1):
                                    pT_halves(n - 1, 2)
                                if has(n, 1) and not (isinstance(n, int) and n == 0):
                                    norm_x(n + 1)
                            if slot_no == 1 and has(n, -1):
                                a_halves(n - 1, 0)
                            if slot_no == 2:
                                if has(n, 0):
                                    q_halves(n, 1)
                                if has(n, -1):
                                    pT_halves(n - 1, 3)
                            if slot_no == 3:
                                if has(n, 1):
                                    x_halves(n + 1)
                            if slot_no == 4:
                                if has(n, -1):
                                    a_halves(n - 1, 1)
                                if has(n, 0):
                                    pT_halves(n, 0)
                                if has(n, -2):
                                    for a in range(2):
                                        act.wait_ge(n_ready, 2 * (n - 2) + a + 1)
                                        nc.scalar.copy(xnT[:, a, :, :], N_BANK[a][:, :].rearrange("p (k t) -> p k t", k=KD))\
                                          .then_inc(xnT_ready, 1)
                            if slot_no == 6:
                                if has(n, 1):
                                    q_halves(n + 1, 0)
                                if has(n, 0):
                                    pT_halves(n, 1)
                                if has(n, -2):
                                    act.wait_ge(gap_ready, n - 1)
                                    nc.scalar.activation(e1[:, :, :], gap[:, :, :], ACT.Exp).then_inc(e1_ready, 1)

                    steps(act, step)

                @block.vector
                def _(dve):
                    ROWS = 18
                    state = {"k": 0}

                    def done(ins):
                        ins.then_inc(rows_done, 1)
                        state["k"] += 1

                    def settle(blk):
                        wait_apart(dve, "dve", rows_done, ROWS * blk + state["k"])

                    def stats_x(blk):
                        dve.wait_ge(xin_loaded, 16 * blk + 16)
                        for a in range(2):
                            nc.vector.bn_stats(bn1[:, a, :], xin[:, a, :]).then_inc(stats1_done, 1)
                        wait_apart(dve, "dve", stats1_done, 2 * blk + 2)
                        for a in range(2):
                            ins = nc.vector.bn_aggr(mv1[:, a, :], bn1[:, a, :])
                        ins.then_inc(stats1_ready, 1)

                    def x_rest(blk):
                        for i in range(2):
                            dve.wait_ge(x_hi, 2 * blk + i + 1)
                            nc.vector.tensor_tensor(xT_lo[:, 2 * i:2 * i + 2, :],
                                                    X_BANK[i][:, :].rearrange("p (k t) -> p k t", k=2),
                                                    xT_hi[:, 2 * i:2 * i + 2, :].bitcast(fp32), ALU.subtract)\
                              .then_inc(x_lo, 1)

                    def q_rest(blk, i):
                        dve.wait_ge(q_hi, KD * blk + 2 * i + 2)
                        for m in (2 * i, 2 * i + 1):
                            nc.vector.scalar_tensor_tensor(
                                out=qT_lo[:, m, :], in0=Q_BANK[i][:, (m % 2) * TB:(m % 2 + 1) * TB],
                                scalar=bqT[:, m:m + 1], in1=qT_hi[:, m, :].bitcast(fp32),
                                op0=ALU.add, op1=ALU.subtract).then_inc(q_lo, 1)

                    dve.wait_ge(prep_pe, 1)
                    dve.wait_ge(consts_ready, 2)
                    ctxT = xnT
                    for b in range(B):
                        nc.vector.tensor_copy(ctxT[:, b, 0:KI, :], bank[b][:, 0:KI * P].rearrange("p (k t) -> p k t", k=KI))
                    nc.vector.tensor_copy(rwT[:, :, :], bank[2][:, 0:KD * E].rearrange("p (k e) -> p k e", k=KD))\
                      .then_inc(prep_dve, 1)
                    stats_x(0)
                    dve.wait_ge(prep_act, 3)
                    nc.vector.tensor_tensor(wq_lo[:, :, :], wq_raw, wq_hi[:, :, :].bitcast(fp32), ALU.subtract)\
                      .then_inc(prep_dve, 1)
                    x_rest(0)
                    dve.wait_ge(prep_pool, 1)
                    dve.wait_ge(prep_act, 3 + B * KD)
                    keys = lambda b, rows: row[rows, b, 0:KD * LKV].rearrange("p (m t) -> p m t", m=KD)
                    diagonal = [(slice(DK * hh, DK * (hh + 1)), slice(LKV * hh, LKV * (hh + 1))) for hh in range(HG)]
                    for b in range(B):
                        for rows, cols in diagonal:
                            last = nc.vector.tensor_copy(k_hi[b][rows, :, cols], keys(b, rows))
                    last.then_inc(prep_split, 1)
                    dve.wait_ge(prep_split, 1)
                    for b in range(B):
                        for rows, cols in diagonal:
                            last = nc.vector.tensor_tensor(k_lo[b][rows, :, cols], keys(b, rows),
                                                           k_hi[b][rows, :, cols].bitcast(fp32), ALU.subtract)
                    last.then_inc(prep_dve, 1)
                    q_rest(0, 0)

                    def late_splits():
                        stats_x(1)
                        dve.wait_ge(prep_pool, 2)
                        dve.wait_ge(prep_pe, 3)
                        vals = lambda b, hh: bank[2 + b][:, :].rearrange("p (g h d) -> p g h d", g=KD, h=HG)[:, :, hh, :]
                        mine = lambda t, hh: t[:, :, :].rearrange("p (g h) n -> p g h n", g=KD)[:, :, hh, DK * hh:DK * (hh + 1)]
                        for b in range(B):
                            for hh in range(HG):
                                last = nc.vector.tensor_copy(mine(v_hi[b], hh), vals(b, hh))
                        last.then_inc(prep_split, 1)
                        dve.wait_ge(prep_split, 2)
                        for b in range(B):
                            for hh in range(HG):
                                last = nc.vector.tensor_tensor(mine(v_lo[b], hh), vals(b, hh),
                                                               mine(v_hi[b], hh).bitcast(fp32), ALU.subtract)
                        last.then_inc(prep_dve, 1)
                        dve.wait_ge(prep_act, 4 + B * KD)
                        nc.vector.tensor_tensor(wo_lo[:, :, :], wo_raw, wo_hi[:, :, :].bitcast(fp32), ALU.subtract)
                        dve.wait_ge(late_loaded, 48)
                        for a in range(2):
                            nc.vector.memset(row[:, a, D:ROW], 0.0)
                        nc.vector.tensor_scalar(gbo_b[:, :], gbo_b[:, :], gates[:, 0:1], None, ALU.mult).then_inc(prep_dve, 1)

                    def maxima(n, idx):
                        g, t = divmod(idx, 2)
                        dve.wait_ge(s_ready, 2 * KD * n + idx + 1)
                        nc.vector.tensor_reduce(neg_max[:, t, HG * g:HG * (g + 1)],
                                                S_BANK[t][:, :].rearrange("p (h t) -> p h t", h=HG),
                                                AX.X, ALU.max, negate=True).then_inc(max_ready, 1)

                    def recips(blk, g):
                        heads = slice(HG * g, HG * (g + 1))
                        dve.wait_ge(exp_done, 2 * KD * blk + 2 * g + 2)
                        nc.vector.reciprocal(rsums[:, :, heads], sums[:, :, heads]).then_inc(rs_ready, 1)

                    def pT_rest(blk, g):
                        for t in range(2):
                            heads, cols = slice(HG * g, HG * (g + 1)), slice(t * P, (t + 1) * P)
                            dve.wait_ge(pt_hi, 2 * KD * blk + 2 * g + t + 1)
                            nc.vector.tensor_tensor(pT_lo[:, heads, cols], PT_BANK[t][:, :].rearrange("p (h t) -> p h t", h=HG),
                                                    pT_hi[:, heads, cols].bitcast(fp32), ALU.subtract).then_inc(pt_lo, 1)

                    def a_rest(blk, i):
                        dve.wait_ge(a_hi, 2 * blk + i + 1)
                        nc.vector.tensor_tensor(aT_lo[:, 2 * i:2 * i + 2, :],
                                                V_BANK[i][:, :].rearrange("p (k t) -> p k t", k=2),
                                                aT_hi[:, 2 * i:2 * i + 2, :].bitcast(fp32), ALU.subtract).then_inc(a_lo, 1)

                    def x1(blk, a):
                        dve.wait_ge(xb_ready, blk + 1)
                        dve.wait_ge(o_ready, 2 * blk + a + 1)
                        nc.vector.scalar_tensor_tensor(out=xres[:, a, :], in0=O_BANK[a][:, :],
                                                       scalar=gates[:, 0:1], in1=xres[:, a, :],
                                                       op0=ALU.mult, op1=ALU.add).then_inc(x1_ready, 1)

                    def stats_x1(blk):
                        dve.wait_ge(x1_ready, 2 * blk + 2)
                        for a in range(2):
                            done(nc.vector.bn_stats(bn2[:, a, :], xres[:, a, :]))
                        settle(blk)
                        for a in range(2):
                            ins = nc.vector.bn_aggr(mv2[:, a, :], bn2[:, a, :])
                        ins.then_inc(stats2_ready, 1)

                    def rows(blk):
                        dve.wait_ge(rstd2_ready, blk + 1)
                        if not isinstance(blk, int) or blk > 0:
                            dve.wait_ge(scattered, 64 * blk)
                        dve.wait_ge(stats2_ready, blk + 1)
                        for a in range(2):
                            done(nc.vector.scalar_tensor_tensor(out=row[:, a, 0:D], in0=xres[:, a, :],
                                                                scalar=mv2[:, a, 0:1], in1=gamma_b[:, :],
                                                                op0=ALU.subtract, op1=ALU.mult))
                        settle(blk)
                        for a in range(2):
                            nc.vector.scalar_tensor_tensor(out=row[:, a, 0:D], in0=row[:, a, 0:D],
                                                           scalar=rstd2[:, a:a + 1], in1=beta_b[:, :],
                                                           op0=ALU.mult, op1=ALU.add).then_inc(row_ready, 1)

                    def route(blk):
                        dve.wait_ge(l_ready, blk + 1)
                        nc.vector.tensor_scalar(logits[:, :, :], L_BANK[:, 0:2 * E].rearrange("p (a e) -> p a e", a=2),
                                                CLAMP, -CLAMP, ALU.min, ALU.max).then_inc(logits_ready, 1)
                        wait_apart(dve, "dve", logits_ready, blk + 1)
                        for a in range(2):
                            done(nc.vector.max(top8[:, a, :], logits[:, a, :]))
                        settle(blk)
                        for a in range(2):
                            done(nc.vector.max_index(topi[:, a, :], top8[:, a, :], logits[:, a, :]))
                        nc.vector.tensor_tensor(gap[:, :, :], top8[:, :, 1:2], top8[:, :, 0:1], ALU.subtract)\
                          .then_inc(gap_ready, 1)
                        settle(blk)
                        done(nc.vector.tensor_copy(idxf[:, :, :], topi[:, :, 0:TOPK]))
                        settle(blk)
                        done(nc.vector.tensor_tensor(
                            onehot[:, :, :, :],
                            expert_id[:, :].unsqueeze(1).unsqueeze(1).to_broadcast([P, 2, TOPK, E]),
                            idxf[:, :, :].unsqueeze(3).to_broadcast([P, 2, TOPK, E]), ALU.is_equal))
                        settle(blk)
                        done(nc.vector.tensor_tensor(chosen[:, :, :], onehot[:, :, 0, :], onehot[:, :, 1, :], ALU.add))
                        settle(blk)
                        nc.vector.tensor_tensor(before[:, 1, :], before[:, 0, :], chosen[:, 0, :], ALU.add)\
                          .then_inc(chosen_ready, 1)

                    def place(blk):
                        dve.wait_ge(chosen_ready, blk + 1)
                        dve.wait_ge(c_ready, blk + 1)
                        nc.vector.tensor_tensor(
                            prod[:, :, :, :], onehot[:, :, :, :],
                            C_BANK[:, 0:2 * E].rearrange("p (a e) -> p a e", a=2).unsqueeze(2).to_broadcast([P, 2, TOPK, E]),
                            ALU.mult).then_inc(c_read, 1)
                        done(nc.vector.tensor_tensor(before[:, 0, :], before[:, 1, :], chosen[:, 1, :], ALU.add))
                        dve.wait_ge(e1_ready, blk + 1)
                        done(nc.vector.tensor_scalar(zsum[:, :, :], e1[:, :, :], 1.0, 1e-12, ALU.add, ALU.add))
                        settle(blk)
                        dve.wait_ge(c_read, blk + 1)
                        done(nc.vector.tensor_reduce(pos[:, :, :], prod[:, :, :, :], AX.X, ALU.add))
                        done(nc.vector.reciprocal(zinv[:, :, :], zsum[:, :, :]))
                        settle(blk)
                        done(nc.vector.tensor_scalar(over[:, :, :], pos[:, :, :], float(CAP), float(E * CAP),
                                                     ALU.is_ge, ALU.mult))
                        done(nc.vector.scalar_tensor_tensor(out=slotf[:, :, :], in0=idxf[:, :, :], scalar=float(CAP),
                                                            in1=pos[:, :, :], op0=ALU.mult, op1=ALU.add))
                        nc.vector.tensor_scalar(row[:, :, C_W0], zinv[:, :, 0], gates[:, 1:2], None, ALU.mult)
                        nc.vector.scalar_tensor_tensor(out=row[:, :, C_W1], in0=e1[:, :, 0], scalar=gates[:, 1:2],
                                                       in1=zinv[:, :, 0], op0=ALU.mult, op1=ALU.mult)
                        nc.vector.tensor_copy(row[:, :, C_TOK], tok_count[:, :])
                        nc.vector.tensor_copy(row[:, :, C_IDX], idxf[:, :, 0])
                        settle(blk)
                        nc.vector.tensor_tensor(slot[:, :, :], slotf[:, :, :], over[:, :, :], ALU.add)\
                          .then_inc(slot_ready, 1)
                        done(nc.vector.tensor_scalar(tok_count[:, :], tok_count[:, :], float(-TB), None, ALU.add))

                    def step(n, b_s, b_v):
                        state["k"] = 0
                        for slot_no in range(2 * KD):
                            if has(n, 0):
                                maxima(n, slot_no)
                            if isinstance(n, int) and n == 0 and slot_no == 1:
                                late_splits()
                            if slot_no == 0:
                                if has(n, -2):
                                    x1(n - 2, 1)
                                if has(n, -1):
                                    pT_rest(n - 1, 2)
                                    recips(n - 1, 3)
                                if has(n, -2):
                                    stats_x1(n - 2)
                            if slot_no == 1 and has(n, -1):
                                a_rest(n - 1, 0)
                            if slot_no == 2:
                                if has(n, 0):
                                    recips(n, 0)
                                    q_rest(n, 1)
                                if has(n, -1):
                                    pT_rest(n - 1, 3)
                            if slot_no == 3:
                                if has(n, 1):
                                    x_rest(n + 1)
                                if has(n, -2):
                                    rows(n - 2)
                            if slot_no == 4:
                                if has(n, -1):
                                    a_rest(n - 1, 1)
                                if has(n, 0):
                                    recips(n, 1)
                                    pT_rest(n, 0)
                            if slot_no == 5:
                                if has(n, 2):
                                    stats_x(n + 2)
                                if has(n, -2):
                                    route(n - 2)
                            if slot_no == 6:
                                if has(n, 0):
                                    recips(n, 2)
                                if has(n, 1):
                                    q_rest(n + 1, 0)
                                if has(n, 0):
                                    pT_rest(n, 1)
                            if slot_no == 7:
                                if has(n, -1):
                                    x1(n - 1, 0)
                                if has(n, -2):
                                    place(n - 2)
                        assert state["k"] in (0, ROWS), state["k"]

                    steps(dve, step)
                    dve.wait_ge(rows_done, ROWS * NB)
                    nc.vector.tensor_copy(chosen[:, 0, :], before[:, 0, :]).then_inc(sums_ready, 1)
                    dve.wait_ge(counts_ready, 1)
                    nc.vector.tensor_copy(counts[:, :], bank[0][0:1, 0:E])

                @block.tensor
                def _(pe):
                    def passes(out_ap, pairs):
                        n, at = 3 * len(pairs), 0
                        for (s_hi, s_lo), (m_hi, m_lo) in pairs:
                            for st, mv in ((s_hi, m_hi), (s_hi, m_lo), (s_lo, m_hi)):
                                last = nc.tensor.matmul(out_ap, st, mv, start=(at == 0), stop=(at == n - 1))
                                at += 1
                        return last

                    pe.wait_ge(kv_loaded, 16 * N_KV)
                    pe.wait_ge(consts_ready, 2)
                    for b in range(B):
                        for k in range(KI):
                            nc.tensor.transpose(bank[b][:, k * P:(k + 1) * P], row[:, b, k * P:(k + 1) * P], ident[:, :])
                    for k in range(KD):
                        a, c = divmod(k, KD // 2)
                        last = nc.tensor.transpose(bank[2][:, k * E:(k + 1) * E],
                                                   row[0:E, a, DI + c * P:DI + (c + 1) * P], ident[0:E, 0:E])
                    last.then_inc(prep_pe, 1)
                    pe.wait_ge(prep_dve, 1)
                    ctxT = xnT
                    for b in range(B):
                        for m in range(KD):
                            for k in range(KI):
                                last = nc.tensor.matmul(bank[4 + b][:, m * LKV:(m + 1) * LKV], wk_raw[:, k, m * P:(m + 1) * P],
                                                        ctxT[:, b, k, :], start=(k == 0), stop=(k == KI - 1))
                    last.then_inc(prep_pe, 1)

                    def transposes_x(blk):
                        pe.wait_ge(xn_ready, 2 * blk + 2)
                        for i in range(2):
                            for kk in range(2):
                                for a in range(2):
                                    last = nc.tensor.transpose(X_BANK[i][:, kk * TB + a * P:kk * TB + (a + 1) * P],
                                                               xin[:, a, (2 * i + kk) * P:(2 * i + kk + 1) * P], ident[:, :])
                            last.then_inc(x_ready, 1)

                    def queries(blk, i):
                        pe.wait_ge(x_lo, 2 * blk + 2)
                        for m in (2 * i, 2 * i + 1):
                            last = passes(Q_BANK[i][:, (m % 2) * TB:(m % 2 + 1) * TB],
                                          [((wq_hi[:, k, m * P:(m + 1) * P], wq_lo[:, k, m * P:(m + 1) * P]),
                                            (xT_hi[:, k, :], xT_lo[:, k, :])) for k in range(KD)])
                        last.then_inc(q_ready, 1)

                    def scores(n, idx, b):
                        g, t = divmod(idx, 2)
                        pe.wait_ge(q_lo, KD * n + g + 1)
                        if not isinstance(n, int) or 2 * KD * n + idx >= 2:
                            pe.wait_ge(exp_done, 2 * KD * n + idx - 1)
                        passes(S_BANK[t][:, :], [((qT_hi[:, g, t * P:(t + 1) * P], qT_lo[:, g, t * P:(t + 1) * P]),
                                                  (k_hi[b][:, g, :], k_lo[b][:, g, :]))]).then_inc(s_ready, 1)

                    def probs_T(blk, g):
                        pe.wait_ge(pn_ready, KD * blk + g + 1)
                        for t in range(2):
                            at = 2 * KD * blk + 2 * g + t
                            if not isinstance(at, int) or at >= 2:
                                pe.wait_ge(pt_lo, at - 1)
                            for hh in range(HG):
                                last = nc.tensor.transpose(PT_BANK[t][:, hh * P:(hh + 1) * P],
                                                           probs[:, t, HG * g + hh, :], ident[:, :])
                            last.then_inc(pt_ready, 1)

                    def heads(blk, i, b):
                        pe.wait_ge(pt_lo, 2 * KD * blk + 4 * i + 4)
                        for gg in range(2):
                            g = 2 * i + gg
                            last = passes(V_BANK[i][:, gg * TB:(gg + 1) * TB],
                                          [((v_hi[b][:, h, :], v_lo[b][:, h, :]), (pT_hi[:, h, :], pT_lo[:, h, :]))
                                           for h in range(HG * g, HG * (g + 1))])
                        last.then_inc(v_ready, 1)

                    def attention_out(blk, a):
                        pe.wait_ge(a_lo, 2 * blk + 2)
                        passes(O_BANK[a][:, :],
                               [((aT_hi[:, k, a * P:(a + 1) * P], aT_lo[:, k, a * P:(a + 1) * P]),
                                 (wo_hi[:, k, :], wo_lo[:, k, :])) for k in range(KD)]).then_inc(o_ready, 1)

                    transposes_x(0)
                    for b in range(B):
                        for k in range(KI):
                            nc.tensor.matmul(bank[2 + b][:, :], ctxT[:, b, k, :], wv_raw[:, k, :], start=(k == 0), stop=False)
                        last = nc.tensor.matmul(bank[2 + b][:, :], ones[0:1, :], bv_row[:, :], start=False, stop=True)
                    last.then_inc(prep_pe, 1)
                    pe.wait_ge(prep_dve, 2)
                    queries(0, 0)
                    pe.wait_ge(prep_dve, 3)

                    def step(n, b_s, b_v):
                        for slot_no in range(2 * KD):
                            if has(n, 0):
                                scores(n, slot_no, b_s)
                            if slot_no == 0 and has(n, -1):
                                probs_T(n - 1, 2)
                                heads(n - 1, 0, b_v)
                            if slot_no == 1 and has(n, 0):
                                if has(n, -3):
                                    pe.wait_ge(c_read, n - 2)
                                queries(n, 1)
                            if slot_no == 2:
                                if has(n, -1):
                                    probs_T(n - 1, 3)
                                if has(n, 1):
                                    if has(n, -2):
                                        pe.wait_ge(x1_ready, 2 * (n - 2) + 2)
                                    transposes_x(n + 1)
                            if slot_no == 3:
                                if has(n, -1):
                                    pe.wait_ge(a_lo, 2 * (n - 1) + 1)
                                    heads(n - 1, 1, b_v)
                            if slot_no == 4:
                                if isinstance(n, int) and n == 0:
                                    pe.wait_ge(prep_dve, 4)
                                if has(n, 0):
                                    probs_T(n, 0)
                                if has(n, -2):
                                    if has(n, 1):
                                        pe.wait_ge(x_lo, 2 * (n + 1) + 1)
                                    else:
                                        pe.wait_ge(x1_ready, 2 * (n - 2) + 1)
                                    if has(n, 0):
                                        pe.wait_ge(q_lo, KD * n + 4)
                                    else:
                                        pe.wait_ge(c_read, n - 2)
                                    for a in range(2):
                                        pe.wait_ge(row_ready, 2 * (n - 2) + a + 1)
                                        for k in range(KD):
                                            last = nc.tensor.transpose(N_BANK[a][:, k * P:(k + 1) * P],
                                                                       row[:, a, k * P:(k + 1) * P], ident[:, :])
                                        last.then_inc(n_ready, 1)
                            if slot_no == 5:
                                if has(n, -2):
                                    pe.wait_ge(xnT_ready, 2 * (n - 2) + 2)
                                    for a in range(2):
                                        for k in range(KD):
                                            last = nc.tensor.matmul(L_BANK[:, a * E:(a + 1) * E], xnT[:, a, k, :], rwT[:, k, :],
                                                                    start=(k == 0), stop=(k == KD - 1))
                                    last.then_inc(l_ready, 1)
                                if has(n, 1):
                                    queries(n + 1, 0)
                            if slot_no == 6:
                                if has(n, 0):
                                    probs_T(n, 1)
                                if has(n, -1):
                                    if isinstance(n, int) and n == 1:
                                        pe.wait_ge(prep_dve, 5)
                                    attention_out(n - 1, 0)
                            if slot_no == 7:
                                if has(n, -2):
                                    pe.wait_ge(chosen_ready, n - 1)
                                    for a in range(2):
                                        nc.tensor.matmul(C_BANK[:, a * E:(a + 1) * E], upper[:, :], chosen[:, a, :],
                                                         start=True, stop=False)
                                        last = nc.tensor.matmul(C_BANK[:, a * E:(a + 1) * E], ones[:, :], before[:, a, :],
                                                                start=False, stop=True)
                                    last.then_inc(c_ready, 1)
                                if has(n, -1):
                                    if has(n, 1):
                                        pe.wait_ge(q_lo, KD * (n + 1) + 2)
                                    else:
                                        pe.wait_ge(x1_ready, 2 * (n - 2) + 2)
                                    attention_out(n - 1, 1)

                    steps(pe, step)
                    pe.wait_ge(sums_ready, 1)
                    nc.tensor.matmul(bank[0][:, 0:E], ones[:, :], chosen[:, 0, :], start=True, stop=True).then_inc(counts_ready, 1)

        with ExitStack() as stage:
            def sb(name, shape, dt=fp32):
                return stage.enter_context(nc.sbuf_tensor(name, shape, dt))

            raw12 = [sb(f"raw12_{i}", [P, NU12, D]) for i in range(2)]
            raw3 = [sb(f"raw3_{i}", [P, KD, FC]) for i in range(2)]
            w12_hi, w12_lo = ([sb(f"w12_{h}{i}", [P, KD, NU12, P], f32r) for i in range(2)] for h in ("hi", "lo"))
            w3_hi, w3_lo = ([sb(f"w3_{h}{i}", [P, NU3, D], f32r) for i in range(2)] for h in ("hi", "lo"))
            xrow = sb("xrow", [P, NT, ROW])
            xT_hi, xT_lo = (sb(f"slotsT_{h}", [P, KD, CAP], f32r) for h in ("hi", "lo"))
            silu = [sb(f"silu{i}", [P, SB]) for i in range(2)]
            h32 = [sb(f"h32_{i}", [P, SB]) for i in range(2)]
            h_hi, h_lo = ([sb(f"h_{h}{i}", [P, NU3, SB], f32r) for i in range(3)] for h in ("hi", "lo"))
            yacc = sb("yacc", [P, NT, D])
            yout = sb("yout", [P, NT, D])
            first_is_e = sb("first_is_e", [P, NT])
            wdiff = sb("wdiff", [P, NT])
            wslot = sb("wslot", [P, NT])
            token = sb("token", [P, NT], i32)
            e_now = sb("e_now", [P, 1])
            nothing = sb("nothing", [P, D])

            raw12_loaded, raw3_loaded = ([sem(f"{n}_loaded{i}") for i in range(2)] for n in ("raw12", "raw3"))
            xrow_loaded = [sem(f"xrow_loaded{i}") for i in range(NSB)]
            tp_ready, hi_done, lo_done = sem("tp_ready"), sem("hi_done"), sem("lo_done")
            g_ready, u_ready = sem("g_ready"), sem("u_ready")
            silu_ready, h32_ready = sem("silu_ready"), sem("h32_ready")
            hhi_ready, hlo_ready = sem("hhi_ready"), sem("hlo_ready")
            y_ready, y_added = sem("y_ready"), sem("y_added")
            yout_ready, yout_free = sem("yout_ready"), sem("yout_free")
            weights_ready, added, idx_done = sem("weights_ready"), sem("added"), sem("idx_done")

            GB, UB, YB, TBK = bank[0:2], bank[2:4], bank[4:6], bank[6:8]
            STEPS = NSB * NU3
            BT = SB // P
            UNITS = NU * NCH + NT
            hbuf = lambda s: 0 if s == 0 else 1 + s % 2

            def blocks(eng, n_e, g1, g2, skip, between, half, end):
                g1(0)

                def whole_g2(s, place):
                    for tt in range(BT):
                        g2(s, place, tt)

                def level(s):
                    def tail():
                        if s < NSB:
                            skip(s, NSB - s)
                        if s > 1:
                            whole_g2(0, s - 2)
                        between()
                        g2(s - 1, s - 1, 0)
                        with eng.If(n_e > (s - 1) * SB + P):
                            g2(s - 1, s - 1, 1)
                        with eng.Else():
                            half(s - 1)
                        if s < NSB:
                            end(s, NSB - s)

                    if s == NSB:
                        tail()
                        return
                    with eng.If(n_e > s * SB):
                        g1(s)
                        if s >= 2:
                            whole_g2(s - 1, s - 2)
                        level(s + 1)
                    with eng.Else():
                        tail()

                level(1)

            def experts(eng, chunk):
                with eng.Fori(0, E) as e:
                    n_e = eng.value_load(counts[0:1, bass.ds(e, 1)], min_val=0, max_val=T)
                    chunk(e, 0, 0, 0, n_e, True, False)
                    with eng.Fori(0, NCH // 2 - 1) as pair:
                        for i in (1, 2):
                            chunk(e, pair * 2 + i, i % 2, pair + 1, n_e, False, False)
                    chunk(e, NCH - 1, (NCH - 1) % 2, NCH // 2, n_e, False, True)

            steps_before = lambda e, c: e * (NCH * STEPS) + c * STEPS
            tiles_before = lambda e, c: e * (NCH * NT) + c * NT
            units_ahead = NU + BT

            def units_before(e, c, first):
                return e * UNITS + units_ahead if first else e * UNITS + c * NU + (units_ahead + NT - BT)

            def place_of(kind, i, first, last):
                if kind == "X":
                    return NU12 + i if last else i - BT if i < 2 * BT else i
                return i + (BT if first and i < NU3 else NT - BT if first else BT if last and i >= NU12 else 0)

            def units_of(s, j, first, last):
                units = []
                if s == 0 and first and j == 0:
                    units = [("X", t) for t in range(BT, 2 * BT)]
                elif s == 0:
                    units = [("U", (j - first) * NU3 + u) for u in range(NU3)]
                elif first and s < NSB - 1 and j == 0:
                    units = [("X", t) for t in range(BT * (s + 1), BT * (s + 2))]
                return [(kind, i, place_of(kind, i, first, last)) for kind, i in units]

            def units_between(first, last):
                units = [("U", u) for u in range(NU3, NU12)] if first else [("X", t) for t in range(BT)] if last else []
                return [(kind, i, place_of(kind, i, first, last)) for kind, i in units]

            ahead = [("U", u) for u in range(NU12)] + [("X", t) for t in range(BT)] + [("U", u) for u in range(NU12, NU)]

            def load_slot_block(eng, e, s):
                eng.dma_start(xrow[:, BT * s:BT * (s + 1), :],
                              xbuf[bass.ds(e * CAP + s * SB, SB), :].rearrange("(t p) c -> p t c", p=P))\
                   .then_inc(xrow_loaded[s], 16)

            with nc.Block() as block:

                @block.sync
                def _(sp):
                    def load_w12(e, c, par):
                        src12 = w12.rearrange("e (h c r p) d -> h e c p r d", h=2, c=NCH, p=P)
                        for half in range(2):
                            sp.dma_start(raw12[par][:, half * NU3:(half + 1) * NU3, :],
                                         src12[half, bass.ds(e, 1), c, :, :, :].rearrange("e p r d -> (e p) r d"))\
                              .then_inc(raw12_loaded[par], 16)

                    def load_w3(e, c, par):
                        src3 = w3.rearrange("e (k p) (c f) -> e c p k f", p=P, f=FC)[bass.ds(e, 1), c, :, :, :]
                        sp.dma_start(raw3[par][:, :, :], src3.rearrange("e p k f -> (e p) k f"))\
                          .then_inc(raw3_loaded[par], 16)

                    def load_weights(e, c, par):
                        load_w12(e, c, par)
                        load_w3(e, c, par)

                    load_w12(0, 0, 0)
                    load_slot_block(sp, 0, 0)
                    load_w3(0, 0, 0)
                    load_weights(0, 1, 1)
                    for s in range(1, NSB):
                        load_slot_block(sp, 0, s)
                    with sp.Fori(0, E - 1) as e:
                        for c in range(NCH):
                            sp.wait_ge(lo_done, units_before(e, c, c == 0))
                            load_weights(e + (c + 2) // NCH, (c + 2) % NCH, c % 2)
                            if c == 1:
                                wait_apart(sp, "sp", weights_ready, e + 1)
                                for s in range(NSB):
                                    load_slot_block(sp, e + 1, s)
                    for c in range(NCH - 1):
                        sp.wait_ge(lo_done, units_before(E - 1, c, c == 0))
                        load_weights(E - 1 if c + 2 < NCH else 0, (c + 2) % NCH, c % 2)
                        if c == 1:
                            sp.wait_ge(weights_ready, E)
                            load_slot_block(sp, 0, 0)

                @block.gpsimd
                def _(pool):
                    nc.gpsimd.memset(nothing[:, :], 0.0)
                    nc.gpsimd.memset(e_now[:, :], 0.0).then_inc(idx_done, 1)
                    pool.sem_inc(yout_free, 1)
                    def expert(e):
                        n_e = pool.value_load(counts[0:1, bass.ds(e, 1)], min_val=0, max_val=T)
                        for s in range(NSB):
                            wait_apart(pool, "pool", xrow_loaded[s], 16 * (e + 1))
                        wait_apart(pool, "pool", idx_done, 3 * e + 1)
                        nc.gpsimd.tensor_scalar(token[:, :], xrow[:, :, C_TOK], -1.0, float(T), ALU.mult, ALU.add)
                        nc.gpsimd.tensor_scalar(first_is_e[:, :], xrow[:, :, C_IDX], e_now[:, 0:1], None, ALU.is_equal)
                        nc.gpsimd.tensor_tensor(wdiff[:, :], xrow[:, :, C_W0], xrow[:, :, C_W1], ALU.subtract)\
                          .then_inc(idx_done, 1)
                        pool.wait_ge(idx_done, 3 * e + 2)
                        nc.gpsimd.tensor_tensor(wdiff[:, :], wdiff[:, :], first_is_e[:, :], ALU.mult).then_inc(idx_done, 1)
                        pool.wait_ge(idx_done, 3 * e + 3)
                        nc.gpsimd.tensor_tensor(wslot[:, :], wdiff[:, :], xrow[:, :, C_W1], ALU.add).then_inc(weights_ready, 1)
                        nc.gpsimd.tensor_scalar_add(e_now[:, :], e_now[:, :], 1.0).then_inc(idx_done, 1)
                        wait_apart(pool, "pool", idx_done, 3 * e + 4)

                        def add_rows(t, rows):
                            nc.gpsimd.indirect_dma_start(
                                out=out_tok, out_offset=bass.IndirectOffsetOnAxis(ap=token[:, t:t + 1], axis=0),
                                in_=rows, in_offset=None, bounds_check=T - 1, oob_is_err=False,
                                compute_op=ALU.add).then_inc(added, 16)

                        def scatter(s, place, tt):
                            wait_apart(pool, "pool", yout_ready, NT * (e + 1) + BT * place + tt + 1)
                            add_rows(BT * s + tt, yout[:, BT * s + tt, :])

                        def skip(s, left):
                            for t in range(BT * s, NT):
                                add_rows(t, nothing[:, :])

                        def half(s):
                            pool.sem_inc(yout_ready, 1)
                            add_rows(BT * s + 1, nothing[:, :])

                        def end(s, left):
                            pool.sem_inc(yout_ready, BT * left)

                        blocks(pool, n_e, lambda s: None, scatter, skip, lambda: None, half, end)
                        wait_apart(pool, "pool", added, 16 * NT * (e + 1))
                        pool.sem_inc(yout_free, 1)

                    with pool.Fori(0, E) as e:
                        expert(e)

                @block.scalar
                def _(act):
                    def hi_half(kind, i, par, at):
                        act.wait_ge(tp_ready, at + 1)
                        src = TBK[i % 2][:, :]
                        if kind == "X":
                            dst, src = xT_hi[:, :, i * P:(i + 1) * P], src.rearrange("p (k t) -> p k t", k=KD)
                        elif i < NU12:
                            dst, src = w12_hi[par][:, :, i, :], src.rearrange("p (k f) -> p k f", k=KD)
                        else:
                            dst = w3_hi[par][:, i - NU12, :]
                        nc.scalar.copy(dst, src).then_inc(hi_done, 1)

                    act.sem_inc(yout_ready, NT)
                    for at, (kind, i) in enumerate(ahead):
                        hi_half(kind, i, 0, at)

                    def chunk(e, c, par, half, n_e, first, last):
                        units = units_before(e, c, first)

                        def g1(s):
                            for j in range(NU3):
                                q = s * NU3 + j
                                at = steps_before(e, c) + q
                                act.wait_ge(g_ready, at + 1)
                                nc.scalar.activation(silu[q % 2][:, :], GB[q % 2][:, 0:SB], ACT.Silu).then_inc(silu_ready, 1)
                                act.wait_ge(h32_ready, at + 1)
                                nc.scalar.copy(h_hi[hbuf(s)][:, j, :], h32[q % 2][:, :]).then_inc(hhi_ready, 1)
                                for kind, i, place in units_of(s, j, first, last):
                                    hi_half(kind, i, 1 - par, units + place)

                        def g2(s, place, tt):
                            if not last:
                                return
                            if place == 0 and tt == 0:
                                act.wait_ge(weights_ready, e + 1)
                                act.wait_ge(yout_free, e + 1)
                            t = BT * s + tt
                            act.wait_ge(y_added, tiles_before(e, c) + BT * place + tt + 3)
                            nc.scalar.activation(yout[:, t, :], yacc[:, t, :], ACT.Copy,
                                                 scale=wslot[:, t:t + 1]).then_inc(yout_ready, 1)

                        def skip(s, left):
                            act.sem_inc(g_ready, NU3 * left)
                            act.sem_inc(h32_ready, NU3 * left)
                            if first and left > 1:
                                act.sem_inc(tp_ready, BT * (left - 1))

                        def between():
                            for kind, i, place in units_between(first, last):
                                hi_half(kind, i, 1 - par, units + place)

                        blocks(act, n_e, g1, g2, skip, between, lambda s: None, lambda s, left: None)
                        for u in range(NU12, NU):
                            hi_half("U", u, 1 - par, units + place_of("U", u, first, last))

                    experts(act, chunk)

                @block.vector
                def _(dve):
                    def lo_half(kind, i, par, at):
                        dve.wait_ge(hi_done, at + 1)
                        src = TBK[i % 2][:, :]
                        if kind == "X":
                            cols = slice(i * P, (i + 1) * P)
                            dst, hi, src = xT_lo[:, :, cols], xT_hi[:, :, cols], src.rearrange("p (k t) -> p k t", k=KD)
                        elif i < NU12:
                            dst, hi, src = w12_lo[par][:, :, i, :], w12_hi[par][:, :, i, :], src.rearrange("p (k f) -> p k f", k=KD)
                        else:
                            dst, hi = w3_lo[par][:, i - NU12, :], w3_hi[par][:, i - NU12, :]
                        nc.vector.tensor_tensor(dst, src, hi.bitcast(fp32), ALU.subtract).then_inc(lo_done, 1)

                    dve.sem_inc(y_added, BT)
                    for at, (kind, i) in enumerate(ahead):
                        lo_half(kind, i, 0, at)

                    def chunk(e, c, par, half, n_e, first, last):
                        units = units_before(e, c, first)

                        def g1(s):
                            for j in range(NU3):
                                q = s * NU3 + j
                                at = steps_before(e, c) + q
                                dve.wait_ge(u_ready, at + 1)
                                dve.wait_ge(silu_ready, at + 1)
                                nc.vector.tensor_tensor(h32[q % 2][:, :], silu[q % 2][:, :], UB[q % 2][:, 0:SB], ALU.mult)\
                                  .then_inc(h32_ready, 1)
                                dve.wait_ge(hhi_ready, at + 1)
                                nc.vector.tensor_tensor(h_lo[hbuf(s)][:, j, :], h32[q % 2][:, :],
                                                        h_hi[hbuf(s)][:, j, :].bitcast(fp32), ALU.subtract).then_inc(hlo_ready, 1)
                                for kind, i, place in units_of(s, j, first, last):
                                    lo_half(kind, i, 1 - par, units + place)

                        def g2(s, place, tt):
                            t = BT * s + tt
                            dve.wait_ge(y_ready, tiles_before(e, c) + BT * place + tt + 1)
                            if first:
                                dve.wait_ge(yout_ready, NT * (e + 1))
                                nc.vector.tensor_copy(yacc[:, t, :], YB[tt][:, :]).then_inc(y_added, 1)
                            else:
                                dve.wait_ge(y_added, tiles_before(e, c) + BT)
                                nc.vector.tensor_tensor(yacc[:, t, :], YB[tt][:, :], yacc[:, t, :], ALU.add)\
                                  .then_inc(y_added, 1)

                        def half(s):
                            dve.sem_inc(y_ready, 1)
                            dve.wait_ge(y_added, tiles_before(e, c) + BT + BT * s + 1)
                            dve.sem_inc(y_added, 1)

                        def skip(s, left):
                            dve.sem_inc(u_ready, NU3 * left)
                            dve.sem_inc(silu_ready, NU3 * left)
                            dve.sem_inc(hhi_ready, NU3 * left)
                            if first and left > 1:
                                dve.sem_inc(hi_done, BT * (left - 1))
                                dve.wait_ge(lo_done, units + NU3 + BT * s)
                                dve.sem_inc(lo_done, BT * (left - 1))

                        def end(s, left):
                            dve.sem_inc(y_ready, BT * left)
                            dve.wait_ge(y_added, tiles_before(e, c) + BT + BT * s)
                            dve.sem_inc(y_added, BT * left)

                        def between():
                            for kind, i, place in units_between(first, last):
                                lo_half(kind, i, 1 - par, units + place)

                        blocks(dve, n_e, g1, g2, skip, between, half, end)
                        for u in range(NU12, NU):
                            lo_half("U", u, 1 - par, units + place_of("U", u, first, last))

                    experts(dve, chunk)

                @block.tensor
                def _(pe):
                    def passes(out_ap, pairs):
                        n, at = 3 * len(pairs), 0
                        for (s_hi, s_lo), (m_hi, m_lo) in pairs:
                            for st, mv in ((s_hi, m_hi), (s_hi, m_lo), (s_lo, m_hi)):
                                last = nc.tensor.matmul(out_ap, st, mv, start=(at == 0), stop=(at == n - 1))
                                at += 1
                        return last

                    def transpose_unit(kind, i, par, at):
                        if not isinstance(at, int) or at >= 2:
                            pe.wait_ge(lo_done, at - 1)
                        for k in range(KD):
                            if kind == "X":
                                src = xrow[:, i, k * P:(k + 1) * P]
                            elif i < NU12:
                                src = raw12[par][:, i, k * P:(k + 1) * P]
                            else:
                                src = raw3[par][:, k, (i - NU12) * P:(i - NU12 + 1) * P]
                            last = nc.tensor.transpose(TBK[i % 2][:, k * P:(k + 1) * P], src, ident[:, :])
                        last.then_inc(tp_ready, 1)

                    for at, (kind, i) in enumerate(ahead):
                        if i == 0:
                            pe.wait_ge(raw12_loaded[0], 32) if kind == "U" else pe.wait_ge(xrow_loaded[0], 16)
                        if i == NU12:
                            pe.wait_ge(raw3_loaded[0], 16)
                        transpose_unit(kind, i, 0, at)

                    def chunk(e, c, par, half, n_e, first, last):
                        units = units_before(e, c, first)
                        loads = e * (NCH // 2) + half + 1

                        def one_unit(kind, i, place):
                            if kind == "U" and i == 0:
                                pe.wait_ge(raw12_loaded[1 - par], 32 * loads)
                            if kind == "X" and i % BT == 0:
                                pe.wait_ge(xrow_loaded[i // BT], 16 * (e + 1) if first else 16 * (e + 2))
                            transpose_unit(kind, i, 1 - par, units + place)

                        def between():
                            for kind, i, place in units_between(first, last):
                                one_unit(kind, i, place)

                        def g1(s):
                            stat = lambda r: [(w12_hi[par][:, k, r, :], w12_lo[par][:, k, r, :]) for k in range(KD)]
                            slots = slice(s * SB, (s + 1) * SB)
                            moving = [(xT_hi[:, k, slots], xT_lo[:, k, slots]) for k in range(KD)]
                            if s == 0:
                                pe.wait_ge(lo_done, units - NU3)
                            elif first:
                                pe.wait_ge(lo_done, units + place_of("X", BT * s + BT - 1, first, last) + 1)
                            for j in range(NU3):
                                q = s * NU3 + j
                                at = steps_before(e, c) + q
                                if not first or q >= 2:
                                    pe.wait_ge(silu_ready, at - 1)
                                passes(GB[q % 2][:, 0:SB], list(zip(stat(j), moving))).then_inc(g_ready, 1)
                                if not first or q >= 2:
                                    pe.wait_ge(h32_ready, at - 1)
                                passes(UB[q % 2][:, 0:SB], list(zip(stat(NU3 + j), moving))).then_inc(u_ready, 1)
                                for kind, i, place in units_of(s, j, first, last):
                                    one_unit(kind, i, place)

                        def g2(s, place, tt):
                            if tt == 0:
                                pe.wait_ge(hlo_ready, steps_before(e, c) + (s + 1) * NU3)
                                if place == 0:
                                    pe.wait_ge(lo_done, units)
                            pe.wait_ge(y_added, tiles_before(e, c) + BT * place + tt + 1)
                            cols = slice(tt * P, (tt + 1) * P)
                            passes(YB[tt][:, :], [((h_hi[hbuf(s)][:, f, cols], h_lo[hbuf(s)][:, f, cols]),
                                                   (w3_hi[par][:, f, :], w3_lo[par][:, f, :]))
                                                  for f in range(NU3)]).then_inc(y_ready, 1)

                        def end(s, left):
                            pe.sem_inc(hlo_ready, NU3 * left)

                        blocks(pe, n_e, g1, g2, lambda s, left: None, between, lambda s: None, end)
                        pe.wait_ge(raw3_loaded[1 - par], 16 * loads)
                        for u in range(NU12, NU):
                            transpose_unit("U", u, 1 - par, units + place_of("U", u, first, last))

                    experts(pe, chunk)


_INS = ['x', 'ctx_512', 'g_xattn', 'g_ffn', 'L0_xattn_Wq', 'L0_xattn_bq', 'L0_xattn_Wk', 'L0_xattn_bk', 'L0_xattn_Wv',
        'L0_xattn_bv', 'L0_xattn_Wo', 'L0_xattn_bo', 'L0_ffn_ln_gamma', 'L0_ffn_ln_beta', 'L0_ffn_router_w',
        'L0_ffn_w12', 'L0_ffn_w3']
_OUTS = [((2, 2048, 512), 'float32')]


def kernel(**inputs):
    import numpy as _np
    import concourse.bacc as _bacc
    from concourse import mybir as _mybir
    from concourse.bass_utils import run_bass_kernel_spmd as _run

    nc = _bacc.Bacc("TRN2", target_bir_lowering=False, num_devices=1)
    arrays, args = {}, []
    for name in _INS:
        a = _np.ascontiguousarray(inputs[name])
        arrays[f"in_{name}_dram"] = a
        args.append(nc.dram_tensor(f"in_{name}_dram", a.shape, _mybir.dt.from_np(a.dtype), kind="ExternalInput").ap())
    for i, (shape, dtype) in enumerate(_OUTS):
        dt = _mybir.dt.from_np(_np.dtype(dtype))
        args.append(nc.dram_tensor(f"out_{i}_dram", shape, dt, kind="ExternalOutput").ap())
    flamingo_gated_layer(nc, *args)
    r = _run(nc, [arrays], core_ids=[0])
    return r.results[0]["out_0_dram"]
```
